# Optimizing a Trainium2 kernel written in Bass

```python
import numpy as np
import jax
import jax.numpy as jnp

def _softmax(x, axis=-1):
    return jax.nn.softmax(x, axis=axis)

def _gelu(x):
    return jax.nn.gelu(x, approximate=True)

def _silu(x):
    return jax.nn.silu(x)

def _sigmoid(x):
    return jax.nn.sigmoid(x)

def _layernorm(x, axis=-1, eps=1e-05):
    m = jnp.mean(x, axis=axis, keepdims=True)
    v = jnp.var(x, axis=axis, keepdims=True)
    return (x - m) / jnp.sqrt(v + eps)

def _scatter_add(tgt, idx, src, axis=0):
    return tgt.at[idx].add(src)

def _segment_sum(src, seg, n):
    return jax.ops.segment_sum(src, seg, n)
kernel_name = 'mk_macaron_d2_jaxref_r8_38a9f0'

def setup_inputs(seed: int=0):
    np.random.seed(seed)
    _w = jnp.asarray

    def _L0_attn_setup():
        import math
        import jax, jax.numpy as jnp
        import numpy as np
        N_EMBD = 128
        N_HEAD = 16
        B, T = (2, 256)

        def _heads(t):
            b, s, d = t.shape
            return t.reshape(b, s, N_HEAD, d // N_HEAD).transpose(0, 2, 1, 3)
        key = jax.random.key(seed)
        ks = jax.random.split(key, 7)
        D = N_EMBD
        s = 0.02
        return {'x': jax.random.normal(ks[0], (B, T, D), dtype=jnp.float32), 'w_attn': jax.random.normal(ks[1], (2 * D, D), dtype=jnp.float32) * s, 'b_attn': jnp.zeros((2 * D,), dtype=jnp.float32), 'w_k2': jax.random.normal(ks[2], (D, D), dtype=jnp.float32) * s, 'b_k2': jnp.zeros((D,), dtype=jnp.float32), 'w_proj': jax.random.normal(ks[3], (D, D), dtype=jnp.float32) * s, 'b_proj': jnp.zeros((D,), dtype=jnp.float32)}
    _L0_attn_in = _L0_attn_setup()

    def _L0_ffn_setup():
        import jax, jax.numpy as jnp
        import numpy as np
        EMB = 128
        FF = 4 * EMB

        def _ternary(w):
            scale = jnp.maximum(jnp.mean(jnp.abs(w)), 1e-08)
            w_t = jnp.clip(jnp.round(w / scale), -1.0, 1.0)
            return w + jax.lax.stop_gradient(w_t - w)
        key = jax.random.key(seed)
        kx, k1, k2, kb1, kb2 = jax.random.split(key, 5)
        x = jax.random.normal(kx, (4, 256, EMB), dtype=jnp.float32)
        lim1 = 1.0 / np.sqrt(EMB)
        lim2 = 1.0 / np.sqrt(FF)
        W1 = jax.random.uniform(k1, (FF, EMB), jnp.float32, -lim1, lim1)
        b1 = jax.random.uniform(kb1, (FF,), jnp.float32, -lim1, lim1)
        W2 = jax.random.uniform(k2, (EMB, FF), jnp.float32, -lim2, lim2)
        b2 = jax.random.uniform(kb2, (EMB,), jnp.float32, -lim2, lim2)
        return {'x': x, 'W1': W1, 'b1': b1, 'W2': W2, 'b2': b2}
    _L0_ffn_in = _L0_ffn_setup()

    def _L1_attn_setup():
        import jax, jax.numpy as jnp
        import numpy as np
        from jax import lax
        N_EMBD = 128
        N_HEAD = 16
        HEAD_DIM = N_EMBD // N_HEAD
        EPS = 1e-06
        B, T = (4, 256)

        def _feature_map(x):
            return jax.nn.elu(x) + 1.0
        key = jax.random.key(seed)
        ks = jax.random.split(key, 5)
        scale = 1.0 / np.sqrt(N_EMBD)
        return {'x': jax.random.normal(ks[0], (B, T, N_EMBD), jnp.float32), 'W_attn': jax.random.normal(ks[1], (N_EMBD, 3 * N_EMBD), jnp.float32) * scale, 'b_attn': jax.random.normal(ks[2], (3 * N_EMBD,), jnp.float32) * 0.01, 'W_proj': jax.random.normal(ks[3], (N_EMBD, N_EMBD), jnp.float32) * scale, 'b_proj': jax.random.normal(ks[4], (N_EMBD,), jnp.float32) * 0.01}
    _L1_attn_in = _L1_attn_setup()

    def _L1_ffn_setup():
        import math
        import jax, jax.numpy as jnp
        import numpy as np
        B, S, D, F, E = (8, 256, 128, 512, 8)
        CAPACITY_FACTOR = 1.0
        key = jax.random.key(seed)
        k1, k2, k3, k4 = jax.random.split(key, 4)
        x = jax.random.normal(k1, (B, S, D), dtype=jnp.float32)
        Wr = jax.random.normal(k2, (D, E), dtype=jnp.float32) * (1.0 / math.sqrt(D))
        W1 = jax.random.normal(k3, (E, D, F), dtype=jnp.float32) * (1.0 / math.sqrt(D))
        W2 = jax.random.normal(k4, (E, F, D), dtype=jnp.float32) * (1.0 / math.sqrt(F))
        return {'x': x, 'Wr': Wr, 'W1': W1, 'W2': W2}
    _L1_ffn_in = _L1_ffn_setup()
    _d = {'L0_attn_x': _L0_attn_in['x'], 'L0_attn_w_attn': _L0_attn_in['w_attn'], 'L0_attn_b_attn': _L0_attn_in['b_attn'], 'L0_attn_w_k2': _L0_attn_in['w_k2'], 'L0_attn_b_k2': _L0_attn_in['b_k2'], 'L0_attn_w_proj': _L0_attn_in['w_proj'], 'L0_attn_b_proj': _L0_attn_in['b_proj'], 'L0_ffn_W1': _L0_ffn_in['W1'], 'L0_ffn_b1': _L0_ffn_in['b1'], 'L0_ffn_W2': _L0_ffn_in['W2'], 'L0_ffn_b2': _L0_ffn_in['b2'], 'L1_attn_W_attn': _L1_attn_in['W_attn'], 'L1_attn_b_attn': _L1_attn_in['b_attn'], 'L1_attn_W_proj': _L1_attn_in['W_proj'], 'L1_attn_b_proj': _L1_attn_in['b_proj'], 'L1_ffn_Wr': _L1_ffn_in['Wr'], 'L1_ffn_W1': _L1_ffn_in['W1'], 'L1_ffn_W2': _L1_ffn_in['W2']}
    _x0 = _d['L0_attn_x']
    _d['L0_attn_x'] = jax.random.normal(jax.random.fold_in(jax.random.key(seed), 1), (4, 512, 128), dtype=_x0.dtype)
    del _x0
    return _d

def reference(L0_attn_x, L0_attn_w_attn, L0_attn_b_attn, L0_attn_w_k2, L0_attn_b_k2, L0_attn_w_proj, L0_attn_b_proj, L0_ffn_W1, L0_ffn_b1, L0_ffn_W2, L0_ffn_b2, L1_attn_W_attn, L1_attn_b_attn, L1_attn_W_proj, L1_attn_b_proj, L1_ffn_Wr, L1_ffn_W1, L1_ffn_W2):

    def _L0_attn_ref(x, w_attn, b_attn, w_k2, b_k2, w_proj, b_proj):
        import math
        import jax, jax.numpy as jnp
        import numpy as np
        N_EMBD = 128
        N_HEAD = 16
        B, T = (2, 256)

        def _heads(t):
            b, s, d = t.shape
            return t.reshape(b, s, N_HEAD, d // N_HEAD).transpose(0, 2, 1, 3)
        b, t, d = x.shape
        hd = d // N_HEAD
        scale = 1.0 / math.sqrt(hd)
        qk = x @ w_attn.T + b_attn
        q, k = jnp.split(qk, 2, axis=-1)
        q, k, v = (_heads(q), _heads(k), _heads(x))
        scores = jnp.einsum('bhqd,bhkd->bhqk', q, k) * scale
        causal = jnp.tril(jnp.ones((t, t), dtype=bool))
        scores = jnp.where(causal, scores, -jnp.inf)
        y_ar = jnp.einsum('bhqk,bhkd->bhqd', jax.nn.softmax(scores, axis=-1), v)
        e = v[:, :, 1:, :] - y_ar[:, :, :-1, :]
        q2 = q[:, :, 1:, :]
        k2 = _heads(x[:, :-1] @ w_k2.T + b_k2)
        qa = -jax.nn.leaky_relu(-q2 * scale, negative_slope=0.02)
        ka = jax.nn.sigmoid(k2 * scale * 0.02)
        ma = jnp.einsum('bhqd,bhkd->bhqk', qa, ka)
        ma = jnp.where(jnp.tril(jnp.ones((t - 1, t - 1), dtype=bool)), ma, 0.0)
        y_ma = jnp.einsum('bhqk,bhkd->bhqd', ma, e)
        y_ma = jnp.concatenate([jnp.zeros_like(y_ma[:, :, :1, :]), y_ma], axis=2)

        def merge(z):
            return z.transpose(0, 2, 1, 3).reshape(b, t, d)
        out = merge(y_ar) @ w_proj.T + b_proj + (merge(y_ma) @ w_proj.T + b_proj)
        return out

    def _L0_ffn_ref(x, W1, b1, W2, b2):
        import jax, jax.numpy as jnp
        import numpy as np
        EMB = 128
        FF = 4 * EMB

        def _ternary(w):
            scale = jnp.maximum(jnp.mean(jnp.abs(w)), 1e-08)
            w_t = jnp.clip(jnp.round(w / scale), -1.0, 1.0)
            return w + jax.lax.stop_gradient(w_t - w)
        h = jnp.einsum('bsd,fd->bsf', x, _ternary(W1)) + b1
        h = jax.nn.gelu(h, approximate=False)
        out = jnp.einsum('bsf,df->bsd', h, _ternary(W2)) + b2
        return out

    def _L1_attn_ref(x, W_attn, b_attn, W_proj, b_proj):
        import jax, jax.numpy as jnp
        import numpy as np
        from jax import lax
        N_EMBD = 128
        N_HEAD = 16
        HEAD_DIM = N_EMBD // N_HEAD
        EPS = 1e-06
        B, T = (4, 256)

        def _feature_map(x):
            return jax.nn.elu(x) + 1.0
        Bb, Tt, C = x.shape
        qkv = x @ W_attn + b_attn
        q, k, v = jnp.split(qkv, 3, axis=-1)

        def to_heads(t):
            return t.reshape(Bb, Tt, N_HEAD, HEAD_DIM).transpose(1, 0, 2, 3)
        q = _feature_map(to_heads(q))
        k = _feature_map(to_heads(k))
        v = to_heads(v)

        def step(carry, inp):
            kv, ksum = carry
            qt, kt, vt = inp
            kv = kv + kt[..., :, None] * vt[..., None, :]
            ksum = ksum + kt
            num = jnp.einsum('bhi,bhij->bhj', qt, kv)
            den = jnp.einsum('bhi,bhi->bh', qt, ksum)[..., None] + EPS
            return ((kv, ksum), num / den)
        init = (jnp.zeros((Bb, N_HEAD, HEAD_DIM, HEAD_DIM), x.dtype), jnp.zeros((Bb, N_HEAD, HEAD_DIM), x.dtype))
        _, y = lax.scan(step, init, (q, k, v))
        y = y.transpose(1, 0, 2, 3).reshape(Bb, Tt, C)
        return y @ W_proj + b_proj

    def _L1_ffn_ref(x, Wr, W1, W2):
        import math
        import jax, jax.numpy as jnp
        import numpy as np
        B, S, D, F, E = (8, 256, 128, 512, 8)
        CAPACITY_FACTOR = 1.0
        b, s, d = x.shape
        t = b * s
        cap = max(math.ceil(t * CAPACITY_FACTOR / E), 1)
        xf = x.reshape(t, d)
        probs = jax.nn.softmax(xf.astype(jnp.float32) @ Wr, axis=-1)
        eidx = jnp.argmax(probs, axis=-1)
        p_tok = jnp.take_along_axis(probs, eidx[:, None], axis=1)[:, 0]
        onehot = jax.nn.one_hot(eidx, E, dtype=jnp.int32)
        rank_all = jnp.cumsum(onehot, axis=0) - onehot
        rank = jnp.take_along_axis(rank_all, eidx[:, None], axis=1)[:, 0]
        keep = rank < cap
        slot = jnp.where(keep, rank, cap)
        dispatch = jnp.zeros((E, cap + 1), dtype=jnp.int32).at[eidx, slot].set(jnp.arange(t, dtype=jnp.int32))
        valid = jnp.zeros((E, cap + 1), dtype=bool).at[eidx, slot].set(keep)
        dispatch = dispatch[:, :cap]
        valid = valid[:, :cap]
        xe = xf[dispatch]
        h = jnp.maximum(jnp.einsum('ecd,edf->ecf', xe, W1), 0.0)
        ye = jnp.einsum('ecf,efd->ecd', h, W2)
        pe = p_tok[dispatch]
        ye = ye * (pe * valid.astype(ye.dtype))[:, :, None]
        y = jnp.zeros((t, d), dtype=x.dtype).at[dispatch.reshape(-1)].add(ye.reshape(E * cap, d).astype(x.dtype))
        return y.reshape(b, s, d)
    x = L0_attn_x
    x = x + 0.5 * _L0_ffn_ref(_layernorm(x, axis=-1), L0_ffn_W1, L0_ffn_b1, L0_ffn_W2, L0_ffn_b2)
    x = x + _L0_attn_ref(_layernorm(x, axis=-1), L0_attn_w_attn, L0_attn_b_attn, L0_attn_w_k2, L0_attn_b_k2, L0_attn_w_proj, L0_attn_b_proj)
    x = x + 0.5 * _L0_ffn_ref(_layernorm(x, axis=-1), L0_ffn_W1, L0_ffn_b1, L0_ffn_W2, L0_ffn_b2)
    x = x + 0.5 * _L1_ffn_ref(_layernorm(x, axis=-1), L1_ffn_Wr, L1_ffn_W1, L1_ffn_W2)
    x = x + _L1_attn_ref(_layernorm(x, axis=-1), L1_attn_W_attn, L1_attn_b_attn, L1_attn_W_proj, L1_attn_b_proj)
    x = x + 0.5 * _L1_ffn_ref(_layernorm(x, axis=-1), L1_ffn_Wr, L1_ffn_W1, L1_ffn_W2)
    return x

_drawn_inputs = setup_inputs


def setup_inputs(seed=0):
    import zlib

    import numpy as np

    out = dict(_drawn_inputs(seed))
    spreads = {'L0_attn_b_attn': (0.0, 0.8), 'L0_attn_b_k2': (0.0, 2.0), 'L0_attn_b_proj': (0.0, 2.0)}
    factors = {'L0_attn_w_attn': 8.0,
     'L0_attn_w_k2': 200.0,
     'L0_attn_w_proj': 8.0,
     'L0_ffn_b1': 8.0,
     'L0_ffn_b2': 188.072,
     'L1_attn_W_attn': 8.0,
     'L1_attn_b_attn': 64.0,
     'L1_attn_W_proj': 8.0,
     'L1_attn_b_proj': 200.0,
     'L1_ffn_Wr': 8.0,
     'L1_ffn_W1': 8.0,
     'L1_ffn_W2': 8.0}
    for name, (base, spread) in spreads.items():
        noise = np.random.default_rng([zlib.crc32(name.encode()), seed]).standard_normal(out[name].shape)
        drawn = base * np.exp(spread * noise) if base else spread * noise
        out[name] = jnp.asarray(drawn.astype(out[name].dtype))
    for name, factor in factors.items():
        out[name] = (out[name] * factor).astype(out[name].dtype)
    return out
```

```python
from contextlib import ExitStack

import numpy as np

import concourse.bass as bass
from concourse import mybir

F32 = mybir.dt.float32
F32R = mybir.dt.float32r
BF16 = mybir.dt.bfloat16
I32 = mybir.dt.int32
ALU = mybir.AluOpType
ACT = mybir.ActivationFunctionType
AX = mybir.AxisListType

P = 128
D = 128
B, T = 4, 512
NT = T // P
H, HD = 16, 8
HL = 4
NS = H // HL
VW = 32
FF = 512
NF = FF // P
E, CAP = 8, B * T // 8
FE = 512
NG = CAP // P
NTOK = B * T
LN_EPS = 1e-5
DEN_EPS = 1e-6
SCALE = 1.0 / np.sqrt(HD)
MA_SCALE = SCALE * 0.02
NPAIR = NT * (NT + 1) // 2
MASKED = -1e30
LOADS = 14

CONST_COLS = {}


def constants():
    p = np.arange(P)[:, None]
    f = np.arange(P)[None, :]
    parts = {
        "ident": (p == f),
        "key_before": (p < f),
        "key_upto": (p <= f),
        "add_q": np.where(f > p, MASKED, 0.0),
        "add_k": np.where(p > f, MASKED, 0.0),
        "same_head": (p // HD == f // HD),
        "same_head_v": (p // HD == np.arange(H * VW)[None, :] // VW),
        "ones": np.ones((P, P)),
        "minus_half": np.full((P, NT), -0.5),
        "down": np.broadcast_to(np.tile(np.arange(E, 0, -1.0), NT), (P, NT * E)),
        "slot_base": np.broadcast_to(np.tile(CAP * np.arange(E), NT), (P, NT * E)),
        "spare_slot": NTOK + P * np.arange(NT)[None, :] + p,
    }
    col = 0
    for name, a in parts.items():
        CONST_COLS[name] = (col, col + a.shape[1])
        col += a.shape[1]
    return np.concatenate([np.asarray(a, np.float32) for a in parts.values()], axis=1)


CONSTS = constants()

SEMS = """held loaded experts_loaded w_abs w_sum w_scale w_half w_low w_tern zeroed pad_zero pad_one stats_in stats moments
var_eps rstd normed xt_mm xt_ready ffn_h ffn_act ffn_out ffn_base ffn_x x_in
qkv_mm proj_evac split_lo q_kept k_kept q_stacked k_stacked ma_q ma_k1 ma_k2 ma_k ma_hi ma_lo
mq_kept mk_kept mq_stacked mk_stacked ka_t_mm ka_tok v_aug smax_mm smax_red max_red max_t max_t_evac
max_rows st_mm exp_done pv_mm y_evac y_t rcp y_norm v_next err err_pad ma_mm ma_masked kv_mm kv_evac
ym_mm yar_mm yar_evac y_sum proj_mm attn_base attn_x x_kept
lg_mm lg_max lg_sub lg_exp top_eq top_cand top_max top_onehot top_sum top_p rank_mm rank_a rank_b rank_c
rank_d rank_e rank_f rank_g rank_h rank_i rank_j scattered
xg0 xg1 xg2 xg3 xg_t xg_evac h_mm h_relu_a h_relu_v ye_mm ye_evac ye_kept0 ye_kept1
gate_in idx_in gathered x_back mixed l1_mm l1_relu l1_min l1_exp l1_feat l1_hi l1_lo l1_v
l1_kt l1_ktok l1_qkept l1_kkept l1_qstk l1_kstk l1_s l1_masked l1_kv l1_kvev l1_y l1_yev l1_yt l1_den l1_rcp l1_yn
l1_y1t l1_y1ev l1_out l1_base l1_x out_done consts_bf bias_prep""".split()


def build(nc, x_in, bias_cols, w_attn_t, w_k2_t, w_proj_t, b_proj, w1_t, w2_t, b2,
          l1_w, l1_bv, l1_wp, l1_bp, wr, mw1, mw2, consts, out):
    ctx = ExitStack()
    with ctx:
        def sb(name, shape, dt=F32):
            return ctx.enter_context(nc.sbuf_tensor("sb_" + name, shape, dt))

        def psum(name, shape):
            return ctx.enter_context(nc.psum_tensor("ps_" + name, shape, F32))

        s = {n: ctx.enter_context(nc.semaphore("s_" + n)) for n in SEMS}
        ye_kept = [s["ye_kept0"], s["ye_kept1"]]
        xg_loaded = [s["xg0"], s["xg1"], s["xg2"], s["xg3"]]

        pair = [psum(f"pair{i}", [P, 2, 512]) for i in range(2)]
        accum = [psum(f"accum{i}", [P, 512]) for i in range(2)]
        turn = [psum(f"turn{i}", [P, 512]) for i in range(2)]

        cst = sb("cst", [P, CONSTS.shape[1]])

        def const(name):
            a, b = CONST_COLS[name]
            return cst[:, a:b]

        ident = const("ident")
        ident_bf = sb("ident_bf", [P, P], BF16)
        add_q_bf = sb("add_q_bf", [P, P], BF16)
        add_k_bf = sb("add_k_bf", [P, P], BF16)
        before_bf = sb("before_bf", [P, P], BF16)
        ones_bf = sb("ones_bf", [P, P], BF16)
        w1 = sb("w1", [P, FF])
        w2 = sb("w2", [P, NF, D])
        wst = sb("wst", [P, 8])
        wqk = sb("wqk", [P, 2 * D])
        wk2 = sb("wk2", [P, D])
        wp = sb("wp", [P, D])
        l1w = sb("l1w", [P, 3 * D])
        l1wp = sb("l1wp", [P, D])
        wr_sb = sb("wr", [P, E])
        cols = sb("cols", [P, NF + 6])
        rows = sb("rows", [P, 4, D])
        mw1_sb = sb("mw1", [P, E, FE])
        mw2_sb = sb("mw2", [P, E, NF, D])

        xa = sb("xa", [P, NT, D])
        xb = sb("xb", [P, NT, D])
        xn = [sb(f"xn{i}", [P, NT, D]) for i in range(3)]
        xnT = sb("xnT", [P, T])
        stats = sb("stats", [P, NT, 6])
        mv = sb("mv", [P, NT, 2])
        ve = sb("ve", [P, NT])
        rstd = sb("rstd", [P, NT])
        qf = sb("qf", [P, T])
        kf = sb("kf", [P, T])
        tmp = sb("tmp", [P, T])
        qs = sb("qs", [P, 2, T], F32R)
        ks = sb("ks", [P, 2, T], F32R)
        qaf = sb("qaf", [P, T])
        kaf = sb("kaf", [P, T])
        ka_tok = sb("ka_tok", [P, NT, D])
        k_pad = sb("k_pad", [P, H, T], F32R)
        q_stk = sb("q_stk", [P, NS, T], F32R)
        qa_pad = sb("qa_pad", [P, H, T], F32R)
        ka_stk = sb("ka_stk", [P, NS, T], F32R)
        v_aug = sb("v_aug", [P, NT, H, VW])
        e_pad = sb("e_pad", [P, NT, H, VW])
        v_next = sb("v_next", [P, NT, D])
        err = v_next
        work = sb("work", [P, 4, 2, 512])
        y_ar = sb("y_ar", [P, NT, D])
        yT = tmp
        y_tmp = [sb("y_tmp", [P, T]), kf]
        kv = sb("kv", [P, NT - 1, D])
        kv1 = v_next[:].rearrange("p t d -> p (t d)")
        mpart = sb("mpart", [P, NS, NPAIR, HL])
        mneg = sb("mneg", [P, NT, H])
        mT = sb("mT", [H, T], F32R)
        rcp = sb("rcp", [P, NT * H])
        r8 = [sb(f"r8_{i}", [P, NT, E]) for i in range(6)]
        r1 = [sb(f"r1_{i}", [P, NT]) for i in range(9)]
        onehot_bf = sb("onehot_bf", [P, NT, E], BF16)
        carry = sb("carry", [P, E])
        spare = sb("spare", [P, NT])
        slot = sb("slot", [P, NT], I32)
        slot_all = sb("slot_all", [P, NTOK // P], I32)
        gate_all = sb("gate_all", [P, NTOK // P])
        spent = e_pad[:].rearrange("p t h v -> p t (h v)")
        xg = spent[:, :, 0:NG * D].rearrange("p n (g d) -> p n g d", d=D)
        ye = spent[:, 0:2, NG * D:2 * NG * D].rearrange("p n (g d) -> p n g d", d=D)
        yg = spent[:, 2:NT, NG * D:2 * NG * D].rearrange("p n (g d) -> p n g d", d=D)

        def dram(name, shape):
            return nc.dram_tensor(name, shape, F32, kind="Internal").ap()

        q_scr = dram("q_scr", [H, 4, HD, T])
        k_scr = dram("k_scr", [H, 3, HD, T])
        mq_scr = dram("mq_scr", [H, 3, HD, T])
        mk_scr = dram("mk_scr", [H, 3, HD, T])
        x_scr = dram("x_scr", [NTOK, D])
        xe_scr = dram("xe_scr", [2 * NTOK, D])
        ye_scr = dram("ye_scr", [2 * NTOK, D])

        def tile_rows(ap, b):
            return ap[bass.ds(b * T, T), :].rearrange("(t p) d -> p t d", p=P)

        def heads(scr, hl):
            return scr.rearrange("(s h) c d t -> h (c d) s t", s=NS)[hl]

        def pad_rows(buf, hl, n):
            return buf[VW * hl:VW * hl + n].rearrange("r (s h) t -> r s h t", s=NS)[:, :, hl, :].bitcast(F32)

        def stk_rows(buf, hl, n):
            return buf[VW * hl:VW * hl + n].bitcast(F32)

        def bc(ap, n):
            return ap.unsqueeze(1).broadcast_to([P, n, ap.shape[1]])

        def h_act(fb):
            return work[:, fb, 0, :]

        def hold(eng, sem, value):
            eng.wait_ge(sem, value)
            eng.sem_inc(s["held"], 1)

        block = ctx.enter_context(nc.Block())

        @block.sync
        def _(sp):
            loads = [(cst[:], consts), (w1[:], w1_t), (w2[:], w2_t.rearrange("(f p) d -> p f d", p=P)),
                     (cols[:, 0:NF + 5], bias_cols),
                     (wqk[:], w_attn_t), (wk2[:], w_k2_t), (wp[:], w_proj_t), (wr_sb[:], wr),
                     (rows[:, 0, :], b2.rearrange("(a d) -> a d", a=1).broadcast_to([P, D])),
                     (rows[:, 1, :], b_proj.rearrange("(a d) -> a d", a=1).broadcast_to([P, D])),
                     (rows[:, 2, :], l1_bv.rearrange("(a d) -> a d", a=1).broadcast_to([P, D])),
                     (rows[:, 3, :], l1_bp.rearrange("(a d) -> a d", a=1).broadcast_to([P, D])),
                     (l1w[:], l1_w), (l1wp[:], l1_wp)]
            for dst, src in loads:
                sp.dma_start(dst, src).then_inc(s["loaded"], 16)
            sp.wait_ge(s["zeroed"], 1)
            zero = work[:].rearrange("p a b c -> p (a b c)")
            sp.dma_start(q_scr[:, 3], zero[:, 0:T]).then_inc(s["pad_zero"], 16)
            for half in range(2):
                r0 = half * NTOK // 2
                for dst in (xe_scr[r0:r0 + NTOK // 2], ye_scr[NTOK + r0:NTOK + r0 + NTOK // 2]):
                    sp.dma_start(dst.rearrange("(p r) d -> p (r d)", p=P), zero[:, 0:1024]).then_inc(s["pad_zero"], 16)
            sp.wait_ge(s["zeroed"], 3)
            ones_row = v_next[0:NS, :, :].rearrange("p a b -> p (a b)")
            for hl in range(HL):
                r = VW * hl + 3 * HD
                dst = k_pad[r:r + 1].rearrange("r (s h) t -> r s h t", s=NS)[:, :, hl, :].bitcast(F32)
                sp.dma_start(dst, ones_row).then_inc(s["pad_one"], 16)
            for e in range(E):
                sp.dma_start(mw1_sb[:, e, :], mw1[e]).then_inc(s["experts_loaded"], 16)
                sp.dma_start(mw2_sb[:, e], mw2[e].rearrange("(f p) d -> p f d", p=P)).then_inc(s["experts_loaded"], 16)

            def stack(hi_lo, scr, kept, order):
                for c, part in enumerate(order):
                    sp.dma_start(scr[:, c], hi_lo[:, part, :].bitcast(F32)).then_inc(kept, 16)

            with sp.Fori(0, B) as b:
                sp.dma_start(xa[:], tile_rows(x_in, b)).then_inc(s["x_in"], 16)
                hold(sp, s["normed"], 16 * b + 8)
                sp.dma_start(v_next[0:P - 1], xn[1][1:P]).then_inc(s["v_next"], 16)
                sp.dma_start(v_next[P - 1:P, 0:NT - 1, :], xn[1][0:1, 1:NT, :]).then_inc(s["v_next"], 16)
                hold(sp, s["split_lo"], 4 * b + 1)
                stack(qs, q_scr, s["q_kept"], (0, 1, 0))
                sp.wait_ge(s["split_lo"], 4 * b + 2)
                stack(ks, k_scr, s["k_kept"], (0, 0, 1))
                sp.wait_ge(s["q_kept"], 48 * b + 48)
                sp.wait_ge(s["pad_zero"], 80)
                for hl in range(HL):
                    sp.dma_start(stk_rows(q_stk, hl, 32), heads(q_scr, hl)).then_inc(s["q_stacked"], 16)
                sp.wait_ge(s["k_kept"], 48 * b + 48)
                for hl in range(HL):
                    sp.dma_start(pad_rows(k_pad, hl, 24), heads(k_scr, hl)).then_inc(s["k_stacked"], 16)
                sp.wait_ge(s["split_lo"], 4 * b + 3)
                stack(qs, mq_scr, s["mq_kept"], (0, 1, 0))
                sp.wait_ge(s["split_lo"], 4 * b + 4)
                stack(ks, mk_scr, s["mk_kept"], (0, 0, 1))
                sp.wait_ge(s["mq_kept"], 48 * b + 48)
                for hl in range(HL):
                    sp.dma_start(pad_rows(qa_pad, hl, 24), heads(mq_scr, hl)).then_inc(s["mq_stacked"], 16)
                sp.wait_ge(s["mk_kept"], 48 * b + 48)
                for hl in range(HL):
                    sp.dma_start(stk_rows(ka_stk, hl, 24), heads(mk_scr, hl)).then_inc(s["mk_stacked"], 16)
                sp.wait_ge(s["max_t_evac"], b + 1)
                sp.wait_ge(s["smax_mm"], 20 * b + 20)
                for hl in range(HL):
                    r = VW * hl + 3 * HD
                    sp.dma_start(q_stk[r:r + 1].bitcast(F32), mT[NS * hl:NS * hl + NS, :].bitcast(F32)).then_inc(s["max_rows"], 16)
                hold(sp, s["ffn_x"], 2 * b + 2)
                sp.dma_start(tile_rows(x_scr, b), xb[:]).then_inc(s["x_kept"], 16)

            def experts(m):
                sp.wait_ge(s["scattered"], 16 * NT * B * (m + 1))
                for e in range(E):
                    n = E * m + e
                    if n >= 4:
                        sp.wait_ge(s["xg_t"], n - 3)
                    src = xe_scr[e * CAP:(e + 1) * CAP].rearrange("(g p) d -> p g d", p=P)
                    sp.dma_start(xg[:, n % 4], src).then_inc(xg_loaded[n % 4], 16)
                    if e >= 2:
                        answer(m, e - 2)
                answer(m, E - 2)
                answer(m, E - 1)

            def answer(m, e):
                n = E * m + e
                sp.wait_ge(s["ye_evac"], n + 1)
                dst = ye_scr[e * CAP:(e + 1) * CAP].rearrange("(g p) d -> p g d", p=P)
                sp.dma_start(dst, ye[:, n % 2]).then_inc(ye_kept[n % 2], 16)

            experts(0)
            with sp.Fori(0, B) as b:
                sp.wait_ge(s["x_kept"], 16 * B + 16)
                sp.dma_start(xa[:], tile_rows(x_scr, b)).then_inc(s["x_back"], 16)
                sp.wait_ge(s["l1_lo"], 2 * b + 1)
                stack(qs, mq_scr, s["l1_qkept"], (0, 1, 0))
                sp.wait_ge(s["l1_lo"], 2 * b + 2)
                stack(ks, mk_scr, s["l1_kkept"], (0, 0, 1))
                sp.wait_ge(s["l1_qkept"], 48 * b + 48)
                for hl in range(HL):
                    sp.dma_start(pad_rows(qa_pad, hl, 24), heads(mq_scr, hl)).then_inc(s["l1_qstk"], 16)
                sp.wait_ge(s["l1_kkept"], 48 * b + 48)
                for hl in range(HL):
                    sp.dma_start(stk_rows(ka_stk, hl, 24), heads(mk_scr, hl)).then_inc(s["l1_kstk"], 16)
                hold(sp, s["l1_x"], b + 1)
                sp.dma_start(tile_rows(x_scr, b), xb[:]).then_inc(s["x_kept"], 16)
            experts(1)
            with sp.Fori(0, B) as b:
                sp.wait_ge(s["mixed"], NT * (B + b))
                sp.wait_ge(s["x_kept"], 32 * B + 16)
                sp.dma_start(xa[:], tile_rows(x_scr, b)).then_inc(s["x_back"], 16)
                hold(sp, s["mixed"], NT * (B + b) + NT)
                sp.dma_start(tile_rows(out, b), xb[:]).then_inc(s["out_done"], 16)
            sp.wait_ge(s["out_done"], 16 * B + 16)
            sp.wait_ge(s["pad_zero"], 80)
            for kept in ye_kept:
                sp.wait_ge(kept, 16 * E)
            sp.wait_ge(s["scattered"], 16 * NT * B * 2)

        @block.gpsimd
        def _(pool):
            pool.memset(work[:], 0.0).then_inc(s["zeroed"], 1)
            pool.memset(v_next[:], 1.0).then_inc(s["zeroed"], 1)
            pool.memset(k_pad[:].bitcast(F32), 0.0).then_inc(s["zeroed"], 1)
            pool.memset(qa_pad[:].bitcast(F32), 0.0).then_inc(s["zeroed"], 1)
            pool.memset(ka_stk[:].bitcast(F32), 0.0).then_inc(s["zeroed"], 1)
            pool.memset(v_aug[:], 0.0).then_inc(s["zeroed"], 1)
            pool.memset(e_pad[:], 0.0).then_inc(s["zeroed"], 1)
            pool.memset(carry[:], 0.0).then_inc(s["zeroed"], 1)
            pool.wait_ge(s["zeroed"], 8)
            pool.memset(v_aug[:, :, :, HD:HD + 1], 1.0).then_inc(s["zeroed"], 1)
            pool.wait_ge(s["loaded"], 16 * LOADS)
            pool.tensor_scalar(rows[:, 0, :], rows[:, 0, :], 0.5, None, ALU.mult).then_inc(s["bias_prep"], 1)
            pool.tensor_scalar(rows[:, 1, :], rows[:, 1, :], 2.0, None, ALU.mult).then_inc(s["bias_prep"], 1)
            pool.tensor_scalar(cols[:, NF + 5:NF + 6], cols[:, NF + 2:NF + 3], -MA_SCALE, None, ALU.mult).then_inc(s["bias_prep"], 1)
            pool.tensor_copy(spare[:], const("spare_slot")).then_inc(s["bias_prep"], 1)
            pool.wait_ge(s["bias_prep"], 4)

            def rsqrt(r):
                hold(pool, s["moments"], NT * r + NT)
                pool.tensor_scalar(ve[:], mv[:, :, 1], LN_EPS, None, ALU.add).then_inc(s["var_eps"], 1)
                pool.wait_ge(s["var_eps"], r + 1)
                pool.tensor_tensor(rstd[:], ve[:], const("minus_half"), ALU.pow).then_inc(s["rstd"], 1)

            def add_bias(r, x, row, done):
                pool.wait_ge(s["normed"], NT * r + NT)
                pool.tensor_tensor(x[:], x[:], bc(rows[:, row, :], NT), ALU.add).then_inc(done, 1)

            def low(n, full, parts, sem, value):
                pool.wait_ge(sem, value)
                pool.tensor_tensor(parts[:, 1, :], full[:], parts[:, 0, :].bitcast(F32), ALU.subtract).then_inc(n, 1)

            def scatter(r):
                hold(pool, s["rank_j"], r + 1)
                pool.wait_ge(s["pad_zero"], 80)
                for t in range(NT):
                    pool.indirect_dma_start(xe_scr, bass.IndirectOffsetOnAxis(ap=slot[:, t:t + 1], axis=0),
                                            xn[2][:, t, :], None).then_inc(s["scattered"], 16)

            def gather(r, ready):
                for kept in ye_kept:
                    pool.wait_ge(kept, ready)
                hold(pool, s["idx_in"], r + 1)
                for t in range(NT):
                    pool.indirect_dma_start(yg[:, t // 2, t % 2, :], None, ye_scr,
                                            bass.IndirectOffsetOnAxis(ap=slot[:, t:t + 1], axis=0)).then_inc(s["gathered"], 16)

            with pool.Fori(0, B) as b:
                rsqrt(4 * b)
                add_bias(4 * b, xa, 0, s["ffn_base"])
                rsqrt(4 * b + 1)
                add_bias(4 * b + 1, xb, 1, s["attn_base"])
                pool.wait_ge(s["zeroed"], 9)
                pool.tensor_copy(v_aug[:].rearrange("p t h v -> p (t h) v")[:, :, 0:HD],
                                 xn[1][:].rearrange("p t (h d) -> p (t h) d", d=HD)).then_inc(s["v_aug"], 1)
                low(s["split_lo"], qf, qs, s["proj_evac"], 5 * b + 2)
                low(s["split_lo"], kf, ks, s["proj_evac"], 5 * b + 4)
                low(s["split_lo"], qaf, qs, s["ma_hi"], 2 * b + 1)
                low(s["split_lo"], kaf, ks, s["ma_hi"], 2 * b + 2)
                pool.wait_ge(s["y_norm"], NS * b + NS)
                pool.wait_ge(s["v_next"], 32 * b + 32)
                pool.tensor_tensor(err[:], v_next[:], y_ar[:], ALU.subtract).then_inc(s["err"], 1)
                hold(pool, s["err"], b + 1)
                for hl in range(HL):
                    dst = e_pad[:].rearrange("p t (s h) v -> p h (t s) v", s=NS)[:, hl, :, HD * hl:HD * hl + HD]
                    src = err[:].rearrange("p t (s h d) -> p h (t s) d", s=NS, h=HL)[:, hl]
                    pool.tensor_copy(dst, src).then_inc(s["err_pad"], 1)
                rsqrt(4 * b + 2)
                add_bias(4 * b + 2, xa, 0, s["ffn_base"])
                rsqrt(4 * b + 3)
                scatter(b)
            pool.wait_ge(s["rank_b"], 2 * B)
            pool.memset(carry[:], 0.0).then_inc(s["zeroed"], 1)
            pool.tensor_copy(spare[:], const("spare_slot")).then_inc(s["zeroed"], 1)
            with pool.Fori(0, B) as b:
                gather(b, 8 * E)
                rsqrt(4 * B + 2 * b)
                add_bias(4 * B + 2 * b, xb, 3, s["l1_base"])
                pool.wait_ge(s["l1_exp"], 2 * b + 1)
                pool.tensor_tensor(qaf[:], qf[:], tmp[:], ALU.add).then_inc(s["l1_feat"], 1)
                pool.wait_ge(s["l1_exp"], 2 * b + 2)
                pool.tensor_tensor(kaf[:], kf[:], y_tmp[0][:], ALU.add).then_inc(s["l1_feat"], 1)
                low(s["l1_lo"], qaf, qs, s["l1_hi"], 2 * b + 1)
                low(s["l1_lo"], kaf, ks, s["l1_hi"], 2 * b + 2)
                rsqrt(4 * B + 2 * b + 1)
                scatter(B + b)
            with pool.Fori(0, B) as b:
                gather(B + b, 16 * E)

        @block.scalar
        def _(act):
            def xt(r):
                act.wait_ge(s["xt_mm"], r + 1)
                act.copy(xnT[:], turn[0][:]).then_inc(s["xt_ready"], 1)

            def gelu(f):
                for fb in range(NF):
                    act.wait_ge(s["ffn_h"], NF * f + fb + 1)
                    act.activation(h_act(fb), pair[fb // 2][:, fb % 2, :], ACT.Gelu,
                                   bias=cols[:, fb:fb + 1]).then_inc(s["ffn_act"], 1)

            def router_exp(r):
                act.wait_ge(s["lg_sub"], r + 1)
                act.activation(r8[1][:], r8[0][:], ACT.Exp).then_inc(s["lg_exp"], 1)

            act.wait_ge(s["bias_prep"], 4)
            with act.Fori(0, B) as b:
                xt(4 * b)
                gelu(2 * b)
                xt(4 * b + 1)
                bq, bk = cols[:, NF:NF + 1], cols[:, NF + 1:NF + 2]
                act.wait_ge(s["qkv_mm"], 3 * b + 1)
                act.activation(qf[:], pair[0][:, 0, :], ACT.Identity, bias=bq).then_inc(s["proj_evac"], 1)
                act.activation(qs[:, 0, :], pair[0][:, 0, :], ACT.Identity, bias=bq).then_inc(s["proj_evac"], 1)
                act.wait_ge(s["qkv_mm"], 3 * b + 2)
                act.activation(kf[:], pair[0][:, 1, :], ACT.Identity, bias=bk).then_inc(s["proj_evac"], 1)
                act.activation(ks[:, 0, :], pair[0][:, 1, :], ACT.Identity, bias=bk).then_inc(s["proj_evac"], 1)
                act.wait_ge(s["qkv_mm"], 3 * b + 3)
                act.activation(tmp[:], pair[1][:, 0, :], ACT.Exp, bias=cols[:, NF + 5:NF + 6],
                               scale=-MA_SCALE).then_inc(s["proj_evac"], 1)
                act.wait_ge(s["ma_q"], b + 1)
                act.wait_ge(s["q_kept"], 48 * b + 48)
                act.copy(qs[:, 0, :], qaf[:]).then_inc(s["ma_hi"], 1)
                act.wait_ge(s["ma_k"], b + 1)
                act.wait_ge(s["k_kept"], 48 * b + 48)
                act.copy(ks[:, 0, :], kaf[:]).then_inc(s["ma_hi"], 1)
                act.wait_ge(s["ka_t_mm"], b + 1)
                act.copy(ka_tok[:].rearrange("p t d -> p (t d)"), turn[1][:]).then_inc(s["ka_tok"], 1)
                act.wait_ge(s["max_t"], b + 1)
                act.copy(mT[:], turn[0][0:H, :]).then_inc(s["max_t_evac"], 1)
                for n in range(NS * NT):
                    w = T - P * (n % NT)
                    for pr in range(2):
                        u = 2 * n + pr
                        act.wait_ge(s["st_mm"], 2 * NS * NT * b + u + 1)
                        if n >= 2:
                            act.wait_ge(s["pv_mm"], NS * NT * b + n - 1)
                        act.activation(work[:, 2 * (n % 2) + pr, :, 0:w], pair[u % 2][:, :, 0:w], ACT.Exp,
                                       scale=SCALE).then_inc(s["exp_done"], 1)
                act.wait_ge(s["yar_mm"], b + 1)
                act.copy(y_tmp[0][:], turn[0][:]).then_inc(s["yar_evac"], 1)
                xt(4 * b + 2)
                gelu(2 * b + 1)
                xt(4 * b + 3)
                router_exp(b)
                act.wait_ge(s["scattered"], 16 * NT * b + 16 * NT)

            def relu_experts(m):
                for e in range(E):
                    n = E * m + e
                    act.wait_ge(s["xg_t"], n + 1)
                    act.copy(y_tmp[n % 2][:, 0:CAP], turn[n % 2][:, 0:CAP]).then_inc(s["xg_evac"], 1)
                    act.wait_ge(s["h_mm"], n + 1)
                    act.activation(work[:, n % 2, 0, :], pair[n % 2][:, 0, :], ACT.Relu).then_inc(s["h_relu_a"], 1)

            relu_experts(0)
            with act.Fori(0, B) as b:
                xt(4 * B + 2 * b)
                bq, bk = cols[:, NF + 3:NF + 4], cols[:, NF + 4:NF + 5]
                act.wait_ge(s["l1_mm"], 3 * b + 1)
                act.activation(qf[:], pair[0][:, 0, :], ACT.Relu, bias=bq).then_inc(s["l1_relu"], 1)
                act.wait_ge(s["l1_mm"], 3 * b + 2)
                act.activation(kf[:], pair[0][:, 1, :], ACT.Relu, bias=bk).then_inc(s["l1_relu"], 1)
                act.wait_ge(s["l1_min"], 2 * b + 1)
                act.activation(tmp[:], tmp[:], ACT.Exp).then_inc(s["l1_exp"], 1)
                act.wait_ge(s["l1_min"], 2 * b + 2)
                act.activation(y_tmp[0][:], y_tmp[0][:], ACT.Exp).then_inc(s["l1_exp"], 1)
                act.wait_ge(s["l1_feat"], 2 * b + 1)
                act.copy(qs[:, 0, :], qaf[:]).then_inc(s["l1_hi"], 1)
                act.wait_ge(s["l1_feat"], 2 * b + 2)
                act.copy(ks[:, 0, :], kaf[:]).then_inc(s["l1_hi"], 1)
                act.wait_ge(s["l1_kt"], b + 1)
                act.copy(ka_tok[:].rearrange("p t d -> p (t d)"), turn[1][:]).then_inc(s["l1_ktok"], 1)
                act.wait_ge(s["l1_y1t"], b + 1)
                act.copy(yT[:], turn[1][:]).then_inc(s["l1_y1ev"], 1)
                xt(4 * B + 2 * b + 1)
                router_exp(B + b)
                act.wait_ge(s["scattered"], 16 * NT * (B + b) + 16 * NT)
            relu_experts(1)

        @block.vector
        def _(dve):
            dve.sem_inc(s["x_kept"], 16)
            dve.sem_inc(s["out_done"], 16)
            dve.wait_ge(s["loaded"], 16 * LOADS)
            w2_flat = w2[:].rearrange("p f d -> p (f d)")
            for i, w in enumerate((w1[:], w2_flat)):
                dve.tensor_reduce(wst[:, i:i + 1], w, AX.X, ALU.add, apply_absolute_value=True).then_inc(s["w_abs"], 1)
            dve.wait_ge(s["w_sum"], 1)
            dve.tensor_scalar(wst[:, 2:4], turn[0][:, 0:2], 1.0 / (FF * D), 1e-8, ALU.mult, ALU.max).then_inc(s["w_scale"], 1)
            dve.wait_ge(s["w_scale"], 1)
            dve.tensor_scalar(wst[:, 4:6], wst[:, 2:4], 0.5, None, ALU.mult).then_inc(s["w_half"], 1)
            dve.tensor_scalar(wst[:, 6:8], wst[:, 2:4], -0.5, None, ALU.mult).then_inc(s["w_half"], 1)
            dve.wait_ge(s["w_half"], 2)
            for i, w in enumerate((w1[:], w2_flat)):
                dve.tensor_scalar(tmp[:], w, wst[:, 6 + i:7 + i], None, ALU.is_lt).then_inc(s["w_low"], 1)
                dve.wait_ge(s["w_low"], i + 1)
                dve.scalar_tensor_tensor(out=w, in0=w, scalar=wst[:, 4 + i:5 + i], in1=tmp[:],
                                         op0=ALU.is_gt, op1=ALU.subtract).then_inc(s["w_tern"], 1)
                dve.wait_ge(s["w_tern"], i + 1)
            for dst, name in ((ident_bf, "ident"), (add_q_bf, "add_q"), (add_k_bf, "add_k"),
                              (before_bf, "key_before"), (ones_bf, "ones")):
                dve.tensor_copy(dst[:], const(name)).then_inc(s["consts_bf"], 1)

            def norm(r, x, dst):
                for t in range(NT):
                    dve.bn_stats(stats[:, t, :], x[:, t, :]).then_inc(s["stats"], 1)
                hold(dve, s["stats"], NT * r + NT)
                for t in range(NT):
                    dve.bn_aggr(mv[:, t, :], stats[:, t, :]).then_inc(s["moments"], 1)
                dve.wait_ge(s["rstd"], r + 1)
                for t in range(NT):
                    dve.tensor_scalar(dst[:, t, :], x[:, t, :], mv[:, t, 0:1], rstd[:, t:t + 1],
                                      ALU.subtract, ALU.mult).then_inc(s["normed"], 1)

            def flat(a):
                return a[:].rearrange("p t d -> p (t d)")

            def ffn_x(f, x, dst):
                dve.wait_ge(s["ffn_out"], f + 1)
                dve.wait_ge(s["ffn_base"], f + 1)
                dve.scalar_tensor_tensor(out=flat(dst), in0=accum[0][:], scalar=0.5, in1=flat(x),
                                         op0=ALU.mult, op1=ALU.add).then_inc(s["ffn_x"], 1)
                dve.wait_ge(s["ffn_x"], f + 1)

            def route(r):
                lg = turn[1][:, 0:NT * E].rearrange("p (t e) -> p t e", e=E)
                dve.wait_ge(s["lg_mm"], r + 1)
                dve.tensor_reduce(r1[0][:], lg, AX.X, ALU.max).then_inc(s["lg_max"], 1)
                dve.wait_ge(s["lg_max"], r + 1)
                dve.tensor_tensor(r8[0][:], lg, r1[0][:].unsqueeze(2).broadcast_to([P, NT, E]), ALU.subtract).then_inc(s["lg_sub"], 1)
                dve.wait_ge(s["lg_sub"], r + 1)
                dve.scalar_tensor_tensor(out=r8[2][:].rearrange("p t e -> p (t e)"), in0=r8[0][:].rearrange("p t e -> p (t e)"),
                                         scalar=0.0, in1=const("down"), op0=ALU.is_ge, op1=ALU.mult).then_inc(s["top_cand"], 1)
                dve.wait_ge(s["top_cand"], r + 1)
                dve.tensor_reduce(r1[1][:], r8[2][:], AX.X, ALU.max).then_inc(s["top_max"], 1)
                dve.wait_ge(s["top_max"], r + 1)
                top = r1[1][:].unsqueeze(2).broadcast_to([P, NT, E])
                dve.tensor_tensor(onehot_bf[:], r8[2][:], top, ALU.is_equal).then_inc(s["top_onehot"], 1)
                dve.tensor_tensor(r8[3][:], r8[2][:], top, ALU.is_equal).then_inc(s["top_eq"], 1)
                dve.wait_ge(s["lg_exp"], r + 1)
                dve.tensor_reduce(r1[2][:], r8[1][:], AX.X, ALU.add).then_inc(s["top_sum"], 1)
                dve.wait_ge(s["top_sum"], r + 1)
                dve.reciprocal(r1[3][:], r1[2][:]).then_inc(s["top_p"], 1)
                rk = accum[1][:, 0:NT * E].rearrange("p (t e) -> p t e", e=E)
                total = accum[1][:, NT * E:NT * E + E]
                dve.wait_ge(s["rank_mm"], r + 1)
                dve.tensor_tensor(r8[4][:], rk, bc(carry[:], NT), ALU.add).then_inc(s["rank_a"], 1)
                dve.wait_ge(s["rank_a"], r + 1)
                dve.tensor_tensor(carry[:], carry[:], total, ALU.add).then_inc(s["rank_b"], 1)
                dve.tensor_tensor(r8[4][:], r8[4][:], r8[3][:], ALU.mult).then_inc(s["rank_c"], 1)
                dve.tensor_tensor(r8[5][:].rearrange("p t e -> p (t e)"), r8[3][:].rearrange("p t e -> p (t e)"),
                                  const("slot_base"), ALU.mult).then_inc(s["rank_c"], 1)
                dve.wait_ge(s["rank_c"], 2 * r + 2)
                dve.tensor_reduce(r1[4][:], r8[4][:], AX.X, ALU.add).then_inc(s["rank_d"], 1)
                dve.tensor_reduce(r1[5][:], r8[5][:], AX.X, ALU.add).then_inc(s["rank_d"], 1)
                dve.wait_ge(s["rank_d"], 2 * r + 2)
                dve.tensor_scalar(r1[6][:], r1[4][:], float(CAP), None, ALU.is_lt).then_inc(s["rank_e"], 1)
                dve.tensor_tensor(r1[7][:], r1[4][:], r1[5][:], ALU.add).then_inc(s["rank_e"], 1)
                dve.wait_ge(s["rank_e"], 2 * r + 2)
                dve.tensor_tensor(r1[7][:], r1[7][:], spare[:], ALU.subtract).then_inc(s["rank_f"], 1)
                dve.scalar_tensor_tensor(out=gate_all[:, bass.ds((r - B if r is not None and late[0] else r) * NT, NT)],
                                         in0=r1[6][:], scalar=0.5, in1=r1[3][:],
                                         op0=ALU.mult, op1=ALU.mult).then_inc(s["rank_h"], 1)
                dve.wait_ge(s["rank_f"], r + 1)
                dve.tensor_tensor(r1[7][:], r1[7][:], r1[6][:], ALU.mult).then_inc(s["rank_g"], 1)
                dve.wait_ge(s["rank_g"], r + 1)
                dve.tensor_tensor(slot[:], r1[7][:], spare[:], ALU.add).then_inc(s["rank_j"], 1)
                hold(dve, s["rank_j"], r + 1)
                dve.tensor_copy(slot_all[:, bass.ds((r - B if late[0] else r) * NT, NT)], slot[:]).then_inc(s["rank_i"], 1)
                dve.tensor_scalar(spare[:], spare[:], float(T), None, ALU.add).then_inc(s["rank_b"], 1)
                dve.wait_ge(s["rank_b"], 2 * r + 2)

            late = [False]

            with dve.Fori(0, B) as b:
                dve.wait_ge(s["x_in"], 16 * b + 16)
                norm(4 * b, xa, xn[0])
                dve.wait_ge(s["x_kept"], 16 * b + 16)
                ffn_x(2 * b, xa, xb)
                norm(4 * b + 1, xb, xn[1])
                dve.wait_ge(s["proj_evac"], 5 * b + 1)
                dve.scalar_tensor_tensor(out=qaf[:], in0=qf[:], scalar=0.02, in1=qf[:],
                                         op0=ALU.mult, op1=ALU.min).then_inc(s["ma_q"], 1)
                dve.wait_ge(s["proj_evac"], 5 * b + 5)
                dve.tensor_scalar(tmp[:], tmp[:], 1.0, None, ALU.add).then_inc(s["ma_k1"], 1)
                dve.wait_ge(s["ma_k1"], b + 1)
                dve.reciprocal(kaf[:], tmp[:]).then_inc(s["ma_k"], 1)
                for n in range(NS * NPAIR // 2):
                    hs, i = n // (NPAIR // 2), 2 * (n % (NPAIR // 2))
                    dve.wait_ge(s["smax_mm"], NS * NPAIR // 2 * b + n + 1)
                    dve.tensor_reduce(mpart[:, hs, i:i + 2, :].rearrange("p i h -> p (i h)"),
                                      pair[n % 2][:].rearrange("p a (h k) -> p (a h) k", h=HL),
                                      AX.X, ALU.max).then_inc(s["smax_red"], 1)
                dve.wait_ge(s["smax_red"], NS * NPAIR // 2 * (b + 1))
                for t in range(NT):
                    i = t * (t + 1) // 2
                    dve.tensor_reduce(mneg[:, t, :].rearrange("p (h s) -> p s h", s=NS),
                                      mpart[:, :, i:i + t + 1, :].rearrange("p s i h -> p s h i"),
                                      AX.X, ALU.max, negate=True).then_inc(s["max_red"], 1)
                for hs in range(NS):
                    dve.wait_ge(s["pv_mm"], NS * NT * b + NT * hs + NT)
                    dve.wait_ge(s["y_t"], NS * b + hs - 1) if hs >= 2 else None
                    dve.tensor_copy(y_tmp[hs % 2][:], accum[hs % 2][:]).then_inc(s["y_evac"], 1)
                    dve.wait_ge(s["y_t"], NS * b + hs + 1)
                    y = turn[hs % 2][:].rearrange("p (t h v) -> p t h v", t=NT, h=HL)
                    rc = rcp[:, 0:NT * HL].rearrange("p (t h) -> p t h", t=NT)
                    dve.reciprocal(rc, y[:, :, :, HD]).then_inc(s["rcp"], 1)
                    dve.wait_ge(s["rcp"], NS * b + hs + 1)
                    dve.tensor_tensor(y_ar[:].rearrange("p t (s h d) -> p s t h d", s=NS, h=HL)[:, hs],
                                      y[:, :, :, 0:HD], rc.unsqueeze(3).broadcast_to([P, NT, HL, HD]),
                                      ALU.mult).then_inc(s["y_norm"], 1)
                    dve.wait_ge(s["y_norm"], NS * b + hs + 1)
                for n in range(2 * NT):
                    dve.wait_ge(s["ma_mm"], 2 * NT * b + n + 1)
                    if n >= 4:
                        dve.wait_ge(s["ym_mm"], NT * b + (n - 4) // 2 + 1)
                    dve.tensor_tensor(work[:, n % 4].rearrange("p a (h q) -> p (a h) q", h=HL),
                                      pair[n % 2][:].rearrange("p a (h q) -> p (a h) q", h=HL),
                                      bc(const("key_before"), 2 * HL), ALU.mult).then_inc(s["ma_masked"], 1)
                    if n % 2 == 1 and n // 2 < NT - 1:
                        dve.wait_ge(s["kv_mm"], (NT - 1) * b + n // 2 + 1)
                        dve.tensor_tensor(kv[:, n // 2, :], turn[1][:, 0:D], const("same_head"), ALU.mult).then_inc(s["kv_evac"], 1)
                dve.wait_ge(s["ym_mm"], NT * b + NT)
                dve.wait_ge(s["yar_evac"], b + 1)
                dve.scalar_tensor_tensor(out=yT[:], in0=accum[0][:], scalar=SCALE, in1=y_tmp[0][:],
                                         op0=ALU.mult, op1=ALU.add).then_inc(s["y_sum"], 1)
                dve.wait_ge(s["proj_mm"], b + 1)
                dve.wait_ge(s["attn_base"], b + 1)
                dve.tensor_tensor(flat(xa), accum[1][:], flat(xb), ALU.add).then_inc(s["attn_x"], 1)
                dve.wait_ge(s["attn_x"], b + 1)
                norm(4 * b + 2, xa, xn[0])
                ffn_x(2 * b + 1, xa, xb)
                norm(4 * b + 3, xb, xn[2])
                route(b)

            def relu_experts(m):
                for e in range(E):
                    n = E * m + e
                    dve.wait_ge(s["h_mm"], n + 1)
                    dve.tensor_scalar(work[:, n % 2, 1, :], pair[n % 2][:, 1, :], 0.0, None, ALU.max).then_inc(s["h_relu_v"], 1)
                    dve.wait_ge(s["ye_mm"], n + 1)
                    if n >= 2:
                        dve.wait_ge(ye_kept[n % 2], 16 * (n // 2))
                    dve.tensor_copy(ye[:, n % 2].rearrange("p g d -> p (g d)"), accum[n % 2][:, 0:NG * D]).then_inc(s["ye_evac"], 1)

            def combine(r, b):
                dve.wait_ge(s["scattered"], 16 * NT * (r + B if late_combine[0] == 0 else 2 * B))
                dve.tensor_copy(slot[:], slot_all[:, bass.ds(b * NT, NT)]).then_inc(s["idx_in"], 1)
                dve.tensor_copy(r1[8][:], gate_all[:, bass.ds(b * NT, NT)]).then_inc(s["gate_in"], 1)
                dve.wait_ge(s["gate_in"], r + 1)
                dve.wait_ge(s["x_back"], 16 * r + 16)
                dve.wait_ge(s["gathered"], 16 * NT * r + 16 * NT)
                for t in range(NT):
                    dve.scalar_tensor_tensor(out=xb[:, t, :], in0=yg[:, t // 2, t % 2, :], scalar=r1[8][:, t:t + 1],
                                             in1=xa[:, t, :], op0=ALU.mult, op1=ALU.add).then_inc(s["mixed"], 1)
                dve.wait_ge(s["mixed"], NT * r + NT)

            late_combine = [0]
            relu_experts(0)
            late[0] = True
            dve.wait_ge(s["zeroed"], 11)
            with dve.Fori(0, B) as b:
                combine(b, b)
                norm(4 * B + 2 * b, xb, xn[1])
                for i, z in enumerate((tmp, y_tmp[0])):
                    dve.wait_ge(s["l1_relu"], 2 * b + i + 1)
                    dve.tensor_scalar(z[:], pair[0][:, i, :], cols[:, NF + 3 + i:NF + 4 + i], 0.0,
                                      ALU.add, ALU.min).then_inc(s["l1_min"], 1)
                dve.wait_ge(s["l1_mm"], 3 * b + 3)
                dve.tensor_tensor(v_aug[:, :, :, 0:HD],
                                  pair[1][:, 0, :].rearrange("p (t h d) -> p t h d", t=NT, h=H),
                                  rows[:, 2, :].rearrange("p (h d) -> p h d", h=H).unsqueeze(1).broadcast_to([P, NT, H, HD]),
                                  ALU.add).then_inc(s["l1_v"], 1)
                for t in range(NT):
                    for pr in range(2):
                        n = 2 * t + pr
                        dve.wait_ge(s["l1_s"], 2 * NT * b + n + 1)
                        if n >= 4:
                            dve.wait_ge(s["l1_y"], NT * b + (n - 4) // 2 + 1)
                        dve.tensor_tensor(work[:, n % 4].rearrange("p a (h q) -> p (a h) q", h=HL),
                                          pair[n % 2][:].rearrange("p a (h q) -> p (a h) q", h=HL),
                                          bc(const("key_upto"), 2 * HL), ALU.mult).then_inc(s["l1_masked"], 1)
                    dve.wait_ge(s["l1_y"], NT * b + t + 1)
                    dve.tensor_copy(y_tmp[1][:], accum[0][:]).then_inc(s["l1_yev"], 1)
                    if t < NT - 1:
                        dve.wait_ge(s["l1_kv"], (NT - 1) * b + t + 1)
                        dve.tensor_tensor(kv1, accum[1][:], const("same_head_v"), ALU.mult).then_inc(s["l1_kvev"], 1)
                    dve.wait_ge(s["l1_yt"], NT * b + t + 1)
                    y = turn[0][:].rearrange("p (h v) -> p h v", v=VW)
                    dve.tensor_scalar(rcp[:, 0:H], y[:, :, HD], DEN_EPS, None, ALU.add).then_inc(s["l1_den"], 1)
                    dve.wait_ge(s["l1_den"], NT * b + t + 1)
                    dve.reciprocal(rcp[:, H:2 * H], rcp[:, 0:H]).then_inc(s["l1_rcp"], 1)
                    dve.wait_ge(s["l1_rcp"], NT * b + t + 1)
                    dve.tensor_tensor(y_ar[:, t, :].rearrange("p (h d) -> p h d", d=HD), y[:, :, 0:HD],
                                      rcp[:, H:2 * H].unsqueeze(2).broadcast_to([P, H, HD]), ALU.mult).then_inc(s["l1_yn"], 1)
                dve.wait_ge(s["l1_out"], b + 1)
                dve.wait_ge(s["l1_base"], b + 1)
                dve.wait_ge(s["x_kept"], 16 * (B + b) + 16)
                dve.tensor_tensor(flat(xb), accum[1][:], flat(xb), ALU.add).then_inc(s["l1_x"], 1)
                dve.wait_ge(s["l1_x"], b + 1)
                norm(4 * B + 2 * b + 1, xb, xn[2])
                route(B + b)
            relu_experts(1)
            late_combine[0] = 1
            with dve.Fori(0, B) as b:
                dve.wait_ge(s["out_done"], 16 * b + 16)
                combine(B + b, b)

        @block.tensor
        def _(pe):
            def mm(dst, lhsT, rhs, start=True, stop=True):
                return pe.matmul(dst, lhsT, rhs, start=start, stop=stop, skip_group_check=True)

            def tile(a, t):
                return a[:, t * P:(t + 1) * P]

            def turn_tiles(dst, src):
                for t in range(NT):
                    last = pe.transpose(tile(dst, t), src[:, t, :], ident)
                return last

            def xt(r):
                pe.wait_ge(s["normed"], NT * r + NT)
                turn_tiles(turn[0], xn_of(r)).then_inc(s["xt_mm"], 1)
                pe.wait_ge(s["xt_ready"], r + 1)

            xn_now = [None]

            def xn_of(r):
                return xn_now[0]

            def ffn(f):
                for fb in range(NF):
                    mm(pair[fb // 2][:, fb % 2, :], tile(w1, fb), xnT[:]).then_inc(s["ffn_h"], 1)
                for fb in range(NF):
                    pe.wait_ge(s["ffn_act"], NF * f + fb + 1)
                    for t in range(NT):
                        last = mm(tile(accum[0], t), tile(h_act(fb), t), w2[:, fb, :],
                                  start=fb == 0 and t == 0, stop=fb == NF - 1)
                last.then_inc(s["ffn_out"], 1)

            def route(r):
                for t in range(NT):
                    last = mm(turn[1][:, t * E:(t + 1) * E], tile(xnT, t), wr_sb[:])
                last.then_inc(s["lg_mm"], 1)
                pe.wait_ge(s["top_onehot"], r + 1)
                for t in range(NT):
                    dst = accum[1][:, t * E:(t + 1) * E]
                    mm(dst, before_bf[:], onehot_bf[:, t, :], stop=t == 0)
                    for before in range(t):
                        mm(dst, ones_bf[:], onehot_bf[:, before, :], start=False, stop=before == t - 1)
                for t in range(NT):
                    last = mm(accum[1][:, NT * E:NT * E + E], ones_bf[:], onehot_bf[:, t, :], start=t == 0, stop=t == NT - 1)
                last.then_inc(s["rank_mm"], 1)

            pe.wait_ge(s["w_abs"], 2)
            mm(turn[0][:, 0:2], const("ones"), wst[:, 0:2]).then_inc(s["w_sum"], 1)
            pe.wait_ge(s["w_tern"], 2)
            pe.wait_ge(s["consts_bf"], 5)
            with pe.Fori(0, B) as b:
                xn_now[0] = xn[0]
                xt(4 * b)
                ffn(2 * b)
                xn_now[0] = xn[1]
                xt(4 * b + 1)
                mm(pair[0][:, 0, :], tile(wqk, 0), xnT[:]).then_inc(s["qkv_mm"], 1)
                mm(pair[0][:, 1, :], tile(wqk, 1), xnT[:]).then_inc(s["qkv_mm"], 1)
                mm(pair[1][:, 0, :], wk2[:], xnT[:]).then_inc(s["qkv_mm"], 1)
                pe.wait_ge(s["ma_k"], b + 1)
                for t in range(NT):
                    last = pe.transpose(tile(turn[1], t), tile(kaf, t), ident)
                last.then_inc(s["ka_t_mm"], 1)
                pe.wait_ge(s["q_stacked"], 64 * b + 64)
                pe.wait_ge(s["k_stacked"], 64 * b + 64)
                pe.wait_ge(s["pad_one"], 64)
                pe.wait_ge(s["proj_evac"], 5 * b + 5)
                pairs = [(qt, kt) for qt in range(NT) for kt in range(qt + 1)]
                for n in range(NS * NPAIR // 2):
                    hs, i = n // (NPAIR // 2), 2 * (n % (NPAIR // 2))
                    if n >= 2:
                        pe.wait_ge(s["smax_red"], NS * NPAIR // 2 * b + n - 1)
                    for a in range(2):
                        qt, kt = pairs[i + a]
                        dst = pair[n % 2][:, a, :]
                        last = mm(dst, tile(q_stk[:, hs, :], qt), k_pad[:, HL * hs:HL * hs + HL, kt * P:(kt + 1) * P],
                                  stop=qt != kt)
                        if qt == kt:
                            last = mm(dst, ident_bf[:], bc(add_q_bf[:], HL), start=False)
                    last.then_inc(s["smax_mm"], 1)
                pe.wait_ge(s["max_red"], NT * b + NT)
                for t in range(NT):
                    last = pe.transpose(turn[0][0:H, t * P:(t + 1) * P], mneg[:, t, :], ident)
                last.then_inc(s["max_t"], 1)

                def scores(n):
                    hs, kt = n // NT, n % NT
                    w = T - P * kt
                    for pr in range(2):
                        u = 2 * n + pr
                        if u >= 2:
                            pe.wait_ge(s["exp_done"], 2 * NS * NT * b + u - 1)
                        for a in range(2):
                            dst = pair[u % 2][:, a, :]
                            mm(dst[:, 0:w], tile(k_pad[:, HL * hs + 2 * pr + a, :], kt), q_stk[:, hs, kt * P:T], stop=False)
                            last = mm(dst[:, 0:P], ident_bf[:], add_k_bf[:], start=False)
                        last.then_inc(s["st_mm"], 1)

                def answers(n):
                    hs, kt = n // NT, n % NT
                    w = T - P * kt
                    pe.wait_ge(s["exp_done"], 2 * NS * NT * b + 2 * n + 2)
                    if kt == 0 and hs >= 2:
                        pe.wait_ge(s["y_evac"], NS * b + hs - 1)
                    for hl in range(HL):
                        last = mm(accum[hs % 2][VW * hl:VW * hl + VW, kt * P:T], v_aug[:, kt, HL * hs + hl, :],
                                  work[:, 2 * (n % 2) + hl // 2, hl % 2, 0:w], start=kt == 0, stop=kt == NT - 1)
                    last.then_inc(s["pv_mm"], 1)

                def turn_answers(hs):
                    pe.wait_ge(s["y_evac"], NS * b + hs + 1)
                    if hs >= 2:
                        pe.wait_ge(s["y_norm"], NS * b + hs - 1)
                    for t in range(NT):
                        last = pe.transpose(tile(turn[hs % 2], t), tile(y_tmp[hs % 2], t), ident)
                    last.then_inc(s["y_t"], 1)

                pe.wait_ge(s["max_rows"], 64 * b + 64)
                pe.wait_ge(s["v_aug"], b + 1)
                pe.wait_ge(s["ka_tok"], b + 1)
                scores(0)
                for n in range(NS * NT):
                    if n + 1 < NS * NT:
                        scores(n + 1)
                    answers(n)
                    if n % NT == 0 and n:
                        turn_answers(n // NT - 1)
                turn_answers(NS - 1)

                def ma_scores(t):
                    for pr in range(2):
                        n = 2 * t + pr
                        if n >= 2:
                            pe.wait_ge(s["ma_masked"], 2 * NT * b + n - 1)
                        for a in range(2):
                            hs = 2 * pr + a
                            last = mm(pair[n % 2][:, a, :], tile(ka_stk[:, hs, :], t),
                                      qa_pad[:, HL * hs:HL * hs + HL, t * P:(t + 1) * P])
                        last.then_inc(s["ma_mm"], 1)

                def ma_answers(t):
                    dst = tile(accum[0], t)
                    if t:
                        pe.wait_ge(s["kv_evac"], (NT - 1) * b + t)
                        mm(dst, kv[:, t - 1, :], tile(qaf, t), stop=False)
                    pe.wait_ge(s["ma_masked"], 2 * NT * b + 2 * t + 2)
                    for hl in range(HL):
                        for hs in range(NS):
                            last = mm(accum[0][VW * hs:VW * hs + VW, t * P:(t + 1) * P], e_pad[:, t, HL * hs + hl, :],
                                      tile(work[:, (2 * t + hs // 2) % 4, hs % 2, :], hl),
                                      start=t == 0 and hl == 0, stop=hl == HL - 1)
                    last.then_inc(s["ym_mm"], 1)

                pe.wait_ge(s["mq_stacked"], 64 * b + 64)
                pe.wait_ge(s["mk_stacked"], 64 * b + 64)
                ma_scores(0)
                pe.wait_ge(s["err"], b + 1)
                pe.wait_ge(s["err_pad"], HL * b + HL)
                pe.wait_ge(s["y_norm"], NS * b + NS)
                for t in range(NT):
                    if t < NT - 1:
                        if t:
                            pe.wait_ge(s["kv_evac"], (NT - 1) * b + t)
                        mm(turn[1][:, 0:D], ka_tok[:, t, :], err[:, t, :], start=t == 0, stop=True).then_inc(s["kv_mm"], 1)
                        ma_scores(t + 1)
                    ma_answers(t)
                turn_tiles(turn[0], y_ar).then_inc(s["yar_mm"], 1)
                pe.wait_ge(s["y_sum"], b + 1)
                for t in range(NT):
                    last = mm(tile(accum[1], t), tile(yT, t), wp[:])
                last.then_inc(s["proj_mm"], 1)
                xn_now[0] = xn[0]
                xt(4 * b + 2)
                ffn(2 * b + 1)
                xn_now[0] = xn[2]
                xt(4 * b + 3)
                route(b)

            def experts(m):
                def up(e):
                    n = E * m + e
                    pe.wait_ge(xg_loaded[n % 4], 16 * (n // 4 + 1))
                    for g in range(NG):
                        last = pe.transpose(tile(turn[n % 2], g), xg[:, n % 4, g, :], ident)
                    last.then_inc(s["xg_t"], 1)
                    pe.wait_ge(s["xg_evac"], n + 1)
                    if n >= 2:
                        pe.wait_ge(s["h_relu_v"], n - 1)
                        pe.wait_ge(s["h_relu_a"], n - 1)
                    for fb in range(NF):
                        last = mm(pair[n % 2][:, fb // 2, (fb % 2) * CAP:(fb % 2 + 1) * CAP],
                                  tile(mw1_sb[:, e, :], fb), y_tmp[n % 2][:, 0:CAP])
                    last.then_inc(s["h_mm"], 1)

                def down(e):
                    n = E * m + e
                    pe.wait_ge(s["h_relu_a"], n + 1)
                    pe.wait_ge(s["h_relu_v"], n + 1)
                    if n >= 2:
                        pe.wait_ge(s["ye_evac"], n - 1)
                    for g in range(NG):
                        for fb in range(NF):
                            last = mm(tile(accum[n % 2], g),
                                      work[:, n % 2, fb // 2, (fb % 2) * CAP + g * P:(fb % 2) * CAP + (g + 1) * P],
                                      mw2_sb[:, e, fb, :], start=fb == 0, stop=fb == NF - 1)
                    last.then_inc(s["ye_mm"], 1)

                up(0)
                for e in range(E):
                    if e + 1 < E:
                        up(e + 1)
                    down(e)

            pe.wait_ge(s["experts_loaded"], 16 * 2 * E)
            experts(0)
            with pe.Fori(0, B) as b:
                xn_now[0] = xn[1]
                xt(4 * B + 2 * b)
                mm(pair[0][:, 0, :], tile(l1w, 0), xnT[:]).then_inc(s["l1_mm"], 1)
                mm(pair[0][:, 1, :], tile(l1w, 1), xnT[:]).then_inc(s["l1_mm"], 1)
                for t in range(NT):
                    last = mm(tile(pair[1][:, 0, :], t), tile(xnT, t), tile(l1w, 2))
                last.then_inc(s["l1_mm"], 1)
                pe.wait_ge(s["l1_feat"], 2 * b + 2)
                for t in range(NT):
                    last = pe.transpose(tile(turn[1], t), tile(kaf, t), ident)
                last.then_inc(s["l1_kt"], 1)
                pe.wait_ge(s["l1_qstk"], 64 * b + 64)
                pe.wait_ge(s["l1_kstk"], 64 * b + 64)
                pe.wait_ge(s["l1_v"], b + 1)
                pe.wait_ge(s["l1_min"], 2 * b + 2)
                pe.wait_ge(s["l1_ktok"], b + 1)

                def l1_scores(t):
                    for pr in range(2):
                        n = 2 * t + pr
                        if n >= 2:
                            pe.wait_ge(s["l1_masked"], 2 * NT * b + n - 1)
                        for a in range(2):
                            hs = 2 * pr + a
                            last = mm(pair[n % 2][:, a, :], tile(ka_stk[:, hs, :], t),
                                      qa_pad[:, HL * hs:HL * hs + HL, t * P:(t + 1) * P])
                        last.then_inc(s["l1_s"], 1)

                def l1_answers(t):
                    pe.wait_ge(s["l1_masked"], 2 * NT * b + 2 * t + 2)
                    if t:
                        pe.wait_ge(s["l1_kvev"], (NT - 1) * b + t)
                        pe.wait_ge(s["l1_yev"], NT * b + t)
                    for hs in range(NS):
                        if t:
                            mm(tile(accum[0], hs), tile(kv1, hs), tile(qaf, t), stop=False)
                        for hl in range(HL):
                            last = mm(accum[0][VW * hl:VW * hl + VW, hs * P:(hs + 1) * P], v_aug[:, t, HL * hs + hl, :],
                                      tile(work[:, (2 * t + hs // 2) % 4, hs % 2, :], hl), start=t == 0)
                    last.then_inc(s["l1_y"], 1)

                l1_scores(0)
                for t in range(NT):
                    l1_answers(t)
                    if t < NT - 1:
                        mm(accum[1][:], ka_tok[:, t, :], v_aug[:, t].rearrange("p h v -> p (h v)"),
                           start=t == 0).then_inc(s["l1_kv"], 1)
                        l1_scores(t + 1)
                    pe.wait_ge(s["l1_yev"], NT * b + t + 1)
                    if t:
                        pe.wait_ge(s["l1_yn"], NT * b + t)
                    for hs in range(NS):
                        last = pe.transpose(tile(turn[0], hs), tile(y_tmp[1], hs), ident)
                    last.then_inc(s["l1_yt"], 1)
                pe.wait_ge(s["l1_yn"], NT * b + NT)
                turn_tiles(turn[1], y_ar).then_inc(s["l1_y1t"], 1)
                pe.wait_ge(s["l1_y1ev"], b + 1)
                for t in range(NT):
                    last = mm(tile(accum[1], t), tile(yT, t), l1wp[:])
                last.then_inc(s["l1_out"], 1)
                xn_now[0] = xn[2]
                xt(4 * B + 2 * b + 1)
                route(B + b)
            experts(1)


def kernel(**inputs):
    import numpy as _np
    import concourse.bacc as _bacc
    from concourse import mybir as _mybir
    from concourse.bass_utils import run_bass_kernel_spmd as _run

    g = {k: _np.asarray(v) for k, v in inputs.items()}
    ins = [
        ("x", g["L0_attn_x"].reshape(NTOK, D)),
        ("bias_cols", _np.concatenate([g["L0_ffn_b1"], g["L0_attn_b_attn"], g["L0_attn_b_k2"],
                                       g["L1_attn_b_attn"][:2 * D]]).reshape(-1, P).T),
        ("w_attn_t", g["L0_attn_w_attn"].T), ("w_k2_t", g["L0_attn_w_k2"].T),
        ("w_proj_t", g["L0_attn_w_proj"].T), ("b_proj", g["L0_attn_b_proj"]),
        ("w1_t", g["L0_ffn_W1"].T),
        ("w2_t", g["L0_ffn_W2"].T), ("b2", g["L0_ffn_b2"]),
        ("l1_w", g["L1_attn_W_attn"]), ("l1_bv", g["L1_attn_b_attn"][2 * D:]),
        ("l1_wp", g["L1_attn_W_proj"]), ("l1_bp", g["L1_attn_b_proj"]),
        ("wr", g["L1_ffn_Wr"]), ("mw1", g["L1_ffn_W1"]), ("mw2", g["L1_ffn_W2"]),
        ("consts", CONSTS),
    ]
    nc = _bacc.Bacc("TRN2", target_bir_lowering=False, num_devices=1)
    arrays, args = {}, []
    for name, a in ins:
        a = _np.ascontiguousarray(a)
        arrays[f"in_{name}"] = a
        args.append(nc.dram_tensor(f"in_{name}", a.shape, _mybir.dt.from_np(a.dtype), kind="ExternalInput").ap())
    args.append(nc.dram_tensor("out_0", (NTOK, D), _mybir.dt.float32, kind="ExternalOutput").ap())
    build(nc, *args)
    r = _run(nc, [arrays], core_ids=[0])
    return r.results[0]["out_0"].reshape(B, T, D)
```

```python
from contextlib import ExitStack

import numpy as np

import concourse.bass as bass
from concourse import mybir

F32 = mybir.dt.float32
F32R = mybir.dt.float32r
BF16 = mybir.dt.bfloat16
I32 = mybir.dt.int32
ALU = mybir.AluOpType
ACT = mybir.ActivationFunctionType
AX = mybir.AxisListType

P = 128
D = 128
B, T = 4, 512
NT = T // P
H, HD = 16, 8
HL = 4
NS = H // HL
VW = 32
FF = 512
NF = FF // P
E, CAP = 8, B * T // 8
LG = 256
FE = 512
NG = CAP // P
NTOK = B * T
LN_EPS = 1e-5
DEN_EPS = 1e-6
SCALE = 1.0 / np.sqrt(HD)
MA_SCALE = SCALE * 0.02
NPAIR = NT * (NT + 1) // 2
MASKED = -1e30
LOADS = 14

CONST_COLS = {}


def constants():
    p = np.arange(P)[:, None]
    f = np.arange(P)[None, :]
    parts = {
        "ident": (p == f),
        "key_before": (p < f),
        "key_upto": (p <= f),
        "add_q": np.where(f > p, MASKED, 0.0),
        "add_k": np.where(p > f, MASKED, 0.0),
        "same_head": (p // HD == f // HD),
        "same_head_v": (p // HD == np.arange(H * VW)[None, :] // VW),
        "ones": np.ones((P, P)),
        "minus_half": np.full((P, NT), -0.5),
        "down": np.broadcast_to(np.tile(np.arange(E, 0, -1.0), NT), (P, NT * E)),
        "slot_base": np.broadcast_to(np.tile(CAP * np.arange(E), NT), (P, NT * E)),
        "spare_slot": NTOK + P * np.arange(NT)[None, :] + p,
    }
    col = 0
    for name, a in parts.items():
        CONST_COLS[name] = (col, col + a.shape[1])
        col += a.shape[1]
    return np.concatenate([np.asarray(a, np.float32) for a in parts.values()], axis=1)


CONSTS = constants()

SEMS = """held loaded experts_loaded w_abs w_sum w_scale w_half w_low w_tern zeroed pad_zero pad_one stats_in stats moments
var_eps rstd normed xt_mm xt_ready ffn_h ffn_act ffn_out ffn_base ffn_x x_in
qkv_mm proj_evac split_hi split_lo q_kept k_kept q_stacked k_stacked ma_q ma_k1 ma_k2 ma_k ma_hi ma_lo
mq_kept mk_kept mq_stacked mk_stacked ka_t_mm ka_tok v_aug smax_mm smax_red max_red max_t max_t_evac
max_rows st_mm exp_done pv_mm y_evac y_t rcp y_norm v_next err err_pad ma_mm ma_masked kv_mm kv_evac
ym_mm yar_mm yar_evac y_sum proj_mm attn_base attn_x x_kept
lg_mm lg_max lg_sub lg_exp top_eq top_cand top_max top_onehot top_sum top_p rank_mm rank_a rank_b rank_c
rank_d rank_e rank_f rank_g rank_h rank_i rank_j scattered
xg0 xg1 xg2 xg3 xg_t xg_evac h_mm h_relu_a h_relu_v ye_mm ye_evac ye_kept0 ye_kept1
gate_in idx_in gathered x_back mixed l1_mm l1_relu l1_min l1_exp l1_feat l1_hi l1_lo l1_v
l1_kt l1_ktok l1_qkept l1_kkept l1_qstk l1_kstk l1_s l1_masked l1_kv l1_kvev l1_y l1_yev l1_yt l1_den l1_rcp l1_yn
l1_y1t l1_y1ev l1_out l1_base l1_x out_done consts_bf bias_prep""".split()


def build(nc, x_in, bias_cols, w_attn_t, w_k2_t, w_proj_t, b_proj, w1_t, w2_t, b2,
          l1_w, l1_bv, l1_wp, l1_bp, wr, mw1, mw2, consts, out):
    ctx = ExitStack()
    with ctx:
        def sb(name, shape, dt=F32):
            return ctx.enter_context(nc.sbuf_tensor("sb_" + name, shape, dt))

        def psum(name, shape):
            return ctx.enter_context(nc.psum_tensor("ps_" + name, shape, F32))

        s = {n: ctx.enter_context(nc.semaphore("s_" + n)) for n in SEMS}
        ye_kept = [s["ye_kept0"], s["ye_kept1"]]
        xg_loaded = [s["xg0"], s["xg1"], s["xg2"], s["xg3"]]

        pair = [psum(f"pair{i}", [P, 2, 512]) for i in range(2)]
        accum = [psum(f"accum{i}", [P, 512]) for i in range(2)]
        turn = [psum(f"turn{i}", [P, 512]) for i in range(2)]

        FRONT_STEPS = 10
        FRONT_AT = {2: 0, 3: 1, 4: 2, 5: 3, 6: 4, 7: 5, 10: 6, 11: 7, 12: 8, 13: 9}
        FRONT_BANKS = [turn[1]]
        TAIL_BANKS = [turn[1], turn[0]]

        cst = sb("cst", [P, CONSTS.shape[1]])

        def const(name):
            a, b = CONST_COLS[name]
            return cst[:, a:b]

        ident = const("ident")
        ident_bf = sb("ident_bf", [P, P], BF16)
        add_q_bf = sb("add_q_bf", [P, P], BF16)
        add_k_bf = sb("add_k_bf", [P, P], BF16)
        before_bf = sb("before_bf", [P, P], BF16)
        ones_bf = sb("ones_bf", [P, P], BF16)
        w1 = sb("w1", [P, FF])
        w2 = sb("w2", [P, NF, D])
        wst = sb("wst", [P, 8])
        wqk = sb("wqk", [P, 2 * D])
        wk2 = sb("wk2", [P, D])
        wp = sb("wp", [P, D])
        l1w = sb("l1w", [P, 3 * D])
        l1wp = sb("l1wp", [P, D])
        wr_sb = sb("wr", [P, E])
        cols = sb("cols", [P, NF + 6])
        rows = sb("rows", [P, 4, D])

        x0 = sb("x0", [P, NT, D])
        x1 = sb("x1", [P, NT, D])
        x_base = sb("x_base", [P, NT, D])
        xa = sb("xa", [P, NT, D])
        xb = sb("xb", [P, NT, D])
        xn = [sb(f"xn{i}", [P, NT, D]) for i in range(3)]
        xnT = sb("xnT", [P, T])
        h_act = sb("h_act", [P, NF, T])
        stats = sb("stats", [P, NT, 6])
        mv = sb("mv", [P, NT, 2])
        ve = sb("ve", [P, NT])
        rstd = sb("rstd", [P, NT])
        qf = sb("qf", [P, T])
        kf = sb("kf", [P, T])
        tmp = sb("tmp", [P, T])
        yT = sb("yT", [P, T])
        qs = sb("qs", [P, 2, T], F32R)
        ks = sb("ks", [P, 2, T], F32R)
        qaf = sb("qaf", [P, T])
        kaf = sb("kaf", [P, T])
        ka_tok = sb("ka_tok", [P, NT, D])
        with nc.sbuf_tensor("sb_k_pad", [P, H, T], F32R) as k_pad:
            pass
        mw1_sb = sb("mw1", [P, E, FE])
        mw2_sb = sb("mw2", [P, E, NF, D])
        q_stk = sb("q_stk", [P, NS, T], F32R)
        qa_pad = sb("qa_pad", [P, H, T], F32R)
        ka_stk = sb("ka_stk", [P, NS, T], F32R)
        v_aug = sb("v_aug", [P, NT, H, VW])
        e_pad = sb("e_pad", [P, NT, H, VW])
        v_next = sb("v_next", [P, NT, D])
        err = v_next
        work = sb("work", [P, 4, 2, 512])
        y_ar = sb("y_ar", [P, NT, D])
        y_tmp = [sb(f"y_tmp{i}", [P, T]) for i in range(2)]
        kv = sb("kv", [P, NT - 1, D])
        kv1 = v_next[:].rearrange("p t d -> p (t d)")
        mpart = sb("mpart", [P, NS, NPAIR, HL])
        mneg = sb("mneg", [P, NT, H])
        mT = sb("mT", [H, T], F32R)
        rcp = sb("rcp", [P, NT * H])
        r8 = [sb(f"r8_{i}", [P, NT, E]) for i in range(6)]
        r1 = [sb(f"r1_{i}", [P, NT]) for i in range(9)]
        onehot_bf = sb("onehot_bf", [P, NT, E], BF16)
        carry = sb("carry", [P, E])
        spare = sb("spare", [P, NT])
        slot = sb("slot", [P, NT], I32)
        slot_all = sb("slot_all", [P, NTOK // P], I32)
        gate_all = sb("gate_all", [P, NTOK // P])
        spent = e_pad[:].rearrange("p t h v -> p t (h v)")
        xg = spent[:, :, 0:NG * D].rearrange("p n (g d) -> p n g d", d=D)
        ye = spent[:, 0:2, NG * D:2 * NG * D].rearrange("p n (g d) -> p n g d", d=D)
        yg = spent[:, 2:NT, NG * D:2 * NG * D].rearrange("p n (g d) -> p n g d", d=D)

        def dram(name, shape):
            return nc.dram_tensor(name, shape, F32, kind="Internal").ap()

        q_scr = dram("q_scr", [H, 4, HD, T])
        k_scr = dram("k_scr", [H, 3, HD, T])
        mq_scr = dram("mq_scr", [H, 3, HD, T])
        mk_scr = dram("mk_scr", [H, 3, HD, T])
        x_scr = dram("x_scr", [NTOK, D])
        xe_scr = dram("xe_scr", [2 * NTOK, D])
        ye_scr = dram("ye_scr", [2 * NTOK, D])

        def tile_rows(ap, b):
            return ap[bass.ds(b * T, T), :].rearrange("(t p) d -> p t d", p=P)

        def heads(scr, hl):
            return scr.rearrange("(s h) c d t -> h (c d) s t", s=NS)[hl]

        def pad_rows(buf, hl, n):
            return buf[VW * hl:VW * hl + n].rearrange("r (s h) t -> r s h t", s=NS)[:, :, hl, :].bitcast(F32)

        def stk_rows(buf, hl, n):
            return buf[VW * hl:VW * hl + n].bitcast(F32)

        def bc(ap, n):
            return ap.unsqueeze(1).broadcast_to([P, n, ap.shape[1]])

        def ffn_of_front(b):
            return 0 if isinstance(b, int) and b == 0 else 2 * b - 1

        def ffn_of_tail(b):
            return 2 * B - 1 if isinstance(b, int) else 2 * b + 2

        def hold(eng, sem, value):
            eng.wait_ge(sem, value)
            eng.sem_inc(s["held"], 1)

        block = ctx.enter_context(nc.Block())

        @block.sync
        def _(sp):
            sp.dma_start(x0[:], tile_rows(x_in, 0)).then_inc(s["x_in"], 16)
            loads = [(cst[:], consts), (w1[:], w1_t), (w2[:], w2_t.rearrange("(f p) d -> p f d", p=P)),
                     (cols[:, 0:NF + 5], bias_cols),
                     (wqk[:], w_attn_t), (wk2[:], w_k2_t), (wp[:], w_proj_t), (wr_sb[:], wr),
                     (rows[:, 0, :], b2.rearrange("(a d) -> a d", a=1).broadcast_to([P, D])),
                     (rows[:, 1, :], b_proj.rearrange("(a d) -> a d", a=1).broadcast_to([P, D])),
                     (rows[:, 2, :], l1_bv.rearrange("(a d) -> a d", a=1).broadcast_to([P, D])),
                     (rows[:, 3, :], l1_bp.rearrange("(a d) -> a d", a=1).broadcast_to([P, D])),
                     (l1w[:], l1_w), (l1wp[:], l1_wp)]
            for dst, src in loads:
                sp.dma_start(dst, src).then_inc(s["loaded"], 16)
            sp.wait_ge(s["zeroed"], 1)
            zero = work[:].rearrange("p a b c -> p (a b c)")
            sp.dma_start(q_scr[:, 3], zero[:, 0:T]).then_inc(s["pad_zero"], 16)
            for half in range(2):
                r0 = half * NTOK // 2
                for dst in (xe_scr[r0:r0 + NTOK // 2], ye_scr[NTOK + r0:NTOK + r0 + NTOK // 2]):
                    sp.dma_start(dst.rearrange("(p r) d -> p (r d)", p=P), zero[:, 0:1024]).then_inc(s["pad_zero"], 16)
            sp.wait_ge(s["zeroed"], 3)
            ones_row = v_next[0:NS, :, :].rearrange("p a b -> p (a b)")
            for hl in range(HL):
                r = VW * hl + 3 * HD
                dst = k_pad[r:r + 1].rearrange("r (s h) t -> r s h t", s=NS)[:, :, hl, :].bitcast(F32)
                sp.dma_start(dst, ones_row).then_inc(s["pad_one"], 16)
            def stack(hi_lo, scr, kept, order):
                for c, part in enumerate(order):
                    sp.dma_start(scr[:, c], hi_lo[:, part, :].bitcast(F32)).then_inc(kept, 16)

            def keep_qk(b):
                hold(sp, s["split_lo"], 4 * b + 1)
                stack(qs, q_scr, s["q_kept"], (0, 1, 0))
                hold(sp, s["split_lo"], 4 * b + 2)
                stack(ks, k_scr, s["k_kept"], (0, 0, 1))

            def load_qk(b):
                hold(sp, s["q_kept"], 48 * b + 48)
                for hl in range(HL):
                    sp.dma_start(stk_rows(q_stk, hl, 32), heads(q_scr, hl)).then_inc(s["q_stacked"], 16)
                hold(sp, s["k_kept"], 48 * b + 48)
                for hl in range(HL):
                    sp.dma_start(pad_rows(k_pad, hl, 24), heads(k_scr, hl)).then_inc(s["k_stacked"], 16)

            def stack_features(b):
                hold(sp, s["split_lo"], 4 * b + 3)
                stack(qs, mq_scr, s["mq_kept"], (0, 1, 0))
                hold(sp, s["split_lo"], 4 * b + 4)
                stack(ks, mk_scr, s["mk_kept"], (0, 0, 1))
                sp.dma_start(v_next[0:P - 1], xn[1][1:P]).then_inc(s["v_next"], 16)
                sp.dma_start(v_next[P - 1:P, 0:NT - 1, :], xn[1][0:1, 1:NT, :]).then_inc(s["v_next"], 16)
                hold(sp, s["mq_kept"], 48 * b + 48)
                for hl in range(HL):
                    sp.dma_start(pad_rows(qa_pad, hl, 24), heads(mq_scr, hl)).then_inc(s["mq_stacked"], 16)
                hold(sp, s["mk_kept"], 48 * b + 48)
                for hl in range(HL):
                    sp.dma_start(stk_rows(ka_stk, hl, 24), heads(mk_scr, hl)).then_inc(s["mk_stacked"], 16)

            def max_rows(b):
                hold(sp, s["max_t_evac"], b + 1)
                for hl in range(HL):
                    r = VW * hl + 3 * HD
                    sp.dma_start(q_stk[r:r + 1].bitcast(F32), mT[NS * hl:NS * hl + NS, :].bitcast(F32)).then_inc(s["max_rows"], 16)

            def batch(b, ahead):
                if ahead:
                    sp.dma_start(x0[:], tile_rows(x_in, b + 1)).then_inc(s["x_in"], 16)
                    keep_qk(b + 1)
                hold(sp, s["st_mm"], 2 * NS * NT * (b + 1))
                if ahead:
                    load_qk(b + 1)
                    stack_features(b + 1)
                else:
                    for e in range(E):
                        sp.dma_start(mw1_sb[:, e, :], mw1[e]).then_inc(s["experts_loaded"], 16)
                        sp.dma_start(mw2_sb[:, e], mw2[e].rearrange("(f p) d -> p f d", p=P)).then_inc(s["experts_loaded"], 16)
                f = ffn_of_tail(b)
                hold(sp, s["ffn_x"], f + 1)
                sp.dma_start(tile_rows(x_scr, b), xb[:]).then_inc(s["x_kept"], 16)
                if ahead:
                    max_rows(b + 1)
                hold(sp, s["scattered"], 16 * NT * b + 16 * NT)

            sp.wait_ge(s["pad_zero"], 80)
            keep_qk(0)
            load_qk(0)
            stack_features(0)
            max_rows(0)
            with sp.Fori(0, B - 1) as b:
                batch(b, True)
            batch(B - 1, False)

            def experts(m):
                sp.wait_ge(s["scattered"], 16 * NT * B * (m + 1))
                for e in range(E):
                    n = E * m + e
                    if n >= 4:
                        sp.wait_ge(s["xg_t"], n - 3)
                    src = xe_scr[e * CAP:(e + 1) * CAP].rearrange("(g p) d -> p g d", p=P)
                    sp.dma_start(xg[:, n % 4], src).then_inc(xg_loaded[n % 4], 16)
                    if e >= 2:
                        answer(m, e - 2)
                answer(m, E - 2)
                answer(m, E - 1)

            def answer(m, e):
                n = E * m + e
                sp.wait_ge(s["ye_evac"], n + 1)
                dst = ye_scr[e * CAP:(e + 1) * CAP].rearrange("(g p) d -> p g d", p=P)
                sp.dma_start(dst, ye[:, n % 2]).then_inc(ye_kept[n % 2], 16)

            experts(0)
            with sp.Fori(0, B) as b:
                sp.wait_ge(s["x_kept"], 16 * B + 16)
                sp.dma_start(xa[:], tile_rows(x_scr, b)).then_inc(s["x_back"], 16)
                sp.wait_ge(s["l1_lo"], 2 * b + 1)
                stack(qs, mq_scr, s["l1_qkept"], (0, 1, 0))
                sp.wait_ge(s["l1_lo"], 2 * b + 2)
                stack(ks, mk_scr, s["l1_kkept"], (0, 0, 1))
                sp.wait_ge(s["l1_qkept"], 48 * b + 48)
                for hl in range(HL):
                    sp.dma_start(pad_rows(qa_pad, hl, 24), heads(mq_scr, hl)).then_inc(s["l1_qstk"], 16)
                sp.wait_ge(s["l1_kkept"], 48 * b + 48)
                for hl in range(HL):
                    sp.dma_start(stk_rows(ka_stk, hl, 24), heads(mk_scr, hl)).then_inc(s["l1_kstk"], 16)
                hold(sp, s["l1_x"], b + 1)
                sp.dma_start(tile_rows(x_scr, b), xb[:]).then_inc(s["x_kept"], 16)
            experts(1)
            with sp.Fori(0, B) as b:
                sp.wait_ge(s["mixed"], NT * (B + b))
                sp.wait_ge(s["x_kept"], 32 * B + 16)
                sp.dma_start(xa[:], tile_rows(x_scr, b)).then_inc(s["x_back"], 16)
                hold(sp, s["mixed"], NT * (B + b) + NT)
                sp.dma_start(tile_rows(out, b), xb[:]).then_inc(s["out_done"], 16)
            sp.wait_ge(s["out_done"], 16 * B + 16)
            sp.wait_ge(s["pad_zero"], 80)
            for kept in ye_kept:
                sp.wait_ge(kept, 16 * E)
            sp.wait_ge(s["scattered"], 16 * NT * B * 2)

        @block.gpsimd
        def _(pool):
            pool.memset(work[:], 0.0).then_inc(s["zeroed"], 1)
            pool.memset(v_next[:], 1.0).then_inc(s["zeroed"], 1)
            pool.memset(k_pad[:].bitcast(F32), 0.0).then_inc(s["zeroed"], 1)
            pool.memset(qa_pad[:].bitcast(F32), 0.0).then_inc(s["zeroed"], 1)
            pool.memset(ka_stk[:].bitcast(F32), 0.0).then_inc(s["zeroed"], 1)
            pool.memset(v_aug[:], 0.0).then_inc(s["zeroed"], 1)
            pool.memset(e_pad[:], 0.0).then_inc(s["zeroed"], 1)
            pool.memset(carry[:], 0.0).then_inc(s["zeroed"], 1)
            pool.wait_ge(s["zeroed"], 8)
            pool.memset(v_aug[:, :, :, HD:HD + 1], 1.0).then_inc(s["zeroed"], 1)
            pool.wait_ge(s["loaded"], 16 * LOADS)
            pool.tensor_scalar(rows[:, 0, :], rows[:, 0, :], 0.5, None, ALU.mult).then_inc(s["bias_prep"], 1)
            pool.tensor_scalar(rows[:, 1, :], rows[:, 1, :], 2.0, None, ALU.mult).then_inc(s["bias_prep"], 1)
            pool.tensor_scalar(cols[:, NF + 5:NF + 6], cols[:, NF + 2:NF + 3], -MA_SCALE, None, ALU.mult).then_inc(s["bias_prep"], 1)
            pool.tensor_copy(spare[:], const("spare_slot")).then_inc(s["bias_prep"], 1)
            pool.wait_ge(s["bias_prep"], 4)

            def rsqrt(r):
                hold(pool, s["moments"], NT * r + NT)
                pool.tensor_scalar(ve[:], mv[:, :, 1], LN_EPS, None, ALU.add).then_inc(s["var_eps"], 1)
                pool.wait_ge(s["var_eps"], r + 1)
                pool.tensor_tensor(rstd[:], ve[:], const("minus_half"), ALU.pow).then_inc(s["rstd"], 1)

            def add_bias(r, x, row, done):
                pool.wait_ge(s["normed"], NT * r + NT)
                pool.tensor_tensor(x[:], x[:], bc(rows[:, row, :], NT), ALU.add).then_inc(done, 1)

            def low(n, full, parts, sem, value):
                pool.wait_ge(sem, value)
                pool.tensor_tensor(parts[:, 1, :], full[:], parts[:, 0, :].bitcast(F32), ALU.subtract).then_inc(n, 1)

            def scatter(r):
                hold(pool, s["rank_j"], r + 1)
                pool.wait_ge(s["pad_zero"], 80)
                for t in range(NT):
                    pool.indirect_dma_start(xe_scr, bass.IndirectOffsetOnAxis(ap=slot[:, t:t + 1], axis=0),
                                            xn[2][:, t, :], None).then_inc(s["scattered"], 16)

            def gather(r, ready):
                for kept in ye_kept:
                    pool.wait_ge(kept, ready)
                hold(pool, s["idx_in"], r + 1)
                for t in range(NT):
                    pool.indirect_dma_start(yg[:, t // 2, t % 2, :], None, ye_scr,
                                            bass.IndirectOffsetOnAxis(ap=slot[:, t:t + 1], axis=0)).then_inc(s["gathered"], 16)

            def front(b):
                f = ffn_of_front(b)
                rsqrt(2 * f)
                add_bias(2 * f, x0, 0, s["ffn_base"])
                rsqrt(2 * f + 1)
                low(s["split_lo"], qf, qs, s["split_hi"], 2 * b + 1)
                low(s["split_lo"], kf, ks, s["split_hi"], 2 * b + 2)

            def values(b):
                pool.tensor_copy(v_aug[:].rearrange("p t h v -> p (t h) v")[:, :, 0:HD],
                                 xn[1][:].rearrange("p t (h d) -> p (t h) d", d=HD)).then_inc(s["v_aug"], 1)

            def features(b):
                low(s["split_lo"], qaf, qs, s["ma_hi"], 2 * b + 1)
                low(s["split_lo"], kaf, ks, s["ma_hi"], 2 * b + 2)
                pool.tensor_tensor(x_base[:], x1[:], bc(rows[:, 1, :], NT), ALU.add).then_inc(s["attn_base"], 1)

            def tail(b, ahead):
                hold(pool, s["y_norm"], NS * b + NS)
                pool.wait_ge(s["v_next"], 32 * b + 32)
                pool.tensor_tensor(err[:], v_next[:], y_ar[:], ALU.subtract).then_inc(s["err"], 1)
                hold(pool, s["err"], b + 1)
                for hl in range(HL):
                    dst = e_pad[:].rearrange("p t (s h) v -> p h (t s) v", s=NS)[:, hl, :, HD * hl:HD * hl + HD]
                    src = err[:].rearrange("p t (s h d) -> p h (t s) d", s=NS, h=HL)[:, hl]
                    pool.tensor_copy(dst, src).then_inc(s["err_pad"], 1)
                if ahead:
                    values(b + 1)
                f = ffn_of_tail(b)
                rsqrt(2 * f)
                add_bias(2 * f, xa, 0, s["ffn_base"])
                if ahead:
                    features(b + 1)
                rsqrt(2 * f + 1)
                scatter(b)

            front(0)
            pool.wait_ge(s["zeroed"], 9)
            values(0)
            features(0)
            with pool.Fori(0, B - 1) as b:
                front(b + 1)
                tail(b, True)
            tail(B - 1, False)
            pool.wait_ge(s["rank_b"], 2 * B)
            pool.memset(carry[:], 0.0).then_inc(s["zeroed"], 1)
            pool.tensor_copy(spare[:], const("spare_slot")).then_inc(s["zeroed"], 1)
            with pool.Fori(0, B) as b:
                gather(b, 8 * E)
                rsqrt(4 * B + 2 * b)
                add_bias(4 * B + 2 * b, xb, 3, s["l1_base"])
                pool.wait_ge(s["l1_exp"], 2 * b + 1)
                pool.tensor_tensor(qaf[:], qf[:], tmp[:], ALU.add).then_inc(s["l1_feat"], 1)
                pool.wait_ge(s["l1_exp"], 2 * b + 2)
                pool.tensor_tensor(kaf[:], kf[:], y_tmp[0][:], ALU.add).then_inc(s["l1_feat"], 1)
                low(s["l1_lo"], qaf, qs, s["l1_hi"], 2 * b + 1)
                low(s["l1_lo"], kaf, ks, s["l1_hi"], 2 * b + 2)
                rsqrt(4 * B + 2 * b + 1)
                scatter(B + b)
            with pool.Fori(0, B) as b:
                gather(B + b, 16 * E)

        @block.scalar
        def _(act):
            def xt(r):
                act.wait_ge(s["xt_mm"], r + 1)
                act.copy(xnT[:], turn[1][:]).then_inc(s["xt_ready"], 1)

            def gelu(f, fb, banks):
                act.wait_ge(s["ffn_h"], NF * f + fb + 1)
                act.activation(h_act[:, fb, :], banks[fb % len(banks)][:], ACT.Gelu,
                               bias=cols[:, fb:fb + 1]).then_inc(s["ffn_act"], 1)

            def router_exp(r):
                act.wait_ge(s["lg_sub"], r + 1)
                act.activation(r8[1][:], r8[0][:], ACT.Exp).then_inc(s["lg_exp"], 1)

            act.wait_ge(s["bias_prep"], 4)
            def front(step, b):
                f = ffn_of_front(b)
                if step == 0:
                    xt(2 * f)
                elif step <= NF:
                    gelu(f, step - 1, FRONT_BANKS)
                elif step == 6:
                    xt(2 * f + 1)
                elif step == 7:
                    act.wait_ge(s["qkv_mm"], 3 * b + 1)
                    act.activation(qf[:], accum[1][:], ACT.Identity, bias=cols[:, NF:NF + 1]).then_inc(s["proj_evac"], 1)
                elif step == 8:
                    act.wait_ge(s["qkv_mm"], 3 * b + 2)
                    act.activation(kf[:], turn[1][:], ACT.Identity, bias=cols[:, NF + 1:NF + 2]).then_inc(s["proj_evac"], 1)
                elif step == 9:
                    act.wait_ge(s["qkv_mm"], 3 * b + 3)
                    act.activation(tmp[:], accum[1][:], ACT.Exp, bias=cols[:, NF + 5:NF + 6],
                                   scale=-MA_SCALE).then_inc(s["proj_evac"], 1)

            def features(b):
                act.wait_ge(s["ma_q"], b + 1)
                act.wait_ge(s["q_kept"], 48 * b + 48)
                act.copy(qs[:, 0, :], qaf[:]).then_inc(s["ma_hi"], 1)
                act.wait_ge(s["ma_k"], b + 1)
                act.wait_ge(s["k_kept"], 48 * b + 48)
                act.copy(ks[:, 0, :], kaf[:]).then_inc(s["ma_hi"], 1)
                act.wait_ge(s["ka_t_mm"], b + 1)
                act.copy(ka_tok[:].rearrange("p t d -> p (t d)"), turn[0][:]).then_inc(s["ka_tok"], 1)

            def max_t(b):
                act.wait_ge(s["max_t"], b + 1)
                act.copy(mT[:], turn[0][0:H, :]).then_inc(s["max_t_evac"], 1)

            def batch(b, ahead):
                for n in range(NS * NT):
                    w = T - P * (n % NT)
                    for pr in range(2):
                        u = 2 * n + pr
                        act.wait_ge(s["st_mm"], 2 * NS * NT * b + u + 1)
                        if n >= 2:
                            act.wait_ge(s["pv_mm"], NS * NT * b + n - 1)
                        act.activation(work[:, 2 * (n % 2) + pr, :, 0:w], pair[u % 2][:, :, 0:w], ACT.Exp,
                                       scale=SCALE).then_inc(s["exp_done"], 1)
                    if ahead and n - 1 in FRONT_AT:
                        front(FRONT_AT[n - 1], b + 1)
                act.wait_ge(s["yar_mm"], b + 1)
                act.copy(y_tmp[0][:], turn[1][:]).then_inc(s["yar_evac"], 1)
                if ahead:
                    features(b + 1)
                f = ffn_of_tail(b)
                xt(2 * f)
                for fb in range(NF):
                    gelu(f, fb, TAIL_BANKS)
                xt(2 * f + 1)
                if ahead:
                    max_t(b + 1)
                router_exp(b)

            for step in range(FRONT_STEPS):
                front(step, 0)
            features(0)
            max_t(0)
            with act.Fori(0, B - 1) as b:
                batch(b, True)
            batch(B - 1, False)
            act.wait_ge(s["scattered"], 16 * NT * B)

            def relu_experts(m):
                for e in range(E):
                    n = E * m + e
                    act.wait_ge(s["xg_t"], n + 1)
                    act.copy(y_tmp[n % 2][:, 0:CAP], turn[n % 2][:, 0:CAP]).then_inc(s["xg_evac"], 1)
                    act.wait_ge(s["h_mm"], n + 1)
                    act.activation(work[:, n % 2, 0, :], pair[n % 2][:, 0, :], ACT.Relu).then_inc(s["h_relu_a"], 1)

            relu_experts(0)
            with act.Fori(0, B) as b:
                xt(4 * B + 2 * b)
                bq, bk = cols[:, NF + 3:NF + 4], cols[:, NF + 4:NF + 5]
                act.wait_ge(s["l1_mm"], 3 * b + 1)
                act.activation(qf[:], pair[0][:, 0, :], ACT.Relu, bias=bq).then_inc(s["l1_relu"], 1)
                act.wait_ge(s["l1_mm"], 3 * b + 2)
                act.activation(kf[:], pair[0][:, 1, :], ACT.Relu, bias=bk).then_inc(s["l1_relu"], 1)
                act.wait_ge(s["l1_min"], 2 * b + 1)
                act.activation(tmp[:], tmp[:], ACT.Exp).then_inc(s["l1_exp"], 1)
                act.wait_ge(s["l1_min"], 2 * b + 2)
                act.activation(y_tmp[0][:], y_tmp[0][:], ACT.Exp).then_inc(s["l1_exp"], 1)
                act.wait_ge(s["l1_feat"], 2 * b + 1)
                act.copy(qs[:, 0, :], qaf[:]).then_inc(s["l1_hi"], 1)
                act.wait_ge(s["l1_feat"], 2 * b + 2)
                act.copy(ks[:, 0, :], kaf[:]).then_inc(s["l1_hi"], 1)
                act.wait_ge(s["l1_kt"], b + 1)
                act.copy(ka_tok[:].rearrange("p t d -> p (t d)"), turn[1][:]).then_inc(s["l1_ktok"], 1)
                act.wait_ge(s["l1_y1t"], b + 1)
                act.copy(yT[:], turn[1][:]).then_inc(s["l1_y1ev"], 1)
                xt(4 * B + 2 * b + 1)
                router_exp(B + b)
                act.wait_ge(s["scattered"], 16 * NT * (B + b) + 16 * NT)
            relu_experts(1)

        @block.vector
        def _(dve):
            dve.sem_inc(s["x_kept"], 16)
            dve.sem_inc(s["out_done"], 16)
            dve.wait_ge(s["loaded"], 16 * LOADS)
            w2_flat = w2[:].rearrange("p f d -> p (f d)")
            for i, w in enumerate((w1[:], w2_flat)):
                dve.tensor_reduce(wst[:, i:i + 1], w, AX.X, ALU.add, apply_absolute_value=True).then_inc(s["w_abs"], 1)
            dve.wait_ge(s["w_sum"], 1)
            dve.tensor_scalar(wst[:, 2:4], turn[0][:, 0:2], 1.0 / (FF * D), 1e-8, ALU.mult, ALU.max).then_inc(s["w_scale"], 1)
            dve.wait_ge(s["w_scale"], 1)
            dve.tensor_scalar(wst[:, 4:6], wst[:, 2:4], 0.5, None, ALU.mult).then_inc(s["w_half"], 1)
            dve.tensor_scalar(wst[:, 6:8], wst[:, 2:4], -0.5, None, ALU.mult).then_inc(s["w_half"], 1)
            dve.wait_ge(s["w_half"], 2)
            for i, w in enumerate((w1[:], w2_flat)):
                dve.tensor_scalar(tmp[:], w, wst[:, 6 + i:7 + i], None, ALU.is_lt).then_inc(s["w_low"], 1)
                dve.wait_ge(s["w_low"], i + 1)
                dve.scalar_tensor_tensor(out=w, in0=w, scalar=wst[:, 4 + i:5 + i], in1=tmp[:],
                                         op0=ALU.is_gt, op1=ALU.subtract).then_inc(s["w_tern"], 1)
                dve.wait_ge(s["w_tern"], i + 1)
            for dst, name in ((ident_bf, "ident"), (add_q_bf, "add_q"), (add_k_bf, "add_k"),
                              (before_bf, "key_before"), (ones_bf, "ones")):
                dve.tensor_copy(dst[:], const(name)).then_inc(s["consts_bf"], 1)

            def moments(r, x):
                for t in range(NT):
                    dve.bn_stats(stats[:, t, :], x[:, t, :]).then_inc(s["stats"], 1)
                hold(dve, s["stats"], NT * r + NT)
                for t in range(NT):
                    dve.bn_aggr(mv[:, t, :], stats[:, t, :]).then_inc(s["moments"], 1)

            def normalise(r, x, dst):
                dve.wait_ge(s["rstd"], r + 1)
                for t in range(NT):
                    dve.tensor_scalar(dst[:, t, :], x[:, t, :], mv[:, t, 0:1], rstd[:, t:t + 1],
                                      ALU.subtract, ALU.mult).then_inc(s["normed"], 1)

            def norm(r, x, dst):
                moments(r, x)
                normalise(r, x, dst)

            def flat(a):
                return a[:].rearrange("p t d -> p (t d)")

            def ffn_x(f, x, dst):
                dve.wait_ge(s["ffn_out"], f + 1)
                dve.wait_ge(s["ffn_base"], f + 1)
                dve.scalar_tensor_tensor(out=flat(dst), in0=accum[1][:], scalar=0.5, in1=flat(x),
                                         op0=ALU.mult, op1=ALU.add).then_inc(s["ffn_x"], 1)
                dve.wait_ge(s["ffn_x"], f + 1)

            def route(r, b):
                lg = accum[0][:, LG:LG + NT * E].rearrange("p (t e) -> p t e", e=E)
                dve.wait_ge(s["lg_mm"], r + 1)
                dve.tensor_reduce(r1[0][:], lg, AX.X, ALU.max).then_inc(s["lg_max"], 1)
                dve.wait_ge(s["lg_max"], r + 1)
                dve.tensor_tensor(r8[0][:], lg, r1[0][:].unsqueeze(2).broadcast_to([P, NT, E]), ALU.subtract).then_inc(s["lg_sub"], 1)
                dve.wait_ge(s["lg_sub"], r + 1)
                dve.scalar_tensor_tensor(out=r8[2][:].rearrange("p t e -> p (t e)"), in0=r8[0][:].rearrange("p t e -> p (t e)"),
                                         scalar=0.0, in1=const("down"), op0=ALU.is_ge, op1=ALU.mult).then_inc(s["top_cand"], 1)
                dve.wait_ge(s["top_cand"], r + 1)
                dve.tensor_reduce(r1[1][:], r8[2][:], AX.X, ALU.max).then_inc(s["top_max"], 1)
                dve.wait_ge(s["top_max"], r + 1)
                top = r1[1][:].unsqueeze(2).broadcast_to([P, NT, E])
                dve.tensor_tensor(onehot_bf[:], r8[2][:], top, ALU.is_equal).then_inc(s["top_onehot"], 1)
                dve.tensor_tensor(r8[3][:], r8[2][:], top, ALU.is_equal).then_inc(s["top_eq"], 1)
                dve.wait_ge(s["lg_exp"], r + 1)
                dve.tensor_reduce(r1[2][:], r8[1][:], AX.X, ALU.add).then_inc(s["top_sum"], 1)
                dve.wait_ge(s["top_sum"], r + 1)
                dve.reciprocal(r1[3][:], r1[2][:]).then_inc(s["top_p"], 1)
                rk = accum[0][:, 0:NT * E].rearrange("p (t e) -> p t e", e=E)
                total = accum[0][:, NT * E:NT * E + E]
                dve.wait_ge(s["rank_mm"], r + 1)
                dve.tensor_tensor(r8[4][:], rk, bc(carry[:], NT), ALU.add).then_inc(s["rank_a"], 1)
                dve.wait_ge(s["rank_a"], r + 1)
                dve.tensor_tensor(carry[:], carry[:], total, ALU.add).then_inc(s["rank_b"], 1)
                dve.tensor_tensor(r8[4][:], r8[4][:], r8[3][:], ALU.mult).then_inc(s["rank_c"], 1)
                dve.tensor_tensor(r8[5][:].rearrange("p t e -> p (t e)"), r8[3][:].rearrange("p t e -> p (t e)"),
                                  const("slot_base"), ALU.mult).then_inc(s["rank_c"], 1)
                dve.wait_ge(s["rank_c"], 2 * r + 2)
                dve.tensor_reduce(r1[4][:], r8[4][:], AX.X, ALU.add).then_inc(s["rank_d"], 1)
                dve.tensor_reduce(r1[5][:], r8[5][:], AX.X, ALU.add).then_inc(s["rank_d"], 1)
                dve.wait_ge(s["rank_d"], 2 * r + 2)
                dve.tensor_scalar(r1[6][:], r1[4][:], float(CAP), None, ALU.is_lt).then_inc(s["rank_e"], 1)
                dve.tensor_tensor(r1[7][:], r1[4][:], r1[5][:], ALU.add).then_inc(s["rank_e"], 1)
                dve.wait_ge(s["rank_e"], 2 * r + 2)
                dve.tensor_tensor(r1[7][:], r1[7][:], spare[:], ALU.subtract).then_inc(s["rank_f"], 1)
                dve.scalar_tensor_tensor(out=gate_all[:, bass.ds(b * NT, NT)],
                                         in0=r1[6][:], scalar=0.5, in1=r1[3][:],
                                         op0=ALU.mult, op1=ALU.mult).then_inc(s["rank_h"], 1)
                dve.wait_ge(s["rank_f"], r + 1)
                dve.tensor_tensor(r1[7][:], r1[7][:], r1[6][:], ALU.mult).then_inc(s["rank_g"], 1)
                dve.wait_ge(s["rank_g"], r + 1)
                dve.tensor_tensor(slot[:], r1[7][:], spare[:], ALU.add).then_inc(s["rank_j"], 1)
                hold(dve, s["rank_j"], r + 1)
                dve.tensor_copy(slot_all[:, bass.ds(b * NT, NT)], slot[:]).then_inc(s["rank_i"], 1)
                dve.tensor_scalar(spare[:], spare[:], float(T), None, ALU.add).then_inc(s["rank_b"], 1)
                dve.wait_ge(s["rank_b"], 2 * r + 2)

            def front_in(b):
                f = ffn_of_front(b)
                dve.wait_ge(s["x_in"], 16 * b + 16)
                norm(2 * f, x0, xn[0])

            def front_mid(b):
                f = ffn_of_front(b)
                ffn_x(f, x0, x1)
                moments(2 * f + 1, x1)

            def split_hi(b, i):
                dve.wait_ge(s["proj_evac"], 3 * b + i + 1)
                dve.tensor_copy((qs, ks)[i][:, 0, :], (qf, kf)[i][:]).then_inc(s["split_hi"], 1)

            def features(b):
                dve.scalar_tensor_tensor(out=qaf[:], in0=qf[:], scalar=0.02, in1=qf[:],
                                         op0=ALU.mult, op1=ALU.min).then_inc(s["ma_q"], 1)
                dve.wait_ge(s["proj_evac"], 3 * b + 3)
                dve.tensor_scalar(tmp[:], tmp[:], 1.0, None, ALU.add).then_inc(s["ma_k1"], 1)
                dve.wait_ge(s["ma_k1"], b + 1)
                dve.reciprocal(kaf[:], tmp[:]).then_inc(s["ma_k"], 1)

            def maxima(b, first, last):
                for n in range(first, last):
                    hs, i = n // (NPAIR // 2), 2 * (n % (NPAIR // 2))
                    dve.wait_ge(s["smax_mm"], NS * NPAIR // 2 * b + n + 1)
                    dve.tensor_reduce(mpart[:, hs, i:i + 2, :].rearrange("p i h -> p (i h)"),
                                      pair[n % 2][:].rearrange("p a (h k) -> p (a h) k", h=HL),
                                      AX.X, ALU.max).then_inc(s["smax_red"], 1)

            def max_of_tiles(b):
                dve.wait_ge(s["smax_red"], NS * NPAIR // 2 * (b + 1))
                for t in range(NT):
                    i = t * (t + 1) // 2
                    dve.tensor_reduce(mneg[:, t, :].rearrange("p (h s) -> p s h", s=NS),
                                      mpart[:, :, i:i + t + 1, :].rearrange("p s i h -> p s h i"),
                                      AX.X, ALU.max, negate=True).then_inc(s["max_red"], 1)

            def answers_out(b, hs):
                dve.wait_ge(s["pv_mm"], NS * NT * b + NT * hs + NT)
                dve.tensor_copy(y_tmp[hs % 2][:], accum[0][:]).then_inc(s["y_evac"], 1)

            def answers_divide(b, hs):
                dve.wait_ge(s["y_t"], NS * b + hs + 1)
                y = turn[0][:].rearrange("p (t h v) -> p t h v", t=NT, h=HL)
                rc = rcp[:, 0:NT * HL].rearrange("p (t h) -> p t h", t=NT)
                dve.reciprocal(rc, y[:, :, :, HD]).then_inc(s["rcp"], 1)
                dve.wait_ge(s["rcp"], NS * b + hs + 1)
                dve.tensor_tensor(y_ar[:].rearrange("p t (s h d) -> p s t h d", s=NS, h=HL)[:, hs],
                                  y[:, :, :, 0:HD], rc.unsqueeze(3).broadcast_to([P, NT, HL, HD]),
                                  ALU.mult).then_inc(s["y_norm"], 1)
                dve.wait_ge(s["y_norm"], NS * b + hs + 1)

            def batch(b, ahead):
                if ahead:
                    front_in(b + 1)
                answers_out(b, 0)
                answers_divide(b, 0)
                answers_out(b, 1)
                if ahead:
                    front_mid(b + 1)
                answers_divide(b, 1)
                if ahead:
                    dve.wait_ge(s["v_next"], 32 * b + 32)
                    normalise(2 * ffn_of_front(b + 1) + 1, x1, xn[1])
                answers_out(b, 2)
                if ahead:
                    split_hi(b + 1, 0)
                answers_divide(b, 2)
                if ahead:
                    split_hi(b + 1, 1)
                answers_out(b, 3)
                answers_divide(b, 3)
                for n in range(2 * NT):
                    dve.wait_ge(s["ma_mm"], 2 * NT * b + n + 1)
                    if n >= 4:
                        dve.wait_ge(s["ym_mm"], NT * b + (n - 4) // 2 + 1)
                    dve.tensor_tensor(work[:, n % 4].rearrange("p a (h q) -> p (a h) q", h=HL),
                                      pair[n % 2][:].rearrange("p a (h q) -> p (a h) q", h=HL),
                                      bc(const("key_before"), 2 * HL), ALU.mult).then_inc(s["ma_masked"], 1)
                    if n % 2 == 1 and n // 2 < NT - 1:
                        dve.wait_ge(s["kv_mm"], (NT - 1) * b + n // 2 + 1)
                        dve.tensor_tensor(kv[:, n // 2, :], turn[0][:, 0:D], const("same_head"), ALU.mult).then_inc(s["kv_evac"], 1)
                dve.wait_ge(s["ym_mm"], NT * b + NT)
                dve.wait_ge(s["yar_evac"], b + 1)
                dve.scalar_tensor_tensor(out=yT[:], in0=accum[0][:], scalar=SCALE, in1=y_tmp[0][:],
                                         op0=ALU.mult, op1=ALU.add).then_inc(s["y_sum"], 1)
                if ahead:
                    maxima(b + 1, 0, 1)
                f = ffn_of_tail(b)
                dve.wait_ge(s["proj_mm"], b + 1)
                dve.wait_ge(s["attn_base"], b + 1)
                dve.tensor_tensor(flat(xa), accum[1][:], flat(x_base), ALU.add).then_inc(s["attn_x"], 1)
                dve.wait_ge(s["attn_x"], b + 1)
                moments(2 * f, xa)
                if ahead:
                    features(b + 1)
                normalise(2 * f, xa, xn[0])
                if ahead:
                    maxima(b + 1, 1, 12)
                dve.wait_ge(s["x_kept"], 16 * b + 16)
                ffn_x(f, xa, xb)
                moments(2 * f + 1, xb)
                if ahead:
                    maxima(b + 1, 12, 13)
                else:
                    dve.wait_ge(s["scattered"], 16 * NT * b)
                normalise(2 * f + 1, xb, xn[2])
                if ahead:
                    maxima(b + 1, 13, NS * NPAIR // 2)
                    max_of_tiles(b + 1)
                route(b, b)

            front_in(0)
            front_mid(0)
            normalise(1, x1, xn[1])
            split_hi(0, 0)
            split_hi(0, 1)
            features(0)
            maxima(0, 0, NS * NPAIR // 2)
            max_of_tiles(0)
            with dve.Fori(0, B - 1) as b:
                batch(b, True)
            batch(B - 1, False)

            def relu_experts(m):
                for e in range(E):
                    n = E * m + e
                    dve.wait_ge(s["h_mm"], n + 1)
                    dve.tensor_scalar(work[:, n % 2, 1, :], pair[n % 2][:, 1, :], 0.0, None, ALU.max).then_inc(s["h_relu_v"], 1)
                    dve.wait_ge(s["ye_mm"], n + 1)
                    if n >= 2:
                        dve.wait_ge(ye_kept[n % 2], 16 * (n // 2))
                    dve.tensor_copy(ye[:, n % 2].rearrange("p g d -> p (g d)"), accum[n % 2][:, 0:NG * D]).then_inc(s["ye_evac"], 1)

            def combine(r, b, scattered):
                dve.wait_ge(s["scattered"], 16 * NT * scattered)
                dve.tensor_copy(slot[:], slot_all[:, bass.ds(b * NT, NT)]).then_inc(s["idx_in"], 1)
                dve.tensor_copy(r1[8][:], gate_all[:, bass.ds(b * NT, NT)]).then_inc(s["gate_in"], 1)
                dve.wait_ge(s["gate_in"], r + 1)
                dve.wait_ge(s["x_back"], 16 * r + 16)
                dve.wait_ge(s["gathered"], 16 * NT * r + 16 * NT)
                for t in range(NT):
                    dve.scalar_tensor_tensor(out=xb[:, t, :], in0=yg[:, t // 2, t % 2, :], scalar=r1[8][:, t:t + 1],
                                             in1=xa[:, t, :], op0=ALU.mult, op1=ALU.add).then_inc(s["mixed"], 1)
                dve.wait_ge(s["mixed"], NT * r + NT)

            relu_experts(0)
            dve.wait_ge(s["zeroed"], 11)
            with dve.Fori(0, B) as b:
                combine(b, b, b + B)
                norm(4 * B + 2 * b, xb, xn[1])
                for i, z in enumerate((tmp, y_tmp[0])):
                    dve.wait_ge(s["l1_relu"], 2 * b + i + 1)
                    dve.tensor_scalar(z[:], pair[0][:, i, :], cols[:, NF + 3 + i:NF + 4 + i], 0.0,
                                      ALU.add, ALU.min).then_inc(s["l1_min"], 1)
                dve.wait_ge(s["l1_mm"], 3 * b + 3)
                dve.tensor_tensor(v_aug[:, :, :, 0:HD],
                                  pair[1][:, 0, :].rearrange("p (t h d) -> p t h d", t=NT, h=H),
                                  rows[:, 2, :].rearrange("p (h d) -> p h d", h=H).unsqueeze(1).broadcast_to([P, NT, H, HD]),
                                  ALU.add).then_inc(s["l1_v"], 1)
                for t in range(NT):
                    for pr in range(2):
                        n = 2 * t + pr
                        dve.wait_ge(s["l1_s"], 2 * NT * b + n + 1)
                        if n >= 4:
                            dve.wait_ge(s["l1_y"], NT * b + (n - 4) // 2 + 1)
                        dve.tensor_tensor(work[:, n % 4].rearrange("p a (h q) -> p (a h) q", h=HL),
                                          pair[n % 2][:].rearrange("p a (h q) -> p (a h) q", h=HL),
                                          bc(const("key_upto"), 2 * HL), ALU.mult).then_inc(s["l1_masked"], 1)
                    dve.wait_ge(s["l1_y"], NT * b + t + 1)
                    dve.tensor_copy(y_tmp[1][:], accum[0][:]).then_inc(s["l1_yev"], 1)
                    if t < NT - 1:
                        dve.wait_ge(s["l1_kv"], (NT - 1) * b + t + 1)
                        dve.tensor_tensor(kv1, accum[1][:], const("same_head_v"), ALU.mult).then_inc(s["l1_kvev"], 1)
                    dve.wait_ge(s["l1_yt"], NT * b + t + 1)
                    y = turn[0][:].rearrange("p (h v) -> p h v", v=VW)
                    dve.tensor_scalar(rcp[:, 0:H], y[:, :, HD], DEN_EPS, None, ALU.add).then_inc(s["l1_den"], 1)
                    dve.wait_ge(s["l1_den"], NT * b + t + 1)
                    dve.reciprocal(rcp[:, H:2 * H], rcp[:, 0:H]).then_inc(s["l1_rcp"], 1)
                    dve.wait_ge(s["l1_rcp"], NT * b + t + 1)
                    dve.tensor_tensor(y_ar[:, t, :].rearrange("p (h d) -> p h d", d=HD), y[:, :, 0:HD],
                                      rcp[:, H:2 * H].unsqueeze(2).broadcast_to([P, H, HD]), ALU.mult).then_inc(s["l1_yn"], 1)
                dve.wait_ge(s["l1_out"], b + 1)
                dve.wait_ge(s["l1_base"], b + 1)
                dve.wait_ge(s["x_kept"], 16 * (B + b) + 16)
                dve.tensor_tensor(flat(xb), accum[1][:], flat(xb), ALU.add).then_inc(s["l1_x"], 1)
                dve.wait_ge(s["l1_x"], b + 1)
                norm(4 * B + 2 * b + 1, xb, xn[2])
                route(B + b, b)
            relu_experts(1)
            with dve.Fori(0, B) as b:
                dve.wait_ge(s["out_done"], 16 * b + 16)
                combine(B + b, b, 2 * B)

        @block.tensor
        def _(pe):
            def mm(dst, lhsT, rhs, start=True, stop=True):
                return pe.matmul(dst, lhsT, rhs, start=start, stop=stop, skip_group_check=True)

            def tile(a, t):
                return a[:, t * P:(t + 1) * P]

            def turn_tiles(dst, src):
                for t in range(NT):
                    last = pe.transpose(tile(dst, t), src[:, t, :], ident)
                return last

            def xt(r, x):
                pe.wait_ge(s["normed"], NT * r + NT)
                turn_tiles(turn[1], x).then_inc(s["xt_mm"], 1)

            def ffn_step(f, i, banks):
                if i == 0:
                    pe.wait_ge(s["xt_ready"], 2 * f + 1)
                if i < NF:
                    if i >= len(banks):
                        pe.wait_ge(s["ffn_act"], NF * f + i - len(banks) + 1)
                    mm(banks[i % len(banks)][:], tile(w1, i), xnT[:]).then_inc(s["ffn_h"], 1)
                if i:
                    pe.wait_ge(s["ffn_act"], NF * f + i)
                    for t in range(NT):
                        last = mm(tile(accum[1], t), tile(h_act[:, i - 1, :], t), w2[:, i - 1, :],
                                  start=i == 1 and t == 0, stop=i == NF)
                    if i == NF:
                        last.then_inc(s["ffn_out"], 1)

            def route(r, ln):
                pe.wait_ge(s["xt_ready"], ln + 1)
                for t in range(NT):
                    last = mm(accum[0][:, LG + t * E:LG + (t + 1) * E], tile(xnT, t), wr_sb[:])
                last.then_inc(s["lg_mm"], 1)
                pe.wait_ge(s["top_onehot"], r + 1)
                for t in range(NT):
                    dst = accum[0][:, t * E:(t + 1) * E]
                    mm(dst, before_bf[:], onehot_bf[:, t, :], stop=t == 0)
                    for before in range(t):
                        mm(dst, ones_bf[:], onehot_bf[:, before, :], start=False, stop=before == t - 1)
                for t in range(NT):
                    last = mm(accum[0][:, NT * E:NT * E + E], ones_bf[:], onehot_bf[:, t, :], start=t == 0, stop=t == NT - 1)
                last.then_inc(s["rank_mm"], 1)
                pe.wait_ge(s["rank_c"], 2 * r + 2)

            pe.wait_ge(s["w_abs"], 2)
            mm(turn[0][:, 0:2], const("ones"), wst[:, 0:2]).then_inc(s["w_sum"], 1)
            pe.wait_ge(s["w_tern"], 2)
            pe.wait_ge(s["consts_bf"], 5)
            def front(step, b):
                f = ffn_of_front(b)
                if step == 0:
                    xt(2 * f, xn[0])
                elif step <= NF + 1:
                    ffn_step(f, step - 1, FRONT_BANKS)
                elif step == 6:
                    xt(2 * f + 1, xn[1])
                elif step == 7:
                    pe.wait_ge(s["xt_ready"], 2 * f + 2)
                    mm(accum[1][:], tile(wqk, 0), xnT[:]).then_inc(s["qkv_mm"], 1)
                elif step == 8:
                    mm(turn[1][:], tile(wqk, 1), xnT[:]).then_inc(s["qkv_mm"], 1)
                elif step == 9:
                    pe.wait_ge(s["proj_evac"], 3 * b + 1)
                    mm(accum[1][:], wk2[:], xnT[:]).then_inc(s["qkv_mm"], 1)

            def key_features(b):
                pe.wait_ge(s["ma_k"], b + 1)
                for t in range(NT):
                    last = pe.transpose(tile(turn[0], t), tile(kaf, t), ident)
                last.then_inc(s["ka_t_mm"], 1)

            pairs = [(qt, kt) for qt in range(NT) for kt in range(qt + 1)]

            def max_scores(b, first, last_n):
                if first == 0:
                    pe.wait_ge(s["q_stacked"], 64 * b + 64)
                    pe.wait_ge(s["k_stacked"], 64 * b + 64)
                for n in range(first, last_n):
                    hs, i = n // (NPAIR // 2), 2 * (n % (NPAIR // 2))
                    if n >= 2:
                        pe.wait_ge(s["smax_red"], NS * NPAIR // 2 * b + n - 1)
                    for a in range(2):
                        qt, kt = pairs[i + a]
                        dst = pair[n % 2][:, a, :]
                        last = mm(dst, tile(q_stk[:, hs, :], qt), k_pad[:, HL * hs:HL * hs + HL, kt * P:(kt + 1) * P],
                                  stop=qt != kt)
                        if qt == kt:
                            last = mm(dst, ident_bf[:], bc(add_q_bf[:], HL), start=False)
                    last.then_inc(s["smax_mm"], 1)

            def max_turn(b):
                pe.wait_ge(s["max_red"], NT * b + NT)
                for t in range(NT):
                    last = pe.transpose(turn[0][0:H, t * P:(t + 1) * P], mneg[:, t, :], ident)
                last.then_inc(s["max_t"], 1)

            def batch(b, ahead):
                def scores(n):
                    hs, kt = n // NT, n % NT
                    w = T - P * kt
                    for pr in range(2):
                        u = 2 * n + pr
                        if u >= 2:
                            pe.wait_ge(s["exp_done"], 2 * NS * NT * b + u - 1)
                        for a in range(2):
                            dst = pair[u % 2][:, a, :]
                            mm(dst[:, 0:w], tile(k_pad[:, HL * hs + 2 * pr + a, :], kt), q_stk[:, hs, kt * P:T], stop=False)
                            last = mm(dst[:, 0:P], ident_bf[:], add_k_bf[:], start=False)
                        last.then_inc(s["st_mm"], 1)

                def answers(n):
                    hs, kt = n // NT, n % NT
                    w = T - P * kt
                    pe.wait_ge(s["exp_done"], 2 * NS * NT * b + 2 * n + 2)
                    if kt == 0 and hs >= 1:
                        pe.wait_ge(s["y_evac"], NS * b + hs)
                    for hl in range(HL):
                        last = mm(accum[0][VW * hl:VW * hl + VW, kt * P:T], v_aug[:, kt, HL * hs + hl, :],
                                  work[:, 2 * (n % 2) + hl // 2, hl % 2, 0:w], start=kt == 0, stop=kt == NT - 1)
                    last.then_inc(s["pv_mm"], 1)

                def turn_answers(hs):
                    pe.wait_ge(s["y_evac"], NS * b + hs + 1)
                    if hs >= 1:
                        pe.wait_ge(s["y_norm"], NS * b + hs)
                    for t in range(NT):
                        last = pe.transpose(tile(turn[0], t), tile(y_tmp[hs % 2], t), ident)
                    last.then_inc(s["y_t"], 1)

                pe.wait_ge(s["max_rows"], 64 * b + 64)
                pe.wait_ge(s["v_aug"], b + 1)
                scores(0)
                for n in range(NS * NT):
                    if n + 1 < NS * NT:
                        scores(n + 1)
                    answers(n)
                    if n % NT == 0 and n:
                        turn_answers(n // NT - 1)
                    if ahead and n in FRONT_AT:
                        front(FRONT_AT[n], b + 1)
                turn_answers(NS - 1)

                def ma_scores(t):
                    for pr in range(2):
                        n = 2 * t + pr
                        if n >= 2:
                            pe.wait_ge(s["ma_masked"], 2 * NT * b + n - 1)
                        for a in range(2):
                            hs = 2 * pr + a
                            last = mm(pair[n % 2][:, a, :], tile(ka_stk[:, hs, :], t),
                                      qa_pad[:, HL * hs:HL * hs + HL, t * P:(t + 1) * P])
                        last.then_inc(s["ma_mm"], 1)

                def ma_answers(t):
                    dst = tile(accum[0], t)
                    if t:
                        pe.wait_ge(s["kv_evac"], (NT - 1) * b + t)
                        mm(dst, kv[:, t - 1, :], tile(qaf, t), stop=False)
                    pe.wait_ge(s["ma_masked"], 2 * NT * b + 2 * t + 2)
                    for hl in range(HL):
                        for hs in range(NS):
                            last = mm(accum[0][VW * hs:VW * hs + VW, t * P:(t + 1) * P], e_pad[:, t, HL * hs + hl, :],
                                      tile(work[:, (2 * t + hs // 2) % 4, hs % 2, :], hl),
                                      start=t == 0 and hl == 0, stop=hl == HL - 1)
                    last.then_inc(s["ym_mm"], 1)

                pe.wait_ge(s["mq_stacked"], 64 * b + 64)
                pe.wait_ge(s["mk_stacked"], 64 * b + 64)
                pe.wait_ge(s["ka_tok"], b + 1)
                ma_scores(0)
                pe.wait_ge(s["err"], b + 1)
                pe.wait_ge(s["err_pad"], HL * b + HL)
                pe.wait_ge(s["y_norm"], NS * b + NS)
                for t in range(NT):
                    if t < NT - 1:
                        if t:
                            pe.wait_ge(s["kv_evac"], (NT - 1) * b + t)
                        mm(turn[0][:, 0:D], ka_tok[:, t, :], err[:, t, :], start=t == 0, stop=True).then_inc(s["kv_mm"], 1)
                        ma_scores(t + 1)
                    ma_answers(t)
                if ahead:
                    pe.wait_ge(s["proj_evac"], 3 * b + 6)
                turn_tiles(turn[1], y_ar).then_inc(s["yar_mm"], 1)
                if ahead:
                    max_scores(b + 1, 0, 2)
                pe.wait_ge(s["y_sum"], b + 1)
                for t in range(NT):
                    last = mm(tile(accum[1], t), tile(yT, t), wp[:])
                last.then_inc(s["proj_mm"], 1)
                f = ffn_of_tail(b)
                if ahead:
                    key_features(b + 1)
                xt(2 * f, xn[0])
                if ahead:
                    max_scores(b + 1, 2, 4)
                    pe.wait_ge(s["ka_tok"], b + 2)
                for i in range(NF + 1):
                    ffn_step(f, i, TAIL_BANKS)
                    if ahead:
                        max_scores(b + 1, 4 + 2 * i, 6 + 2 * i)
                xt(2 * f + 1, xn[2])
                if ahead:
                    max_scores(b + 1, 14, NS * NPAIR // 2)
                    max_turn(b + 1)
                route(b, 2 * f + 1)

            for step in range(FRONT_STEPS):
                front(step, 0)
            key_features(0)
            pe.wait_ge(s["pad_one"], 64)
            max_scores(0, 0, NS * NPAIR // 2)
            pe.wait_ge(s["ka_tok"], 1)
            max_turn(0)
            with pe.Fori(0, B - 1) as b:
                batch(b, True)
            batch(B - 1, False)

            def experts(m):
                def up(e):
                    n = E * m + e
                    pe.wait_ge(xg_loaded[n % 4], 16 * (n // 4 + 1))
                    for g in range(NG):
                        last = pe.transpose(tile(turn[n % 2], g), xg[:, n % 4, g, :], ident)
                    last.then_inc(s["xg_t"], 1)
                    pe.wait_ge(s["xg_evac"], n + 1)
                    if n >= 2:
                        pe.wait_ge(s["h_relu_v"], n - 1)
                        pe.wait_ge(s["h_relu_a"], n - 1)
                    for fb in range(NF):
                        last = mm(pair[n % 2][:, fb // 2, (fb % 2) * CAP:(fb % 2 + 1) * CAP],
                                  tile(mw1_sb[:, e, :], fb), y_tmp[n % 2][:, 0:CAP])
                    last.then_inc(s["h_mm"], 1)

                def down(e):
                    n = E * m + e
                    pe.wait_ge(s["h_relu_a"], n + 1)
                    pe.wait_ge(s["h_relu_v"], n + 1)
                    if n >= 2:
                        pe.wait_ge(s["ye_evac"], n - 1)
                    for g in range(NG):
                        for fb in range(NF):
                            last = mm(tile(accum[n % 2], g),
                                      work[:, n % 2, fb // 2, (fb % 2) * CAP + g * P:(fb % 2) * CAP + (g + 1) * P],
                                      mw2_sb[:, e, fb, :], start=fb == 0, stop=fb == NF - 1)
                    last.then_inc(s["ye_mm"], 1)

                up(0)
                for e in range(E):
                    if e + 1 < E:
                        up(e + 1)
                    down(e)

            pe.wait_ge(s["experts_loaded"], 16 * 2 * E)
            experts(0)
            with pe.Fori(0, B) as b:
                xt(4 * B + 2 * b, xn[1])
                pe.wait_ge(s["xt_ready"], 4 * B + 2 * b + 1)
                mm(pair[0][:, 0, :], tile(l1w, 0), xnT[:]).then_inc(s["l1_mm"], 1)
                mm(pair[0][:, 1, :], tile(l1w, 1), xnT[:]).then_inc(s["l1_mm"], 1)
                for t in range(NT):
                    last = mm(tile(pair[1][:, 0, :], t), tile(xnT, t), tile(l1w, 2))
                last.then_inc(s["l1_mm"], 1)
                pe.wait_ge(s["l1_feat"], 2 * b + 2)
                for t in range(NT):
                    last = pe.transpose(tile(turn[1], t), tile(kaf, t), ident)
                last.then_inc(s["l1_kt"], 1)
                pe.wait_ge(s["l1_qstk"], 64 * b + 64)
                pe.wait_ge(s["l1_kstk"], 64 * b + 64)
                pe.wait_ge(s["l1_v"], b + 1)
                pe.wait_ge(s["l1_min"], 2 * b + 2)
                pe.wait_ge(s["l1_ktok"], b + 1)

                def l1_scores(t):
                    for pr in range(2):
                        n = 2 * t + pr
                        if n >= 2:
                            pe.wait_ge(s["l1_masked"], 2 * NT * b + n - 1)
                        for a in range(2):
                            hs = 2 * pr + a
                            last = mm(pair[n % 2][:, a, :], tile(ka_stk[:, hs, :], t),
                                      qa_pad[:, HL * hs:HL * hs + HL, t * P:(t + 1) * P])
                        last.then_inc(s["l1_s"], 1)

                def l1_answers(t):
                    pe.wait_ge(s["l1_masked"], 2 * NT * b + 2 * t + 2)
                    if t:
                        pe.wait_ge(s["l1_kvev"], (NT - 1) * b + t)
                        pe.wait_ge(s["l1_yev"], NT * b + t)
                    for hs in range(NS):
                        if t:
                            mm(tile(accum[0], hs), tile(kv1, hs), tile(qaf, t), stop=False)
                        for hl in range(HL):
                            last = mm(accum[0][VW * hl:VW * hl + VW, hs * P:(hs + 1) * P], v_aug[:, t, HL * hs + hl, :],
                                      tile(work[:, (2 * t + hs // 2) % 4, hs % 2, :], hl), start=t == 0)
                    last.then_inc(s["l1_y"], 1)

                l1_scores(0)
                for t in range(NT):
                    l1_answers(t)
                    if t < NT - 1:
                        mm(accum[1][:], ka_tok[:, t, :], v_aug[:, t].rearrange("p h v -> p (h v)"),
                           start=t == 0).then_inc(s["l1_kv"], 1)
                        l1_scores(t + 1)
                    pe.wait_ge(s["l1_yev"], NT * b + t + 1)
                    if t:
                        pe.wait_ge(s["l1_yn"], NT * b + t)
                    for hs in range(NS):
                        last = pe.transpose(tile(turn[0], hs), tile(y_tmp[1], hs), ident)
                    last.then_inc(s["l1_yt"], 1)
                pe.wait_ge(s["l1_yn"], NT * b + NT)
                turn_tiles(turn[1], y_ar).then_inc(s["l1_y1t"], 1)
                pe.wait_ge(s["l1_y1ev"], b + 1)
                for t in range(NT):
                    last = mm(tile(accum[1], t), tile(yT, t), l1wp[:])
                last.then_inc(s["l1_out"], 1)
                xt(4 * B + 2 * b + 1, xn[2])
                route(B + b, 4 * B + 2 * b + 1)
            experts(1)


def kernel(**inputs):
    import numpy as _np
    import concourse.bacc as _bacc
    from concourse import mybir as _mybir
    from concourse.bass_utils import run_bass_kernel_spmd as _run

    g = {k: _np.asarray(v) for k, v in inputs.items()}
    ins = [
        ("x", g["L0_attn_x"].reshape(NTOK, D)),
        ("bias_cols", _np.concatenate([g["L0_ffn_b1"], g["L0_attn_b_attn"], g["L0_attn_b_k2"],
                                       g["L1_attn_b_attn"][:2 * D]]).reshape(-1, P).T),
        ("w_attn_t", g["L0_attn_w_attn"].T), ("w_k2_t", g["L0_attn_w_k2"].T),
        ("w_proj_t", g["L0_attn_w_proj"].T), ("b_proj", g["L0_attn_b_proj"]),
        ("w1_t", g["L0_ffn_W1"].T),
        ("w2_t", g["L0_ffn_W2"].T), ("b2", g["L0_ffn_b2"]),
        ("l1_w", g["L1_attn_W_attn"]), ("l1_bv", g["L1_attn_b_attn"][2 * D:]),
        ("l1_wp", g["L1_attn_W_proj"]), ("l1_bp", g["L1_attn_b_proj"]),
        ("wr", g["L1_ffn_Wr"]), ("mw1", g["L1_ffn_W1"]), ("mw2", g["L1_ffn_W2"]),
        ("consts", CONSTS),
    ]
    nc = _bacc.Bacc("TRN2", target_bir_lowering=False, num_devices=1)
    arrays, args = {}, []
    for name, a in ins:
        a = _np.ascontiguousarray(a)
        arrays[f"in_{name}"] = a
        args.append(nc.dram_tensor(f"in_{name}", a.shape, _mybir.dt.from_np(a.dtype), kind="ExternalInput").ap())
    args.append(nc.dram_tensor("out_0", (NTOK, D), _mybir.dt.float32, kind="ExternalOutput").ap())
    build(nc, *args)
    r = _run(nc, [arrays], core_ids=[0])
    return r.results[0]["out_0"].reshape(B, T, D)
```

```python
from contextlib import ExitStack

import numpy as np

import concourse.bass as bass
from concourse import mybir

F32 = mybir.dt.float32
F32R = mybir.dt.float32r
BF16 = mybir.dt.bfloat16
I32 = mybir.dt.int32
ALU = mybir.AluOpType
ACT = mybir.ActivationFunctionType
AX = mybir.AxisListType

P = 128
D = 128
B, T = 4, 512
NT = T // P
H, HD = 16, 8
HL = 4
NS = H // HL
VW = 32
FF = 512
NF = FF // P
E, CAP = 8, B * T // 8
LG = 256
FE = 512
NG = CAP // P
NTOK = B * T
LN_EPS = 1e-5
DEN_EPS = 1e-6
SCALE = 1.0 / np.sqrt(HD)
MA_SCALE = SCALE * 0.02
NPAIR = NT * (NT + 1) // 2
MASKED = -1e30
LOADS, FIRST_LOADS = 14, 4

CONST_COLS = {}


def constants():
    p = np.arange(P)[:, None]
    f = np.arange(P)[None, :]
    parts = {
        "ident": (p == f),
        "key_before": (p < f),
        "key_upto": (p <= f),
        "add_q": np.where(f > p, MASKED, 0.0),
        "add_k": np.where(p > f, MASKED, 0.0),
        "same_head": (p // HD == f // HD),
        "same_head_v": (p // HD == np.arange(H * VW)[None, :] // VW),
        "ones": np.ones((P, P)),
        "minus_half": np.full((P, NT), -0.5),
        "down": np.broadcast_to(np.tile(np.arange(E, 0, -1.0), NT), (P, NT * E)),
        "slot_base": np.broadcast_to(np.tile(CAP * np.arange(E), NT), (P, NT * E)),
        "spare_slot": NTOK + P * np.arange(NT)[None, :] + p,
    }
    col = 0
    for name, a in parts.items():
        CONST_COLS[name] = (col, col + a.shape[1])
        col += a.shape[1]
    return np.concatenate([np.asarray(a, np.float32) for a in parts.values()], axis=1)


CONSTS = constants()

SEMS = """held loaded experts_loaded first_loaded pads_zeroed xt_low h_evac w_abs w_sum w_scale w_half w_low
w_tern zeroed pad_zero pad_one stats moments var_eps rstd normed xt_mm xt_ready ffn_h ffn_act ffn_out
ffn_base ffn_x x_in qkv_mm proj_evac split_hi split_lo q_kept k_kept q_stacked k_stacked ma_q ma_k ma_hi
ma_lo mq_kept mk_kept mq_stacked mk_stacked ka_t_mm ka_tok v_aug smax_mm smax_red max_red max_t
max_t_evac max_rows st_mm exp_done pv_mm y_evac y_t rcp y_norm v_next err err_pad ma_mm ma_masked kv_mm
kv_evac ym_mm yar_mm yar_evac y_sum proj_mm attn_base attn_x x_kept lg_mm lg_max lg_sub lg_exp top_eq
top_cand top_max top_onehot top_sum top_p rank_mm rank_a rank_b rank_c rank_d rank_e rank_f rank_g
rank_h rank_i rank_j scattered xg0 xg1 xg2 xg3 xg_t xg_evac h_mm h_relu_a h_relu_v ye_mm ye_evac
ye_kept0 ye_kept1 last_gathered0 last_gathered1 last_gathered2 last_gathered3 gate_in idx_in gathered
x_back mixed l1_mm l1_z l1_min l1_exp l1_feat l1_hi l1_lo l1_khi l1_klo l1_v l1_vaug l1_qaf l1_kt
l1_ktok l1_qkept l1_kkept l1_qstk l1_kstk l1_s l1_masked l1_kv l1_kvev l1_y l1_yev l1_yt l1_den l1_rcp
l1_yn l1_y1t l1_y1ev l1_out l1_base l1_x out_done consts_bf bias_prep""".split()


def build(nc, x_in, bias_cols, w_attn_t, w_k2_t, w_proj_t, b_proj, w1_t, w2_t, b2,
          l1_w, l1_bv, l1_wp, l1_bp, wr, mw1, mw2, consts, out):
    ctx = ExitStack()
    with ctx:
        def sb(name, shape, dt=F32):
            return ctx.enter_context(nc.sbuf_tensor("sb_" + name, shape, dt))

        def psum(name, shape):
            return ctx.enter_context(nc.psum_tensor("ps_" + name, shape, F32))

        s = {n: ctx.enter_context(nc.semaphore("s_" + n)) for n in SEMS}
        ye_kept = [s["ye_kept0"], s["ye_kept1"]]
        last_gathered = [s[f"last_gathered{b}"] for b in range(B)]
        xg_loaded = [s["xg0"], s["xg1"], s["xg2"], s["xg3"]]

        pair = [psum(f"pair{i}", [P, 2, 512]) for i in range(2)]
        accum = [psum(f"accum{i}", [P, 512]) for i in range(2)]
        turn = [psum(f"turn{i}", [P, 512]) for i in range(2)]

        FRONT_STEPS = 11
        FRONT_AT = {3: 0, 4: 1, 5: 2, 6: 3, 7: 4, 8: 5, 9: 6, 12: 7, 13: 8, 14: 9, 15: 10}
        HIDDEN_BANKS = [turn[0], turn[1]]
        WITH_FFN = [4, 6, 9, 12, 15, 17]

        cst = sb("cst", [P, CONSTS.shape[1]])

        def const(name):
            a, b = CONST_COLS[name]
            return cst[:, a:b]

        ident = const("ident")
        ident_bf = sb("ident_bf", [P, P], BF16)
        add_q_bf = sb("add_q_bf", [P, P], BF16)
        add_k_bf = sb("add_k_bf", [P, P], BF16)
        before_bf = sb("before_bf", [P, P], BF16)
        ones_bf = sb("ones_bf", [P, P], BF16)
        w1 = sb("w1", [P, FF])
        w1r = sb("w1r", [P, FF], F32R)
        w2 = sb("w2", [P, NF, D])
        wst = sb("wst", [P, 8])
        wqk = sb("wqk", [P, 2 * D])
        wk2 = sb("wk2", [P, D])
        wp = sb("wp", [P, D])
        l1w = sb("l1w", [P, 3 * D])
        l1wp = sb("l1wp", [P, D])
        wr_sb = sb("wr", [P, E])
        cols = sb("cols", [P, NF + 6])
        rows = sb("rows", [P, 4, D])

        x0 = sb("x0", [P, NT, D])
        x1 = sb("x1", [P, NT, D])
        x_base = sb("x_base", [P, NT, D])
        xa = sb("xa", [P, NT, D])
        xb = sb("xb", [P, NT, D])
        xn = [sb(f"xn{i}", [P, NT, D]) for i in range(3)]
        xnT = sb("xnT", [P, T])
        xs = sb("xs", [P, 2, T], F32R)
        h_act = sb("h_act", [P, NF, T])
        stats = sb("stats", [P, NT, 6])
        mv = sb("mv", [P, NT, 2])
        ve = sb("ve", [P, NT])
        rstd = sb("rstd", [P, NT])
        qf = sb("qf", [P, T])
        kf = sb("kf", [P, T])
        tmp = sb("tmp", [P, T])
        yT = sb("yT", [P, T])
        qs = sb("qs", [P, 2, T], F32R)
        ks = sb("ks", [P, 2, T], F32R)
        qaf = sb("qaf", [P, T])
        kaf = sb("kaf", [P, T])
        ka_tok = sb("ka_tok", [P, NT, D])
        with nc.sbuf_tensor("sb_k_pad", [P, H, T], F32R) as k_pad:
            pass
        mw1_sb = sb("mw1", [P, E, FE])
        mw2_sb = sb("mw2", [P, E, NF, D])
        q_stk = sb("q_stk", [P, NS, T], F32R)
        qa_pad = sb("qa_pad", [P, H, T], F32R)
        ka_stk = sb("ka_stk", [P, NS, T], F32R)
        v_aug = sb("v_aug", [P, NT, H, VW])
        e_pad = sb("e_pad", [P, NT, H, VW])
        v_next = sb("v_next", [P, NT, D])
        err = v_next
        work = sb("work", [P, 4, 2, 512])
        y_ar = sb("y_ar", [P, NT, D])
        y_tmp = [sb(f"y_tmp{i}", [P, T]) for i in range(2)]
        kv = sb("kv", [P, NT - 1, D])
        kv1 = [v_next[:].rearrange("p t d -> p (t d)"), h_act[:, 2, :]]
        mpart = sb("mpart", [P, NS, NPAIR, HL])
        mneg = sb("mneg", [P, NT, H])
        mT = sb("mT", [H, T], F32R)
        rcp = sb("rcp", [P, NT * H])
        r8 = [sb(f"r8_{i}", [P, NT, E]) for i in range(6)]
        r1 = [sb(f"r1_{i}", [P, NT]) for i in range(9)]
        onehot_bf = sb("onehot_bf", [P, NT, E], BF16)
        carry = sb("carry", [P, E])
        spare = sb("spare", [P, NT])
        slot = sb("slot", [P, NT], I32)
        slot_all = sb("slot_all", [P, NTOK // P], I32)
        gate_all = sb("gate_all", [P, NTOK // P])
        slot_in = sb("slot_in", [P, NT], I32)
        q_feat, v_new = h_act[:, 0, :], h_act[:, 1, :]
        spent = e_pad[:].rearrange("p t h v -> p t (h v)")
        xg = spent[:, :, 0:NG * D].rearrange("p n (g d) -> p n g d", d=D)
        ye = spent[:, 0:2, NG * D:2 * NG * D].rearrange("p n (g d) -> p n g d", d=D)
        yg = spent[:, 2:NT, NG * D:2 * NG * D].rearrange("p n (g d) -> p n g d", d=D)

        x_last = h_act[:].rearrange("p b (t d) -> p b t d", d=D)
        y_last = work[:].rearrange("p b a c -> p (b a c)")[:, 0:B * NT * D].rearrange("p (b t d) -> p b t d", b=B, d=D)

        def dram(name, shape):
            return nc.dram_tensor(name, shape, F32, kind="Internal").ap()

        q_scr = dram("q_scr", [H, 4, HD, T])
        k_scr = dram("k_scr", [H, 3, HD, T])
        mq_scr = dram("mq_scr", [H, 3, HD, T])
        mk_scr = dram("mk_scr", [H, 4, HD, T])
        x_scr = dram("x_scr", [NTOK, D])
        xe_scr = dram("xe_scr", [2 * NTOK, D])
        ye_scr = dram("ye_scr", [2 * NTOK, D])

        def tile_rows(ap, b):
            return ap[bass.ds(b * T, T), :].rearrange("(t p) d -> p t d", p=P)

        def sets(scr):
            return scr.rearrange("(s h) c d t -> (h c d) s t", s=NS)

        def heads(scr, hl):
            return scr.rearrange("(s h) c d t -> h (c d) s t", s=NS)[hl]

        def pad_rows(buf, hl, n):
            return buf[VW * hl:VW * hl + n].rearrange("r (s h) t -> r s h t", s=NS)[:, :, hl, :].bitcast(F32)

        def bc(ap, n):
            return ap.unsqueeze(1).broadcast_to([P, n, ap.shape[1]])

        def ffn_of_front(b):
            return 0 if isinstance(b, int) and b == 0 else 2 * b - 1

        def ffn_of_tail(b):
            return 2 * B - 1 if isinstance(b, int) and b == B - 1 else 2 * b + 2

        def norm_of_entry(b):
            return 4 * B + ffn_of_front(b)

        def norm_of_exit(b):
            return 4 * B + ffn_of_tail(b)

        def bank_of_entry(b, i):
            return (turn[1], accum[1], accum[0])[i] if isinstance(b, int) else turn[1]

        def hold(eng, sem, value):
            eng.wait_ge(sem, value)
            eng.sem_inc(s["held"], 1)

        block = ctx.enter_context(nc.Block())

        @block.sync
        def _(sp):
            sp.dma_start(x0[:], tile_rows(x_in, 0)).then_inc(s["x_in"], 16)
            loads = [(cst[:], consts), (w1[:], w1_t), (w2[:], w2_t.rearrange("(f p) d -> p f d", p=P)),
                     (cols[:, 0:NF + 5], bias_cols),
                     (wqk[:], w_attn_t), (wk2[:], w_k2_t), (wp[:], w_proj_t), (wr_sb[:], wr),
                     (rows[:, 0, :], b2.rearrange("(a d) -> a d", a=1).broadcast_to([P, D])),
                     (rows[:, 1, :], b_proj.rearrange("(a d) -> a d", a=1).broadcast_to([P, D])),
                     (rows[:, 2, :], l1_bv.rearrange("(a d) -> a d", a=1).broadcast_to([P, D])),
                     (rows[:, 3, :], l1_bp.rearrange("(a d) -> a d", a=1).broadcast_to([P, D])),
                     (l1w[:], l1_w), (l1wp[:], l1_wp)]
            for n, (dst, src) in enumerate(loads):
                sp.dma_start(dst, src).then_inc(s["loaded"] if n >= FIRST_LOADS else s["first_loaded"], 16)
            sp.wait_ge(s["zeroed"], 1)
            zero = work[:].rearrange("p a b c -> p (a b c)")
            for scr in (q_scr, mk_scr):
                sp.dma_start(scr[:, 3], zero[:, 0:T]).then_inc(s["pad_zero"], 16)
            for half in range(2):
                r0 = half * NTOK // 2
                for dst in (xe_scr[r0:r0 + NTOK // 2], ye_scr[NTOK + r0:NTOK + r0 + NTOK // 2]):
                    sp.dma_start(dst.rearrange("(p r) d -> p (r d)", p=P), zero[:, 0:1024]).then_inc(s["pad_zero"], 16)
            sp.wait_ge(s["zeroed"], 4)
            ones_row = v_next[0:NS, :, :].rearrange("p a b -> p (a b)")
            for hl in range(HL):
                r = VW * hl + 3 * HD
                dst = k_pad[r:r + 1].rearrange("r (s h) t -> r s h t", s=NS)[:, :, hl, :].bitcast(F32)
                sp.dma_start(dst, ones_row).then_inc(s["pad_one"], 16)

            def stack(hi_lo, scr, kept, order):
                for c, part in enumerate(order):
                    sp.dma_start(scr[:, c], hi_lo[:, part, :].bitcast(F32)).then_inc(kept, 16)

            def keep_qk(b):
                hold(sp, s["split_lo"], 2 * b + 1)
                stack(qs, q_scr, s["q_kept"], (0, 1, 0))
                hold(sp, s["split_lo"], 2 * b + 2)
                stack(ks, k_scr, s["k_kept"], (0, 0, 1))

            def load_qk(b):
                hold(sp, s["q_kept"], 48 * b + 48)
                sp.dma_start(q_stk[:].bitcast(F32), sets(q_scr)).then_inc(s["q_stacked"], 16)
                hold(sp, s["k_kept"], 48 * b + 48)
                for hl in range(HL):
                    sp.dma_start(pad_rows(k_pad, hl, 24), heads(k_scr, hl)).then_inc(s["k_stacked"], 16)

            def stack_features(b):
                hold(sp, s["ma_lo"], 2 * b + 1)
                stack(qs, mq_scr, s["mq_kept"], (0, 1, 0))
                hold(sp, s["ma_lo"], 2 * b + 2)
                stack(ks, mk_scr, s["mk_kept"], (0, 0, 1))
                sp.dma_start(v_next[0:P - 1], xn[1][1:P]).then_inc(s["v_next"], 16)
                sp.dma_start(v_next[P - 1:P, 0:NT - 1, :], xn[1][0:1, 1:NT, :]).then_inc(s["v_next"], 16)
                hold(sp, s["mq_kept"], 48 * b + 48)
                for hl in range(HL):
                    sp.dma_start(pad_rows(qa_pad, hl, 24), heads(mq_scr, hl)).then_inc(s["mq_stacked"], 16)
                hold(sp, s["mk_kept"], 48 * b + 48)
                sp.dma_start(ka_stk[:].bitcast(F32), sets(mk_scr)).then_inc(s["mk_stacked"], 16)

            def max_rows(b):
                hold(sp, s["max_t_evac"], b + 1)
                sp.dma_start(q_stk[3 * HD::VW].bitcast(F32), mT[:].bitcast(F32)).then_inc(s["max_rows"], 16)

            def batch(b, ahead):
                if ahead:
                    sp.dma_start(x0[:], tile_rows(x_in, b + 1)).then_inc(s["x_in"], 16)
                    keep_qk(b + 1)
                hold(sp, s["st_mm"], 2 * NS * NT * (b + 1))
                if ahead:
                    load_qk(b + 1)
                    stack_features(b + 1)
                else:
                    for e in range(E):
                        sp.dma_start(mw1_sb[:, e, :], mw1[e]).then_inc(s["experts_loaded"], 16)
                        sp.dma_start(mw2_sb[:, e], mw2[e].rearrange("(f p) d -> p f d", p=P)).then_inc(s["experts_loaded"], 16)
                f = ffn_of_tail(b)
                hold(sp, s["ffn_x"], f + 1)
                sp.dma_start(tile_rows(x_scr, b), xb[:]).then_inc(s["x_kept"], 16)
                if ahead:
                    max_rows(b + 1)

            sp.wait_ge(s["pad_zero"], 96)
            keep_qk(0)
            load_qk(0)
            stack_features(0)
            max_rows(0)
            with sp.Fori(0, B - 1) as b:
                batch(b, True)
            batch(B - 1, False)

            def experts(m):
                sp.wait_ge(s["scattered"], 16 * NT * B * (m + 1))
                for e in range(4):
                    rows_in(m, e)
                for e in range(E):
                    if e + 4 < E:
                        rows_in(m, e + 4)
                    answer(m, e)

            def rows_in(m, e):
                n = E * m + e
                if n >= 4:
                    sp.wait_ge(s["xg_t"], n - 3)
                src = xe_scr[e * CAP:(e + 1) * CAP].rearrange("(g p) d -> p g d", p=P)
                sp.dma_start(xg[:, n % 4], src).then_inc(xg_loaded[n % 4], 16)

            def answer(m, e):
                n = E * m + e
                sp.wait_ge(s["ye_evac"], n + 1)
                dst = ye_scr[e * CAP:(e + 1) * CAP].rearrange("(g p) d -> p g d", p=P)
                sp.dma_start(dst, ye[:, n % 2]).then_inc(ye_kept[n % 2], 16)

            experts(0)

            def x_in_again(b):
                sp.dma_start(xa[:], tile_rows(x_scr, b)).then_inc(s["x_back"], 16)

            def stack_l1(b):
                hold(sp, s["l1_lo"], b + 1)
                stack(qs, mq_scr, s["l1_qkept"], (0, 1, 0))
                hold(sp, s["l1_klo"], b + 1)
                stack(ks, mk_scr, s["l1_kkept"], (0, 0, 1))
                hold(sp, s["l1_qkept"], 48 * b + 48)
                if not (isinstance(b, int) and b == 0):
                    hold(sp, s["l1_s"], 2 * NT * b)
                for hl in range(HL):
                    sp.dma_start(pad_rows(qa_pad, hl, 24), heads(mq_scr, hl)).then_inc(s["l1_qstk"], 16)
                hold(sp, s["l1_kkept"], 48 * b + 48)
                sp.dma_start(ka_stk[:].bitcast(F32), sets(mk_scr)).then_inc(s["l1_kstk"], 16)

            def x_out_again(b):
                hold(sp, s["l1_x"], b + 1)
                sp.dma_start(tile_rows(x_scr, b), xb[:]).then_inc(s["x_kept"], 16)

            sp.wait_ge(s["x_kept"], 16 * B + 16)
            x_in_again(0)
            stack_l1(0)
            with sp.Fori(0, B - 1) as b:
                x_in_again(b + 1)
                stack_l1(b + 1)
                x_out_again(b)
            x_out_again(B - 1)
            sp.wait_ge(s["x_kept"], 32 * B + 16)
            sp.dma_start(x_last[:], x_scr.rearrange("(b t p) d -> p b t d", p=P, t=NT)).then_inc(s["x_back"], 16)
            experts(1)
            for b in range(B):
                sp.wait_ge(s["mixed"], NT * (B + b + 1))
                sp.dma_start(tile_rows(out, b), x_last[:, b]).then_inc(s["out_done"], 16)
            sp.wait_ge(s["out_done"], 16 * B)
            sp.wait_ge(s["pad_zero"], 96)
            for kept in ye_kept:
                sp.wait_ge(kept, 16 * E)
            sp.wait_ge(s["scattered"], 16 * NT * B * 2)

        @block.gpsimd
        def _(pool):
            pool.memset(work[:], 0.0).then_inc(s["zeroed"], 1)
            pool.memset(v_next[:], 1.0).then_inc(s["zeroed"], 1)
            pool.memset(carry[:], 0.0).then_inc(s["zeroed"], 1)

            def rsqrt(r):
                hold(pool, s["moments"], NT * r + NT)
                pool.tensor_scalar(ve[:], mv[:, :, 1], LN_EPS, None, ALU.add).then_inc(s["var_eps"], 1)
                pool.wait_ge(s["var_eps"], r + 1)
                pool.tensor_tensor(rstd[:], ve[:], const("minus_half"), ALU.pow).then_inc(s["rstd"], 1)

            def add_bias(r, x, row, done):
                pool.wait_ge(s["normed"], NT * r + NT)
                pool.tensor_tensor(x[:], x[:], bc(rows[:, row, :], NT), ALU.add).then_inc(done, 1)

            def low(n, full, parts, sem, value):
                pool.wait_ge(sem, value)
                pool.tensor_tensor(parts[:, 1, :], full[:], parts[:, 0, :].bitcast(F32), ALU.subtract).then_inc(n, 1)

            def scatter(r):
                hold(pool, s["rank_j"], r + 1)
                pool.wait_ge(s["pad_zero"], 96)
                for t in range(NT):
                    pool.indirect_dma_start(xe_scr, bass.IndirectOffsetOnAxis(ap=slot[:, t:t + 1], axis=0),
                                            xn[2][:, t, :], None).then_inc(s["scattered"], 16)

            def gather(r, ready):
                for kept in ye_kept:
                    pool.wait_ge(kept, ready)
                hold(pool, s["idx_in"], r + 1)
                for t in range(NT):
                    pool.indirect_dma_start(yg[:, t // 2, t % 2, :], None, ye_scr,
                                            bass.IndirectOffsetOnAxis(ap=slot_in[:, t:t + 1], axis=0)).then_inc(s["gathered"], 16)

            def front_first(b):
                f = ffn_of_front(b)
                rsqrt(2 * f)
                add_bias(2 * f, x0, 0, s["ffn_base"])

            def front_second(b):
                rsqrt(2 * ffn_of_front(b) + 1)

            def values(b):
                hold(pool, s["normed"], NT * (2 * ffn_of_front(b) + 2))
                pool.tensor_copy(v_aug[:].rearrange("p t h v -> p (t h) v")[:, :, 0:HD],
                                 xn[1][:].rearrange("p t (h d) -> p (t h) d", d=HD)).then_inc(s["v_aug"], 1)

            def features(b):
                low(s["ma_lo"], qaf, qs, s["ma_hi"], 2 * b + 1)
                low(s["ma_lo"], kaf, ks, s["ma_hi"], 2 * b + 2)
                pool.tensor_tensor(x_base[:], x1[:], bc(rows[:, 1, :], NT), ALU.add).then_inc(s["attn_base"], 1)

            def errors(b, hs):
                pool.wait_ge(s["y_norm"], NS * b + hs + 1)
                if hs == 0:
                    pool.wait_ge(s["v_next"], 32 * b + 32)
                value, answer = (a[:].rearrange("p t (s h d) -> p s t h d", s=NS, h=HL)[:, hs] for a in (v_next, y_ar))
                blocks = e_pad[:].rearrange("p t (s h) v -> p s t (h v)", s=NS)[:, hs]
                dst = bass.AP(e_pad, blocks.offset, [blocks.ap[0], blocks.ap[1], [VW + HD, HL], [1, HD]])
                pool.tensor_tensor(dst, value, answer, ALU.subtract).then_inc(s["err_pad"], 1)
                pool.tensor_tensor(value, value, answer, ALU.subtract).then_inc(s["err"], 1)

            def tail(b, ahead):
                if ahead:
                    values(b + 1)
                f = ffn_of_tail(b)
                rsqrt(2 * f)
                add_bias(2 * f, xa, 0, s["ffn_base"])
                if ahead:
                    features(b + 1)
                rsqrt(2 * f + 1)
                scatter(b)

            pool.wait_ge(s["first_loaded"], 16 * FIRST_LOADS)
            rsqrt(0)
            pool.wait_ge(s["loaded"], 16 * (LOADS - FIRST_LOADS))
            pool.tensor_scalar(rows[:, 0, :], rows[:, 0, :], 0.5, None, ALU.mult).then_inc(s["bias_prep"], 1)
            pool.tensor_scalar(rows[:, 1, :], rows[:, 1, :], 2.0, None, ALU.mult).then_inc(s["bias_prep"], 1)
            pool.tensor_scalar(cols[:, NF + 5:NF + 6], cols[:, NF + 2:NF + 3], MA_SCALE, None, ALU.mult).then_inc(s["bias_prep"], 1)
            pool.tensor_copy(spare[:], const("spare_slot")).then_inc(s["bias_prep"], 1)
            pool.wait_ge(s["bias_prep"], 4)
            add_bias(0, x0, 0, s["ffn_base"])
            pool.memset(k_pad[:].bitcast(F32), 0.0).then_inc(s["zeroed"], 1)
            front_second(0)
            pool.wait_ge(s["pads_zeroed"], 3)
            values(0)
            pool.memset(qa_pad[:].bitcast(F32), 0.0).then_inc(s["zeroed"], 1)
            features(0)
            with pool.Fori(0, B - 1) as b:
                front_first(b + 1)
                errors(b, 0)
                errors(b, 1)
                front_second(b + 1)
                errors(b, 2)
                errors(b, 3)
                tail(b, True)
                hold(pool, s["scattered"], 16 * NT * b + 16 * NT)
            for hs in range(NS):
                errors(B - 1, hs)
            tail(B - 1, False)
            pool.wait_ge(s["rank_b"], 2 * B)
            pool.memset(carry[:], 0.0).then_inc(s["zeroed"], 1)
            pool.tensor_copy(spare[:], const("spare_slot")).then_inc(s["zeroed"], 1)

            def enter(b):
                gather(b, 8 * E)
                rsqrt(norm_of_entry(b))
                low(s["l1_lo"], q_feat, qs, s["l1_hi"], b + 1)

            def switch_values(b):
                hold(pool, s["l1_v"], b + 1)
                pool.tensor_copy(v_aug[:].rearrange("p t h v -> p (t h) v")[:, :, 0:HD],
                                 v_new.rearrange("p (t h d) -> p (t h) d", t=NT, h=H)).then_inc(s["l1_vaug"], 1)

            def switch_base(b):
                pool.tensor_tensor(x_base[:], x1[:], bc(rows[:, 3, :], NT), ALU.add).then_inc(s["l1_base"], 1)

            enter(0)
            switch_values(0)
            switch_base(0)
            with pool.Fori(0, B - 1) as b:
                enter(b + 1)
                rsqrt(norm_of_exit(b))
                hold(pool, s["l1_y"], NT * b + NT)
                switch_values(b + 1)
                switch_base(b + 1)
                scatter(B + b)
            rsqrt(norm_of_exit(B - 1))
            scatter(2 * B - 1)
            for kept in ye_kept:
                pool.wait_ge(kept, 16 * E)
            pool.wait_ge(s["ye_mm"], 2 * E)
            for b in range(B):
                for t in range(NT):
                    i = NT * b + t
                    pool.indirect_dma_start(y_last[:, b, t, :], None, ye_scr,
                                            bass.IndirectOffsetOnAxis(ap=slot_all[:, i:i + 1], axis=0)).then_inc(last_gathered[b], 16)

        @block.scalar
        def _(act):
            def xt(r, dst):
                act.wait_ge(s["xt_mm"], r + 1)
                act.copy(dst, turn[1][:]).then_inc(s["xt_ready"], 1)

            def gelu(f, fb):
                act.wait_ge(s["ffn_h"], NF * f + fb + 1)
                act.activation(h_act[:, fb, :], HIDDEN_BANKS[fb % 2][:], ACT.Gelu,
                               bias=cols[:, fb:fb + 1]).then_inc(s["ffn_act"], 1)

            def router_exp(r):
                act.wait_ge(s["lg_sub"], r + 1)
                act.activation(r8[1][:], r8[0][:], ACT.Exp).then_inc(s["lg_exp"], 1)

            def front(step, b):
                f = ffn_of_front(b)
                if step == 0:
                    xt(2 * f, xs[:, 0, :])
                elif step == 5 and isinstance(b, int):
                    for fb in range(NF):
                        gelu(f, fb)
                elif step == 5:
                    act.wait_ge(s["h_evac"], NF * b)
                    act.activation(h_act[:], h_act[:], ACT.Gelu).then_inc(s["ffn_act"], NF)
                elif step == 7:
                    xt(2 * f + 1, xnT[:])
                elif step == 8:
                    act.wait_ge(s["qkv_mm"], 3 * b + 1)
                    act.activation(qf[:], accum[1][:], ACT.Identity, bias=cols[:, NF:NF + 1]).then_inc(s["proj_evac"], 1)
                elif step == 9:
                    act.wait_ge(s["qkv_mm"], 3 * b + 2)
                    act.activation(kf[:], turn[1][:], ACT.Identity, bias=cols[:, NF + 1:NF + 2]).then_inc(s["proj_evac"], 1)
                elif step == 10:
                    act.wait_ge(s["qkv_mm"], 3 * b + 3)
                    act.activation(kaf[:], accum[1][:], ACT.Sigmoid, bias=cols[:, NF + 5:NF + 6],
                                   scale=MA_SCALE).then_inc(s["ma_k"], 1)

            def features(b):
                act.wait_ge(s["ma_q"], b + 1)
                act.wait_ge(s["q_kept"], 48 * b + 48)
                act.copy(qs[:, 0, :], qaf[:]).then_inc(s["ma_hi"], 1)
                act.wait_ge(s["ma_k"], b + 1)
                act.wait_ge(s["k_kept"], 48 * b + 48)
                act.copy(ks[:, 0, :], kaf[:]).then_inc(s["ma_hi"], 1)
                act.wait_ge(s["ka_t_mm"], b + 1)
                act.copy(ka_tok[:].rearrange("p t d -> p (t d)"), turn[0][:]).then_inc(s["ka_tok"], 1)

            def max_t(b):
                act.wait_ge(s["max_t"], b + 1)
                act.copy(mT[:], turn[0][0:H, :]).then_inc(s["max_t_evac"], 1)

            def batch(b, ahead):
                for n in range(NS * NT):
                    w = T - P * (n % NT)
                    for pr in range(2):
                        u = 2 * n + pr
                        act.wait_ge(s["st_mm"], 2 * NS * NT * b + u + 1)
                        if n >= 2:
                            act.wait_ge(s["pv_mm"], NS * NT * b + n - 1)
                        act.activation(work[:, 2 * (n % 2) + pr, :, 0:w], pair[u % 2][:, :, 0:w], ACT.Exp,
                                       scale=SCALE).then_inc(s["exp_done"], 1)
                    if ahead and n - 1 in FRONT_AT:
                        front(FRONT_AT[n - 1], b + 1)
                if ahead:
                    front(FRONT_AT[NS * NT - 1], b + 1)
                act.wait_ge(s["yar_mm"], b + 1)
                act.copy(y_tmp[0][:], turn[1][:]).then_inc(s["yar_evac"], 1)
                if ahead:
                    features(b + 1)
                f = ffn_of_tail(b)
                xt(2 * f, xs[:, 0, :])
                for fb in range(NF):
                    gelu(f, fb)
                xt(2 * f + 1, xnT[:])
                if ahead:
                    max_t(b + 1)
                router_exp(b)

            front(0, 0)
            act.wait_ge(s["bias_prep"], 4)
            for step in range(1, FRONT_STEPS):
                front(step, 0)
            features(0)
            max_t(0)
            with act.Fori(0, B - 1) as b:
                batch(b, True)
            batch(B - 1, False)
            act.wait_ge(s["scattered"], 16 * NT * B)

            def relu_experts(m):
                def rows_in(n):
                    act.wait_ge(s["xg_t"], n + 1)
                    if n >= 2:
                        act.wait_ge(s["h_mm"], n - 1)
                    act.copy(y_tmp[n % 2][:, 0:CAP], turn[n % 2][:, 0:CAP]).then_inc(s["xg_evac"], 1)

                rows_in(E * m)
                for e in range(E):
                    n = E * m + e
                    if e + 1 < E:
                        rows_in(n + 1)
                    act.wait_ge(s["h_mm"], n + 1)
                    act.activation(work[:, n % 2, 0, :], pair[n % 2][:, 0, :], ACT.Relu).then_inc(s["h_relu_a"], 1)

            relu_experts(0)

            def enter(step, b):
                if step == 0:
                    xt(norm_of_entry(b), xnT[:])
                else:
                    z(b, step - 1)
                    exp_of_least(b, step - 1)

            def z(b, i):
                act.wait_ge(s["l1_mm"], 3 * b + i + 1)
                act.activation((qf, kf)[i][:], bank_of_entry(b, i)[:], ACT.Identity,
                               bias=cols[:, NF + 3 + i:NF + 4 + i]).then_inc(s["l1_z"], 1)

            def exp_of_least(b, i):
                act.wait_ge(s["l1_min"], 2 * b + i + 1)
                least = (tmp, y_tmp[0])[i]
                act.activation(least[:], least[:], ACT.Exp).then_inc(s["l1_exp"], 1)

            def round_features(b):
                act.wait_ge(s["l1_feat"], 2 * b + 1)
                act.copy(qs[:, 0, :], q_feat).then_inc(s["l1_hi"], 1)

            def switch(b):
                act.copy(qaf[:], q_feat).then_inc(s["l1_qaf"], 1)
                act.wait_ge(s["l1_kt"], b + 1)
                act.copy(ka_tok[:].rearrange("p t d -> p (t d)"), turn[0][:]).then_inc(s["l1_ktok"], 1)

            def attend(b, ahead):
                if ahead:
                    enter(0, b + 1)
                    enter(1, b + 1)
                act.wait_ge(s["l1_y1t"], b + 1)
                act.copy(yT[:], turn[0][:]).then_inc(s["l1_y1ev"], 1)
                if ahead:
                    round_features(b + 1)
                    enter(2, b + 1)
                    switch(b + 1)
                xt(norm_of_exit(b), xnT[:])
                router_exp(B + b)

            enter(0, 0)
            for i in range(2):
                z(0, i)
            for i in range(2):
                exp_of_least(0, i)
            round_features(0)
            switch(0)
            with act.Fori(0, B - 1) as b:
                attend(b, True)
            attend(B - 1, False)
            act.wait_ge(s["scattered"], 16 * NT * 2 * B)
            relu_experts(1)

        @block.vector
        def _(dve):
            dve.sem_inc(s["x_kept"], 16)

            def moments(r, x):
                for t in range(NT):
                    dve.bn_stats(stats[:, t, :], x[:, t, :]).then_inc(s["stats"], 1)
                hold(dve, s["stats"], NT * r + NT)
                for t in range(NT):
                    dve.bn_aggr(mv[:, t, :], stats[:, t, :]).then_inc(s["moments"], 1)

            def normalise(r, x, dst):
                dve.wait_ge(s["rstd"], r + 1)
                for t in range(NT):
                    dve.tensor_scalar(dst[:, t, :], x[:, t, :], mv[:, t, 0:1], rstd[:, t:t + 1],
                                      ALU.subtract, ALU.mult).then_inc(s["normed"], 1)

            def norm(r, x, dst):
                moments(r, x)
                normalise(r, x, dst)

            def low(f):
                dve.wait_ge(s["xt_ready"], 2 * f + 1)
                dve.tensor_tensor(xs[:, 1, :], turn[1][:], xs[:, 0, :].bitcast(F32), ALU.subtract).then_inc(s["xt_low"], 1)

            def flat(a):
                return a[:].rearrange("p t d -> p (t d)")

            def ffn_x(f, x, dst):
                dve.wait_ge(s["ffn_out"], f + 1)
                dve.wait_ge(s["ffn_base"], f + 1)
                dve.scalar_tensor_tensor(out=flat(dst), in0=accum[1][:], scalar=0.5, in1=flat(x),
                                         op0=ALU.mult, op1=ALU.add).then_inc(s["ffn_x"], 1)
                dve.wait_ge(s["ffn_x"], f + 1)

            def route(r, b):
                lg = accum[0][:, LG:LG + NT * E].rearrange("p (t e) -> p t e", e=E)
                dve.wait_ge(s["lg_mm"], r + 1)
                dve.tensor_reduce(r1[0][:], lg, AX.X, ALU.max).then_inc(s["lg_max"], 1)
                dve.wait_ge(s["lg_max"], r + 1)
                dve.tensor_tensor(r8[0][:], lg, r1[0][:].unsqueeze(2).broadcast_to([P, NT, E]), ALU.subtract).then_inc(s["lg_sub"], 1)
                dve.wait_ge(s["lg_sub"], r + 1)
                dve.scalar_tensor_tensor(out=r8[2][:].rearrange("p t e -> p (t e)"), in0=r8[0][:].rearrange("p t e -> p (t e)"),
                                         scalar=0.0, in1=const("down"), op0=ALU.is_ge, op1=ALU.mult).then_inc(s["top_cand"], 1)
                dve.wait_ge(s["top_cand"], r + 1)
                dve.tensor_reduce(r1[1][:], r8[2][:], AX.X, ALU.max).then_inc(s["top_max"], 1)
                dve.wait_ge(s["top_max"], r + 1)
                top = r1[1][:].unsqueeze(2).broadcast_to([P, NT, E])
                dve.tensor_tensor(onehot_bf[:], r8[2][:], top, ALU.is_equal).then_inc(s["top_onehot"], 1)
                dve.tensor_tensor(r8[3][:], r8[2][:], top, ALU.is_equal).then_inc(s["top_eq"], 1)
                dve.wait_ge(s["lg_exp"], r + 1)
                dve.tensor_reduce(r1[2][:], r8[1][:], AX.X, ALU.add).then_inc(s["top_sum"], 1)
                dve.wait_ge(s["top_sum"], r + 1)
                dve.reciprocal(r1[3][:], r1[2][:]).then_inc(s["top_p"], 1)
                rk = accum[0][:, 0:NT * E].rearrange("p (t e) -> p t e", e=E)
                total = accum[0][:, NT * E:NT * E + E]
                dve.wait_ge(s["rank_mm"], r + 1)
                dve.tensor_tensor(r8[4][:], rk, bc(carry[:], NT), ALU.add).then_inc(s["rank_a"], 1)
                dve.wait_ge(s["rank_a"], r + 1)
                dve.tensor_tensor(carry[:], carry[:], total, ALU.add).then_inc(s["rank_b"], 1)
                dve.tensor_tensor(r8[4][:], r8[4][:], r8[3][:], ALU.mult).then_inc(s["rank_c"], 1)
                dve.tensor_tensor(r8[5][:].rearrange("p t e -> p (t e)"), r8[3][:].rearrange("p t e -> p (t e)"),
                                  const("slot_base"), ALU.mult).then_inc(s["rank_c"], 1)
                dve.wait_ge(s["rank_c"], 2 * r + 2)
                dve.tensor_reduce(r1[4][:], r8[4][:], AX.X, ALU.add).then_inc(s["rank_d"], 1)
                dve.tensor_reduce(r1[5][:], r8[5][:], AX.X, ALU.add).then_inc(s["rank_d"], 1)
                dve.wait_ge(s["rank_d"], 2 * r + 2)
                dve.tensor_scalar(r1[6][:], r1[4][:], float(CAP), None, ALU.is_lt).then_inc(s["rank_e"], 1)
                dve.tensor_tensor(r1[7][:], r1[4][:], r1[5][:], ALU.add).then_inc(s["rank_e"], 1)
                dve.wait_ge(s["rank_e"], 2 * r + 2)
                dve.tensor_tensor(r1[7][:], r1[7][:], spare[:], ALU.subtract).then_inc(s["rank_f"], 1)
                dve.scalar_tensor_tensor(out=gate_all[:, bass.ds(b * NT, NT)],
                                         in0=r1[6][:], scalar=0.5, in1=r1[3][:],
                                         op0=ALU.mult, op1=ALU.mult).then_inc(s["rank_h"], 1)
                dve.wait_ge(s["rank_f"], r + 1)
                dve.tensor_tensor(r1[7][:], r1[7][:], r1[6][:], ALU.mult).then_inc(s["rank_g"], 1)
                dve.wait_ge(s["rank_g"], r + 1)
                dve.tensor_tensor(slot[:], r1[7][:], spare[:], ALU.add).then_inc(s["rank_j"], 1)
                hold(dve, s["rank_j"], r + 1)
                dve.tensor_copy(slot_all[:, bass.ds(b * NT, NT)], slot[:]).then_inc(s["rank_i"], 1)
                dve.tensor_scalar(spare[:], spare[:], float(T), None, ALU.add).then_inc(s["rank_b"], 1)
                dve.wait_ge(s["rank_b"], 2 * r + 2)

            def front_in(b):
                f = ffn_of_front(b)
                dve.wait_ge(s["x_in"], 16 * b + 16)
                norm(2 * f, x0, xn[0])

            def block_out(b, i):
                dve.wait_ge(s["ffn_h"], NF * ffn_of_front(b) + i + 1)
                dve.tensor_scalar(h_act[:, i, :], turn[1][:], cols[:, i:i + 1], None, ALU.add).then_inc(s["h_evac"], 1)

            def front_mid(b):
                f = ffn_of_front(b)
                ffn_x(f, x0, x1)
                moments(2 * f + 1, x1)

            def split(b, i):
                dve.wait_ge(s["proj_evac"], 2 * b + i + 1)
                full, parts = (qf, kf)[i], (qs, ks)[i]
                dve.tensor_copy(parts[:, 0, :], full[:]).then_inc(s["split_hi"], 1)
                dve.wait_ge(s["split_hi"], 2 * b + i + 1)
                dve.tensor_tensor(parts[:, 1, :], full[:], parts[:, 0, :].bitcast(F32), ALU.subtract).then_inc(s["split_lo"], 1)

            def query_features(b):
                dve.scalar_tensor_tensor(out=qaf[:], in0=qf[:], scalar=0.02, in1=qf[:],
                                         op0=ALU.mult, op1=ALU.min).then_inc(s["ma_q"], 1)

            def maxima(b, first, last):
                for n in range(first, last):
                    hs, i = n // (NPAIR // 2), 2 * (n % (NPAIR // 2))
                    dve.wait_ge(s["smax_mm"], NS * NPAIR // 2 * b + n + 1)
                    dve.tensor_reduce(mpart[:, hs, i:i + 2, :].rearrange("p i h -> p (i h)"),
                                      pair[n % 2][:].rearrange("p a (h k) -> p (a h) k", h=HL),
                                      AX.X, ALU.max).then_inc(s["smax_red"], 1)

            def max_of_tiles(b):
                dve.wait_ge(s["smax_red"], NS * NPAIR // 2 * (b + 1))
                for t in range(NT):
                    i = t * (t + 1) // 2
                    dve.tensor_reduce(mneg[:, t, :].rearrange("p (h s) -> p s h", s=NS),
                                      mpart[:, :, i:i + t + 1, :].rearrange("p s i h -> p s h i"),
                                      AX.X, ALU.max, negate=True).then_inc(s["max_red"], 1)

            def answers_out(b, hs):
                dve.wait_ge(s["pv_mm"], NS * NT * b + NT * hs + NT)
                dve.tensor_copy(y_tmp[hs % 2][:], accum[0][:]).then_inc(s["y_evac"], 1)

            def answers_divide(b, hs):
                dve.wait_ge(s["y_t"], NS * b + hs + 1)
                y = turn[0][:].rearrange("p (t h v) -> p t h v", t=NT, h=HL)
                rc = rcp[:, 0:NT * HL].rearrange("p (t h) -> p t h", t=NT)
                dve.reciprocal(rc, y[:, :, :, HD]).then_inc(s["rcp"], 1)
                dve.wait_ge(s["rcp"], NS * b + hs + 1)
                dve.tensor_tensor(y_ar[:].rearrange("p t (s h d) -> p s t h d", s=NS, h=HL)[:, hs],
                                  y[:, :, :, 0:HD], rc.unsqueeze(3).broadcast_to([P, NT, HL, HD]),
                                  ALU.mult).then_inc(s["y_norm"], 1)
                dve.wait_ge(s["y_norm"], NS * b + hs + 1)

            def batch(b, ahead):
                if ahead:
                    front_in(b + 1)
                answers_out(b, 0)
                if ahead:
                    low(ffn_of_front(b + 1))
                answers_divide(b, 0)
                if ahead:
                    for i in range(NF - 1):
                        block_out(b + 1, i)
                answers_out(b, 1)
                if ahead:
                    block_out(b + 1, NF - 1)
                answers_divide(b, 1)
                if ahead:
                    front_mid(b + 1)
                answers_out(b, 2)
                if ahead:
                    dve.wait_ge(s["v_next"], 32 * b + 32)
                    dve.wait_ge(s["v_aug"], b + 1)
                    normalise(2 * ffn_of_front(b + 1) + 1, x1, xn[1])
                answers_divide(b, 2)
                if ahead:
                    split(b + 1, 0)
                answers_out(b, 3)
                if ahead:
                    split(b + 1, 1)
                answers_divide(b, 3)
                for n in range(2 * NT):
                    dve.wait_ge(s["ma_mm"], 2 * NT * b + n + 1)
                    if n >= 4:
                        dve.wait_ge(s["ym_mm"], NT * b + (n - 4) // 2 + 1)
                    dve.tensor_tensor(work[:, n % 4].rearrange("p a (h q) -> p (a h) q", h=HL),
                                      pair[n % 2][:].rearrange("p a (h q) -> p (a h) q", h=HL),
                                      bc(const("key_before"), 2 * HL), ALU.mult).then_inc(s["ma_masked"], 1)
                    if n % 2 == 1 and n // 2 < NT - 1:
                        dve.wait_ge(s["kv_mm"], (NT - 1) * b + n // 2 + 1)
                        dve.tensor_tensor(kv[:, n // 2, :], turn[0][:, 0:D], const("same_head"), ALU.mult).then_inc(s["kv_evac"], 1)
                dve.wait_ge(s["ym_mm"], NT * b + NT)
                dve.wait_ge(s["yar_evac"], b + 1)
                dve.scalar_tensor_tensor(out=yT[:], in0=accum[0][:], scalar=SCALE, in1=y_tmp[0][:],
                                         op0=ALU.mult, op1=ALU.add).then_inc(s["y_sum"], 1)
                if ahead:
                    maxima(b + 1, 0, 1)
                f = ffn_of_tail(b)
                dve.wait_ge(s["proj_mm"], b + 1)
                dve.wait_ge(s["attn_base"], b + 1)
                dve.tensor_tensor(flat(xa), accum[1][:], flat(x_base), ALU.add).then_inc(s["attn_x"], 1)
                dve.wait_ge(s["attn_x"], b + 1)
                moments(2 * f, xa)
                if ahead:
                    query_features(b + 1)
                    maxima(b + 1, 1, 2)
                normalise(2 * f, xa, xn[0])
                if ahead:
                    maxima(b + 1, 2, 3)
                low(f)
                if ahead:
                    maxima(b + 1, 3, 15)
                dve.wait_ge(s["x_kept"], 16 * b + 16)
                ffn_x(f, xa, xb)
                moments(2 * f + 1, xb)
                if ahead:
                    maxima(b + 1, 15, 16)
                normalise(2 * f + 1, xb, xn[2])
                if ahead:
                    maxima(b + 1, 16, NS * NPAIR // 2)
                    max_of_tiles(b + 1)
                route(b, b)

            dve.wait_ge(s["x_in"], 16)
            moments(0, x0)
            dve.wait_ge(s["first_loaded"], 16 * FIRST_LOADS)
            w2_flat = w2[:].rearrange("p f d -> p (f d)")
            for i, w in enumerate((w1[:], w2_flat)):
                dve.tensor_reduce(wst[:, i:i + 1], w, AX.X, ALU.add, apply_absolute_value=True).then_inc(s["w_abs"], 1)
            normalise(0, x0, xn[0])
            dve.wait_ge(s["w_sum"], 1)
            dve.tensor_scalar(wst[:, 2:4], turn[0][:, 0:2], 1.0 / (FF * D), 1e-8, ALU.mult, ALU.max).then_inc(s["w_scale"], 1)
            dve.wait_ge(s["w_scale"], 1)
            dve.tensor_scalar(wst[:, 4:6], wst[:, 2:4], 0.5, None, ALU.mult).then_inc(s["w_half"], 1)
            dve.tensor_scalar(wst[:, 6:8], wst[:, 2:4], -0.5, None, ALU.mult).then_inc(s["w_half"], 1)
            dve.wait_ge(s["w_half"], 2)
            for i, w in enumerate((w1[:], w2_flat)):
                dve.tensor_scalar(tmp[:], w, wst[:, 6 + i:7 + i], None, ALU.is_lt).then_inc(s["w_low"], 1)
                dve.wait_ge(s["w_low"], i + 1)
                dve.scalar_tensor_tensor(out=(w1r[:], w)[i], in0=w, scalar=wst[:, 4 + i:5 + i], in1=tmp[:],
                                         op0=ALU.is_gt, op1=ALU.subtract).then_inc(s["w_tern"], 1)
                dve.wait_ge(s["w_tern"], i + 1)
            low(0)
            dve.memset(v_aug[:], 0.0).then_inc(s["pads_zeroed"], 1)
            dve.memset(e_pad[:], 0.0).then_inc(s["pads_zeroed"], 1)
            dve.wait_ge(s["pads_zeroed"], 2)
            dve.memset(v_aug[:, :, :, HD:HD + 1], 1.0).then_inc(s["pads_zeroed"], 1)
            for dst, name in ((ident_bf, "ident"), (add_q_bf, "add_q"), (add_k_bf, "add_k"),
                              (before_bf, "key_before"), (ones_bf, "ones")):
                dve.tensor_copy(dst[:], const(name)).then_inc(s["consts_bf"], 1)
            front_mid(0)
            normalise(1, x1, xn[1])
            split(0, 0)
            split(0, 1)
            query_features(0)
            maxima(0, 0, NS * NPAIR // 2)
            max_of_tiles(0)
            with dve.Fori(0, B - 1) as b:
                batch(b, True)
            batch(B - 1, False)

            def relu_experts(m):
                for e in range(E):
                    n = E * m + e
                    dve.wait_ge(s["h_mm"], n + 1)
                    dve.tensor_scalar(work[:, n % 2, 1, :], pair[n % 2][:, 1, :], 0.0, None, ALU.max).then_inc(s["h_relu_v"], 1)
                    dve.wait_ge(s["ye_mm"], n + 1)
                    if n >= 2:
                        dve.wait_ge(ye_kept[n % 2], 16 * (n // 2))
                    dve.tensor_copy(ye[:, n % 2].rearrange("p g d -> p (g d)"), accum[n % 2][:, 0:NG * D]).then_inc(s["ye_evac"], 1)

            def pick(b):
                dve.tensor_copy(slot_in[:], slot_all[:, bass.ds(b * NT, NT)]).then_inc(s["idx_in"], 1)
                dve.tensor_copy(r1[8][:], gate_all[:, bass.ds(b * NT, NT)]).then_inc(s["gate_in"], 1)

            def combine(r, dst):
                dve.wait_ge(s["gate_in"], r + 1)
                dve.wait_ge(s["x_back"], 16 * r + 16)
                dve.wait_ge(s["gathered"], 16 * NT * r + 16 * NT)
                for t in range(NT):
                    dve.scalar_tensor_tensor(out=dst[:, t, :], in0=yg[:, t // 2, t % 2, :], scalar=r1[8][:, t:t + 1],
                                             in1=xa[:, t, :], op0=ALU.mult, op1=ALU.add).then_inc(s["mixed"], 1)
                dve.wait_ge(s["mixed"], NT * r + NT)

            relu_experts(0)
            dve.wait_ge(s["zeroed"], 7)

            def enter_in(b):
                if not (isinstance(b, int) and b == 0):
                    dve.wait_ge(s["l1_base"], b)
                combine(b, x1)
                moments(norm_of_entry(b), x1)

            def least(b, i):
                dve.wait_ge(s["l1_z"], 2 * b + i + 1)
                dve.tensor_scalar((tmp, y_tmp[0])[i][:], (qf, kf)[i][:], 0.0, None, ALU.min).then_inc(s["l1_min"], 1)

            def feature(b, i):
                dve.wait_ge(s["l1_exp"], 2 * b + i + 1)
                dve.scalar_tensor_tensor(out=(q_feat, kaf[:])[i], in0=(qf, kf)[i][:], scalar=0.0, in1=(tmp, y_tmp[0])[i][:],
                                         op0=ALU.max, op1=ALU.add).then_inc(s["l1_feat"], 1)

            def split_keys(b):
                dve.wait_ge(s["l1_feat"], 2 * b + 2)
                dve.tensor_copy(ks[:, 0, :], kaf[:]).then_inc(s["l1_khi"], 1)
                dve.wait_ge(s["l1_khi"], b + 1)
                dve.tensor_tensor(ks[:, 1, :], kaf[:], ks[:, 0, :].bitcast(F32), ALU.subtract).then_inc(s["l1_klo"], 1)

            def values(b):
                dve.wait_ge(s["l1_mm"], 3 * b + 3)
                dve.tensor_tensor(v_new.rearrange("p (t d) -> p t d", t=NT), bank_of_entry(b, 2)[:].rearrange("p (t d) -> p t d", t=NT),
                                  bc(rows[:, 2, :], NT), ALU.add).then_inc(s["l1_v"], 1)

            def mask(b, t):
                for pr in range(2):
                    n = 2 * t + pr
                    dve.wait_ge(s["l1_s"], 2 * NT * b + n + 1)
                    if n >= 4:
                        dve.wait_ge(s["l1_y"], NT * b + (n - 4) // 2 + 1)
                    dve.tensor_tensor(work[:, n % 4].rearrange("p a (h q) -> p (a h) q", h=HL),
                                      pair[n % 2][:].rearrange("p a (h q) -> p (a h) q", h=HL),
                                      bc(const("key_upto"), 2 * HL), ALU.mult).then_inc(s["l1_masked"], 1)

            def state(b, t):
                dve.wait_ge(s["l1_kv"], (NT - 1) * b + t + 1)
                dve.tensor_tensor(kv1[t % 2], accum[1][:], const("same_head_v"), ALU.mult).then_inc(s["l1_kvev"], 1)

            def numerators(b, t):
                dve.wait_ge(s["l1_y"], NT * b + t + 1)
                if t:
                    dve.wait_ge(s["l1_yt"], NT * b + t)
                dve.tensor_copy(y_tmp[1][:], accum[0][:]).then_inc(s["l1_yev"], 1)

            def divide(b, t):
                dve.wait_ge(s["l1_yt"], NT * b + t + 1)
                y = turn[0][:].rearrange("p (h v) -> p h v", v=VW)
                dve.tensor_scalar(rcp[:, 0:H], y[:, :, HD], DEN_EPS, None, ALU.add).then_inc(s["l1_den"], 1)
                dve.wait_ge(s["l1_den"], NT * b + t + 1)
                dve.reciprocal(rcp[:, H:2 * H], rcp[:, 0:H]).then_inc(s["l1_rcp"], 1)
                dve.wait_ge(s["l1_rcp"], NT * b + t + 1)
                dve.tensor_tensor(y_ar[:, t, :].rearrange("p (h d) -> p h d", d=HD), y[:, :, 0:HD],
                                  rcp[:, H:2 * H].unsqueeze(2).broadcast_to([P, H, HD]), ALU.mult).then_inc(s["l1_yn"], 1)

            def open_next(b):
                mask(b, 0)
                state(b, 0)

            def attend(b, ahead):
                if ahead:
                    pick(b + 1)
                for t in range(NT):
                    if t + 1 < NT:
                        mask(b, t + 1)
                    numerators(b, t)
                    if t + 1 < NT - 1:
                        state(b, t + 1)
                    if ahead and t == 2:
                        enter_in(b + 1)
                    if ahead and t == 3:
                        normalise(norm_of_entry(b + 1), x1, xn[1])
                    divide(b, t)
                if ahead:
                    least(b + 1, 0)
                    feature(b + 1, 0)
                    least(b + 1, 1)
                dve.wait_ge(s["l1_out"], b + 1)
                dve.wait_ge(s["l1_base"], b + 1)
                dve.wait_ge(s["x_kept"], 16 * (B + b) + 16)
                dve.tensor_tensor(flat(xb), accum[1][:], flat(x_base), ALU.add).then_inc(s["l1_x"], 1)
                dve.wait_ge(s["l1_x"], b + 1)
                moments(norm_of_exit(b), xb)
                if ahead:
                    feature(b + 1, 1)
                    split_keys(b + 1)
                    values(b + 1)
                hold(dve, s["scattered"], 16 * NT * (B + b))
                normalise(norm_of_exit(b), xb, xn[2])
                route(B + b, b)
                if ahead:
                    open_next(b + 1)

            pick(0)
            enter_in(0)
            normalise(norm_of_entry(0), x1, xn[1])
            for i in range(2):
                least(0, i)
            for i in range(2):
                feature(0, i)
            split_keys(0)
            values(0)
            open_next(0)
            with dve.Fori(0, B - 1) as b:
                attend(b, True)
            attend(B - 1, False)
            relu_experts(1)
            dve.wait_ge(s["x_back"], 16 * B + 16)
            for b in range(B):
                dve.wait_ge(last_gathered[b], 16 * NT)
                for t in range(NT):
                    dve.scalar_tensor_tensor(out=x_last[:, b, t, :], in0=y_last[:, b, t, :],
                                             scalar=gate_all[:, NT * b + t:NT * b + t + 1],
                                             in1=x_last[:, b, t, :], op0=ALU.mult, op1=ALU.add).then_inc(s["mixed"], 1)

        @block.tensor
        def _(pe):
            def mm(dst, lhsT, rhs, start=True, stop=True):
                return pe.matmul(dst, lhsT, rhs, start=start, stop=stop, skip_group_check=True)

            def tile(a, t):
                return a[:, t * P:(t + 1) * P]

            def turn_tiles(dst, src):
                for t in range(NT):
                    last = pe.transpose(tile(dst, t), src[:, t, :], ident)
                return last

            def xt(r, x):
                pe.wait_ge(s["normed"], NT * r + NT)
                turn_tiles(turn[1], x).then_inc(s["xt_mm"], 1)

            def hidden(dst, f, i):
                mm(dst, tile(w1r, i), xs[:, 0, :], stop=False)
                if i == 0:
                    pe.wait_ge(s["xt_low"], f + 1)
                mm(dst, tile(w1r, i), xs[:, 1, :], start=False).then_inc(s["ffn_h"], 1)

            def output(f, i):
                pe.wait_ge(s["ffn_act"], NF * f + i + 1)
                for t in range(NT):
                    last = mm(tile(accum[1], t), tile(h_act[:, i, :], t), w2[:, i, :],
                              start=i == 0 and t == 0, stop=i == NF - 1)
                if i == NF - 1:
                    last.then_inc(s["ffn_out"], 1)

            def ffn(f, between):
                pe.wait_ge(s["xt_ready"], 2 * f + 1)
                for i in range(NF + 1):
                    if i >= 2 and i < NF:
                        pe.wait_ge(s["ffn_act"], NF * f + i - 1)
                    if i < NF:
                        hidden(HIDDEN_BANKS[i % 2][:], f, i)
                    if i:
                        output(f, i - 1)
                    between(i)

            def route(r, ln):
                pe.wait_ge(s["xt_ready"], ln + 1)
                for t in range(NT):
                    last = mm(accum[0][:, LG + t * E:LG + (t + 1) * E], tile(xnT, t), wr_sb[:])
                last.then_inc(s["lg_mm"], 1)
                pe.wait_ge(s["top_onehot"], r + 1)
                for t in range(NT):
                    dst = accum[0][:, t * E:(t + 1) * E]
                    mm(dst, before_bf[:], onehot_bf[:, t, :], stop=t == 0)
                    for before in range(t):
                        mm(dst, ones_bf[:], onehot_bf[:, before, :], start=False, stop=before == t - 1)
                for t in range(NT):
                    last = mm(accum[0][:, NT * E:NT * E + E], ones_bf[:], onehot_bf[:, t, :], start=t == 0, stop=t == NT - 1)
                last.then_inc(s["rank_mm"], 1)
                pe.wait_ge(s["rank_c"], 2 * r + 2)

            pe.wait_ge(s["w_abs"], 2)
            mm(turn[0][:, 0:2], const("ones"), wst[:, 0:2]).then_inc(s["w_sum"], 1)

            def front(step, b):
                f = ffn_of_front(b)
                if step == 0:
                    xt(2 * f, xn[0])
                elif step <= NF:
                    if step == 1:
                        pe.wait_ge(s["xt_low"], f + 1)
                    else:
                        pe.wait_ge(s["h_evac"], NF * (b - 1) + step - 1)
                    hidden(turn[1][:], f, step - 1)
                elif step == 6:
                    for i in range(NF):
                        output(f, i)
                elif step == 7:
                    xt(2 * f + 1, xn[1])
                elif step == 8:
                    pe.wait_ge(s["xt_ready"], 2 * f + 2)
                    mm(accum[1][:], tile(wqk, 0), xnT[:]).then_inc(s["qkv_mm"], 1)
                elif step == 9:
                    mm(turn[1][:], tile(wqk, 1), xnT[:]).then_inc(s["qkv_mm"], 1)
                elif step == 10:
                    pe.wait_ge(s["proj_evac"], 2 * b + 1)
                    mm(accum[1][:], wk2[:], xnT[:]).then_inc(s["qkv_mm"], 1)

            def turn_keys(b):
                pe.wait_ge(s["ma_k"], b + 1)
                for t in range(NT):
                    last = pe.transpose(tile(turn[0], t), tile(kaf, t), ident)
                last.then_inc(s["ka_t_mm"], 1)

            pairs = [(qt, kt) for qt in range(NT) for kt in range(qt + 1)]

            def max_scores(b, first, last_n):
                if first == 0:
                    pe.wait_ge(s["q_stacked"], 16 * b + 16)
                    pe.wait_ge(s["k_stacked"], 64 * b + 64)
                for n in range(first, last_n):
                    hs, i = n // (NPAIR // 2), 2 * (n % (NPAIR // 2))
                    if n >= 2:
                        pe.wait_ge(s["smax_red"], NS * NPAIR // 2 * b + n - 1)
                    for a in range(2):
                        qt, kt = pairs[i + a]
                        dst = pair[n % 2][:, a, :]
                        last = mm(dst, tile(q_stk[:, hs, :], qt), k_pad[:, HL * hs:HL * hs + HL, kt * P:(kt + 1) * P],
                                  stop=qt != kt)
                        if qt == kt:
                            last = mm(dst, ident_bf[:], bc(add_q_bf[:], HL), start=False)
                    last.then_inc(s["smax_mm"], 1)

            def max_turn(b):
                pe.wait_ge(s["max_red"], NT * b + NT)
                for t in range(NT):
                    last = pe.transpose(turn[0][0:H, t * P:(t + 1) * P], mneg[:, t, :], ident)
                last.then_inc(s["max_t"], 1)

            def batch(b, ahead):
                def scores(n):
                    hs, kt = n // NT, n % NT
                    w = T - P * kt
                    for pr in range(2):
                        u = 2 * n + pr
                        if u >= 2:
                            pe.wait_ge(s["exp_done"], 2 * NS * NT * b + u - 1)
                        for a in range(2):
                            dst = pair[u % 2][:, a, :]
                            mm(dst[:, 0:w], tile(k_pad[:, HL * hs + 2 * pr + a, :], kt), q_stk[:, hs, kt * P:T], stop=False)
                            last = mm(dst[:, 0:P], ident_bf[:], add_k_bf[:], start=False)
                        last.then_inc(s["st_mm"], 1)

                def answers(n):
                    hs, kt = n // NT, n % NT
                    w = T - P * kt
                    pe.wait_ge(s["exp_done"], 2 * NS * NT * b + 2 * n + 2)
                    if kt == 0 and hs >= 1:
                        pe.wait_ge(s["y_evac"], NS * b + hs)
                    for hl in range(HL):
                        last = mm(accum[0][VW * hl:VW * hl + VW, kt * P:T], v_aug[:, kt, HL * hs + hl, :],
                                  work[:, 2 * (n % 2) + hl // 2, hl % 2, 0:w], start=kt == 0, stop=kt == NT - 1)
                    last.then_inc(s["pv_mm"], 1)

                def turn_answers(hs):
                    pe.wait_ge(s["y_evac"], NS * b + hs + 1)
                    if hs >= 1:
                        pe.wait_ge(s["y_norm"], NS * b + hs)
                    for t in range(NT):
                        last = pe.transpose(tile(turn[0], t), tile(y_tmp[hs % 2], t), ident)
                    last.then_inc(s["y_t"], 1)

                pe.wait_ge(s["max_rows"], 16 * b + 16)
                pe.wait_ge(s["v_aug"], b + 1)
                scores(0)
                for n in range(NS * NT):
                    if n + 1 < NS * NT:
                        scores(n + 1)
                    answers(n)
                    if n % NT == 0 and n:
                        turn_answers(n // NT - 1)
                    if ahead and n in FRONT_AT:
                        front(FRONT_AT[n], b + 1)
                turn_answers(NS - 1)

                def ma_scores(t):
                    for pr in range(2):
                        n = 2 * t + pr
                        if n >= 2:
                            pe.wait_ge(s["ma_masked"], 2 * NT * b + n - 1)
                        for a in range(2):
                            hs = 2 * pr + a
                            last = mm(pair[n % 2][:, a, :], tile(ka_stk[:, hs, :], t),
                                      qa_pad[:, HL * hs:HL * hs + HL, t * P:(t + 1) * P])
                        last.then_inc(s["ma_mm"], 1)

                def ma_answers(t):
                    dst = tile(accum[0], t)
                    if t:
                        pe.wait_ge(s["kv_evac"], (NT - 1) * b + t)
                        mm(dst, kv[:, t - 1, :], tile(qaf, t), stop=False)
                    pe.wait_ge(s["ma_masked"], 2 * NT * b + 2 * t + 2)
                    for hl in range(HL):
                        for hs in range(NS):
                            last = mm(accum[0][VW * hs:VW * hs + VW, t * P:(t + 1) * P], e_pad[:, t, HL * hs + hl, :],
                                      tile(work[:, (2 * t + hs // 2) % 4, hs % 2, :], hl),
                                      start=t == 0 and hl == 0, stop=hl == HL - 1)
                    last.then_inc(s["ym_mm"], 1)

                pe.wait_ge(s["mq_stacked"], 64 * b + 64)
                pe.wait_ge(s["mk_stacked"], 16 * b + 16)
                pe.wait_ge(s["ka_tok"], b + 1)
                ma_scores(0)
                pe.wait_ge(s["err"], NS * b + NS)
                pe.wait_ge(s["err_pad"], NS * b + NS)
                pe.wait_ge(s["y_norm"], NS * b + NS)
                for t in range(NT):
                    if t < NT - 1:
                        if t:
                            pe.wait_ge(s["kv_evac"], (NT - 1) * b + t)
                        mm(turn[0][:, 0:D], ka_tok[:, t, :], err[:, t, :], start=t == 0, stop=True).then_inc(s["kv_mm"], 1)
                        ma_scores(t + 1)
                    ma_answers(t)
                if ahead:
                    pe.wait_ge(s["ma_k"], b + 2)
                turn_tiles(turn[1], y_ar).then_inc(s["yar_mm"], 1)
                if ahead:
                    max_scores(b + 1, 0, 2)
                pe.wait_ge(s["y_sum"], b + 1)
                for t in range(NT):
                    last = mm(tile(accum[1], t), tile(yT, t), wp[:])
                last.then_inc(s["proj_mm"], 1)
                f = ffn_of_tail(b)
                if ahead:
                    turn_keys(b + 1)
                    max_scores(b + 1, 2, 4)
                xt(2 * f, xn[0])
                if ahead:
                    pe.wait_ge(s["ka_tok"], b + 2)
                ffn(f, lambda i: max_scores(b + 1, WITH_FFN[i], WITH_FFN[i + 1]) if ahead else None)
                xt(2 * f + 1, xn[2])
                if ahead:
                    max_scores(b + 1, WITH_FFN[-1], NS * NPAIR // 2)
                    max_turn(b + 1)
                route(b, 2 * f + 1)

            xt(0, xn[0])
            pe.wait_ge(s["w_tern"], 2)
            ffn(0, lambda i: None)
            for step in range(7, FRONT_STEPS):
                front(step, 0)
            turn_keys(0)
            pe.wait_ge(s["consts_bf"], 5)
            pe.wait_ge(s["pad_one"], 64)
            max_scores(0, 0, NS * NPAIR // 2)
            pe.wait_ge(s["ka_tok"], 1)
            max_turn(0)
            with pe.Fori(0, B - 1) as b:
                batch(b, True)
            batch(B - 1, False)

            def experts(m):
                def turn_rows(e):
                    n = E * m + e
                    pe.wait_ge(xg_loaded[n % 4], 16 * (n // 4 + 1))
                    if n >= 2:
                        pe.wait_ge(s["xg_evac"], n - 1)
                    for g in range(NG):
                        last = pe.transpose(tile(turn[n % 2], g), xg[:, n % 4, g, :], ident)
                    last.then_inc(s["xg_t"], 1)

                def up(e):
                    n = E * m + e
                    pe.wait_ge(s["xg_evac"], n + 1)
                    if n >= 2:
                        pe.wait_ge(s["h_relu_v"], n - 1)
                        pe.wait_ge(s["h_relu_a"], n - 1)
                    for fb in range(NF):
                        last = mm(pair[n % 2][:, fb // 2, (fb % 2) * CAP:(fb % 2 + 1) * CAP],
                                  tile(mw1_sb[:, e, :], fb), y_tmp[n % 2][:, 0:CAP])
                    last.then_inc(s["h_mm"], 1)

                def down(e):
                    n = E * m + e
                    pe.wait_ge(s["h_relu_a"], n + 1)
                    pe.wait_ge(s["h_relu_v"], n + 1)
                    if n >= 2:
                        pe.wait_ge(s["ye_evac"], n - 1)
                    for g in range(NG):
                        for fb in range(NF):
                            last = mm(tile(accum[n % 2], g),
                                      work[:, n % 2, fb // 2, (fb % 2) * CAP + g * P:(fb % 2) * CAP + (g + 1) * P],
                                      mw2_sb[:, e, fb, :], start=fb == 0, stop=fb == NF - 1)
                    last.then_inc(s["ye_mm"], 1)

                turn_rows(0)
                up(0)
                turn_rows(1)
                for e in range(E):
                    if e + 1 < E:
                        up(e + 1)
                    if e + 2 < E:
                        turn_rows(e + 2)
                    down(e)

            pe.wait_ge(s["experts_loaded"], 16 * 2 * E)
            experts(0)

            def enter(step, b):
                if step == 0:
                    xt(norm_of_entry(b), xn[1])
                elif step <= 2:
                    if step == 1:
                        pe.wait_ge(s["xt_ready"], norm_of_entry(b) + 1)
                    elif bank_of_entry(b, 1) is turn[1]:
                        pe.wait_ge(s["l1_z"], 2 * b + 1)
                    mm(bank_of_entry(b, step - 1)[:], tile(l1w, step - 1), xnT[:]).then_inc(s["l1_mm"], 1)
                else:
                    if bank_of_entry(b, 2) is turn[1]:
                        pe.wait_ge(s["l1_z"], 2 * b + 2)
                    for t in range(NT):
                        last = mm(tile(bank_of_entry(b, 2), t), tile(xnT, t), tile(l1w, 2))
                    last.then_inc(s["l1_mm"], 1)

            def turn_key_features(b):
                pe.wait_ge(s["l1_feat"], 2 * b + 2)
                for t in range(NT):
                    last = pe.transpose(tile(turn[0], t), tile(kaf, t), ident)
                last.then_inc(s["l1_kt"], 1)

            def scores(b, t):
                for pr in range(2):
                    n = 2 * t + pr
                    if n >= 2:
                        pe.wait_ge(s["l1_masked"], 2 * NT * b + n - 1)
                    for a in range(2):
                        hs = 2 * pr + a
                        last = mm(pair[n % 2][:, a, :], tile(ka_stk[:, hs, :], t),
                                  qa_pad[:, HL * hs:HL * hs + HL, t * P:(t + 1) * P])
                    last.then_inc(s["l1_s"], 1)

            def state(b, t):
                if t:
                    pe.wait_ge(s["l1_kvev"], (NT - 1) * b + t)
                mm(accum[1][:], ka_tok[:, t, :], v_aug[:, t].rearrange("p h v -> p (h v)"),
                   start=t == 0).then_inc(s["l1_kv"], 1)

            def open_next(b):
                pe.wait_ge(s["l1_qstk"], 64 * b + 64)
                pe.wait_ge(s["l1_kstk"], 16 * b + 16)
                scores(b, 0)
                pe.wait_ge(s["l1_vaug"], b + 1)
                pe.wait_ge(s["l1_ktok"], b + 1)
                state(b, 0)

            def attend(b, ahead):
                def answers(t):
                    pe.wait_ge(s["l1_masked"], 2 * NT * b + 2 * t + 2)
                    if t:
                        pe.wait_ge(s["l1_kvev"], (NT - 1) * b + t)
                        pe.wait_ge(s["l1_yev"], NT * b + t)
                    for hs in range(NS):
                        if t:
                            mm(tile(accum[0], hs), tile(kv1[(t - 1) % 2], hs), tile(qaf, t), stop=False)
                        for hl in range(HL):
                            last = mm(accum[0][VW * hl:VW * hl + VW, hs * P:(hs + 1) * P], v_aug[:, t, HL * hs + hl, :],
                                      tile(work[:, (2 * t + hs // 2) % 4, hs % 2, :], hl), start=t == 0)
                    last.then_inc(s["l1_y"], 1)

                pe.wait_ge(s["l1_qaf"], b + 1)
                for t in range(NT):
                    if t + 1 < NT:
                        scores(b, t + 1)
                    answers(t)
                    if t + 1 < NT - 1:
                        state(b, t + 1)
                    if ahead and t == 3:
                        enter(0, b + 1)
                    pe.wait_ge(s["l1_yev"], NT * b + t + 1)
                    if t:
                        pe.wait_ge(s["l1_yn"], NT * b + t)
                    for hs in range(NS):
                        last = pe.transpose(tile(turn[0], hs), tile(y_tmp[1], hs), ident)
                    last.then_inc(s["l1_yt"], 1)
                if ahead:
                    enter(1, b + 1)
                pe.wait_ge(s["l1_yn"], NT * b + NT)
                turn_tiles(turn[0], y_ar).then_inc(s["l1_y1t"], 1)
                if ahead:
                    enter(2, b + 1)
                pe.wait_ge(s["l1_y1ev"], b + 1)
                for t in range(NT):
                    last = mm(tile(accum[1], t), tile(yT, t), l1wp[:])
                last.then_inc(s["l1_out"], 1)
                if ahead:
                    enter(3, b + 1)
                    turn_key_features(b + 1)
                    pe.wait_ge(s["l1_v"], b + 2)
                xt(norm_of_exit(b), xn[2])
                route(B + b, norm_of_exit(b))
                if ahead:
                    open_next(b + 1)

            for step in range(4):
                enter(step, 0)
            turn_key_features(0)
            open_next(0)
            with pe.Fori(0, B - 1) as b:
                attend(b, True)
            attend(B - 1, False)
            experts(1)


def kernel(**inputs):
    import numpy as _np
    import concourse.bacc as _bacc
    from concourse import mybir as _mybir
    from concourse.bass_utils import run_bass_kernel_spmd as _run

    g = {k: _np.asarray(v) for k, v in inputs.items()}
    ins = [
        ("x", g["L0_attn_x"].reshape(NTOK, D)),
        ("bias_cols", _np.concatenate([g["L0_ffn_b1"], g["L0_attn_b_attn"], g["L0_attn_b_k2"],
                                       g["L1_attn_b_attn"][:2 * D]]).reshape(-1, P).T),
        ("w_attn_t", g["L0_attn_w_attn"].T), ("w_k2_t", g["L0_attn_w_k2"].T),
        ("w_proj_t", g["L0_attn_w_proj"].T), ("b_proj", g["L0_attn_b_proj"]),
        ("w1_t", g["L0_ffn_W1"].T),
        ("w2_t", g["L0_ffn_W2"].T), ("b2", g["L0_ffn_b2"]),
        ("l1_w", g["L1_attn_W_attn"]), ("l1_bv", g["L1_attn_b_attn"][2 * D:]),
        ("l1_wp", g["L1_attn_W_proj"]), ("l1_bp", g["L1_attn_b_proj"]),
        ("wr", g["L1_ffn_Wr"]), ("mw1", g["L1_ffn_W1"]), ("mw2", g["L1_ffn_W2"]),
        ("consts", CONSTS),
    ]
    nc = _bacc.Bacc("TRN2", target_bir_lowering=False, num_devices=1)
    arrays, args = {}, []
    for name, a in ins:
        a = _np.ascontiguousarray(a)
        arrays[f"in_{name}"] = a
        args.append(nc.dram_tensor(f"in_{name}", a.shape, _mybir.dt.from_np(a.dtype), kind="ExternalInput").ap())
    args.append(nc.dram_tensor("out_0", (NTOK, D), _mybir.dt.float32, kind="ExternalOutput").ap())
    build(nc, *args)
    r = _run(nc, [arrays], core_ids=[0])
    return r.results[0]["out_0"].reshape(B, T, D)
```
